# Optimizing a Trainium2 kernel written in Bass

```python
import numpy as np
import jax
import jax.numpy as jnp

def _softmax(x, axis=-1):
    return jax.nn.softmax(x, axis=axis)

def _gelu(x):
    return jax.nn.gelu(x, approximate=True)

def _silu(x):
    return jax.nn.silu(x)

def _sigmoid(x):
    return jax.nn.sigmoid(x)

def _layernorm(x, axis=-1, eps=1e-05):
    m = jnp.mean(x, axis=axis, keepdims=True)
    v = jnp.var(x, axis=axis, keepdims=True)
    return (x - m) / jnp.sqrt(v + eps)

def _scatter_add(tgt, idx, src, axis=0):
    return tgt.at[idx].add(src)

def _segment_sum(src, seg, n):
    return jax.ops.segment_sum(src, seg, n)
kernel_name = 'mk_gnn_resnorm_d4_gnn_r8_42ed6c'

def setup_inputs(seed: int=0):
    np.random.seed(seed)
    _w = jnp.asarray

    def _rec_inputs():
        import jax
        import jax.numpy as jnp
        _gk = jax.random.key(seed)
        x = -0.000202 + 1 * jax.random.normal(jax.random.fold_in(_gk, 1), (6250, 128), jnp.float32)
        _s = jax.random.randint(jax.random.fold_in(_gk, 2), (100000,), 0, 6250, jnp.int32)
        _d = jax.random.randint(jax.random.fold_in(_gk, 3), (100000,), 0, 6250, jnp.int32)
        _loop = jnp.arange(6250, dtype=jnp.int32)
        src = jnp.concatenate([_s, _d, _loop])
        dst = jnp.concatenate([_d, _s, _loop])
        _o = jnp.argsort(dst, stable=True)
        src = src[_o]
        dst = dst[_o]
        edge_attr_128 = 2.93046e-05 + 1.00006 * jax.random.normal(jax.random.fold_in(_gk, 11), (206250, 128), jnp.float32)
        return (x, src, dst, edge_attr_128)
    x, src, dst, edge_attr_128 = _rec_inputs()

    def _L0_gnn_setup():
        import jax, jax.numpy as jnp
        import numpy as np
        N_NODES = 6250
        N_EDGES = 80000
        HIDDEN = 128
        HEADS = 8
        HEAD_DIM = HIDDEN // HEADS
        ALPHA = 0.2
        LN_EPS = 1e-05
        key = jax.random.key(seed)
        ks = jax.random.split(key, 12)

        def xavier(k, shape):
            fan_in, fan_out = (shape[-2], shape[-1])
            lim = float(np.sqrt(6.0 / (fan_in + fan_out)))
            return jax.random.uniform(k, shape, jnp.float32, -lim, lim)
        x = jax.random.normal(ks[0], (N_NODES, HIDDEN), jnp.float32)
        edge_index = jax.random.randint(ks[1], (2, N_EDGES), 0, N_NODES)
        edge_attr = jax.random.normal(ks[2], (N_EDGES, HIDDEN), jnp.float32)
        W = xavier(ks[3], (HEADS, HIDDEN, HEAD_DIM))
        a = xavier(ks[4], (HEADS, 2 * HEAD_DIM, 1))
        eb_w = xavier(ks[5], (HEADS, HIDDEN))
        eb_b = jnp.zeros((HEADS,), jnp.float32)
        eg_w = xavier(ks[6], (HEADS * HEAD_DIM, HIDDEN))
        eg_b = jnp.zeros((HEADS * HEAD_DIM,), jnp.float32)
        ln_g = jnp.ones((HIDDEN,), jnp.float32)
        ln_b = jnp.zeros((HIDDEN,), jnp.float32)
        return {'x': x, 'edge_index': edge_index, 'edge_attr': edge_attr, 'W': W, 'a': a, 'eb_w': eb_w, 'eb_b': eb_b, 'eg_w': eg_w, 'eg_b': eg_b, 'ln_g': ln_g, 'ln_b': ln_b}
    _L0_gnn_all = _L0_gnn_setup()
    _L0_gnn_in = {k: v for k, v in _L0_gnn_all.items() if k in ('W', 'a', 'eb_w', 'eb_b', 'eg_w', 'eg_b', 'ln_g', 'ln_b')}
    del _L0_gnn_all

    def _L1_gnn_setup():
        import jax, jax.numpy as jnp
        import numpy as np
        N_NODES = 6250
        N_EDGES = 200000
        F_IN = 128
        UNITS = 128
        LEAKY_SLOPE = 0.2
        key = jax.random.key(seed)
        k1, k2, k3, k4 = jax.random.split(key, 4)
        node_states = jax.random.normal(k1, (N_NODES, F_IN), dtype=jnp.float32)
        edges = jax.random.randint(k2, (N_EDGES, 2), 0, N_NODES, dtype=jnp.int32)
        kernel = jax.random.normal(k3, (F_IN, UNITS), dtype=jnp.float32) * (1.0 / np.sqrt(F_IN))
        kernel_attention = jax.random.normal(k4, (2 * UNITS, 1), dtype=jnp.float32) * (1.0 / np.sqrt(2 * UNITS))
        return {'node_states': node_states, 'edges': edges, 'kernel': kernel, 'kernel_attention': kernel_attention}
    _L1_gnn_all = _L1_gnn_setup()
    _L1_gnn_in = {k: v for k, v in _L1_gnn_all.items() if k in ('kernel', 'kernel_attention')}
    del _L1_gnn_all

    def _L2_gnn_setup():
        import jax, jax.numpy as jnp
        import numpy as np
        N_NODES = 12500
        N_EDGES = 75000
        HIDDEN = 128
        key = jax.random.key(seed)
        ks = jax.random.split(key, 12)
        s = 0.05
        x = jax.random.normal(ks[0], (N_NODES, HIDDEN), dtype=jnp.float32)
        edge_index = jax.random.randint(ks[1], (2, N_EDGES), 0, N_NODES, dtype=jnp.int64)
        edge_features = jax.random.normal(ks[2], (N_EDGES, HIDDEN), dtype=jnp.float32)
        global_feat = jax.random.normal(ks[3], (1, HIDDEN), dtype=jnp.float32)
        W_c = jax.random.normal(ks[4], (3 * HIDDEN, HIDDEN), dtype=jnp.float32) * s
        b_c = jnp.zeros((HIDDEN,), dtype=jnp.float32)
        W1 = jax.random.normal(ks[5], (HIDDEN, HIDDEN), dtype=jnp.float32) * s
        b1 = jnp.zeros((HIDDEN,), dtype=jnp.float32)
        W2 = jax.random.normal(ks[6], (HIDDEN, HIDDEN), dtype=jnp.float32) * s
        b2 = jnp.zeros((HIDDEN,), dtype=jnp.float32)
        W3 = jax.random.normal(ks[7], (HIDDEN, HIDDEN), dtype=jnp.float32) * s
        b3 = jnp.zeros((HIDDEN,), dtype=jnp.float32)
        return {'x': x, 'edge_index': edge_index, 'edge_features': edge_features, 'global_feat': global_feat, 'W_c': W_c, 'b_c': b_c, 'W1': W1, 'b1': b1, 'W2': W2, 'b2': b2, 'W3': W3, 'b3': b3}
    _L2_gnn_all = _L2_gnn_setup()
    _L2_gnn_in = {k: v for k, v in _L2_gnn_all.items() if k in ('global_feat', 'W_c', 'b_c', 'W1', 'b1', 'W2', 'b2', 'W3', 'b3')}
    del _L2_gnn_all

    def _L3_gnn_setup():
        import jax, jax.numpy as jnp
        from jax import lax
        import numpy as np
        N_NODES = 6250
        N_EDGES = 100000
        IN_CH = 128
        HEADS = 4
        OUT_CH = 32
        TOP_K = 8

        def _topk_mask_1h(e_h, row, k):
            E = e_h.shape[0]
            order = jnp.lexsort((-e_h, row))
            srow = row[order]
            seg_start = jnp.searchsorted(srow, srow, side='left')
            pos_in_seg = jnp.arange(E, dtype=seg_start.dtype) - seg_start
            keep_sorted = pos_in_seg < k
            return jnp.zeros((E,), jnp.bool_).at[order].set(keep_sorted)
        key = jax.random.key(seed)
        k1, k2, k3, k4 = jax.random.split(key, 4)
        x = jax.random.normal(k1, (N_NODES, IN_CH), jnp.float32)
        edge_index = jax.random.randint(k2, (2, N_EDGES), 0, N_NODES, dtype=jnp.int32)
        scale = float(np.sqrt(2.0 / (IN_CH + HEADS * OUT_CH)))
        W = jax.random.normal(k3, (IN_CH, HEADS * OUT_CH), jnp.float32) * scale
        att = jax.random.normal(k4, (HEADS, 2 * OUT_CH), jnp.float32) * 0.1
        return {'x': x, 'W': W, 'att': att, 'edge_index': edge_index}
    _L3_gnn_all = _L3_gnn_setup()
    _L3_gnn_in = {k: v for k, v in _L3_gnn_all.items() if k in ('W', 'att')}
    del _L3_gnn_all
    return {'x': x, 'src': src, 'dst': dst, 'edge_attr_128': edge_attr_128, 'L0_gnn_W': _L0_gnn_in['W'], 'L0_gnn_a': _L0_gnn_in['a'], 'L0_gnn_eb_w': _L0_gnn_in['eb_w'], 'L0_gnn_eb_b': _L0_gnn_in['eb_b'], 'L0_gnn_eg_w': _L0_gnn_in['eg_w'], 'L0_gnn_eg_b': _L0_gnn_in['eg_b'], 'L0_gnn_ln_g': _L0_gnn_in['ln_g'], 'L0_gnn_ln_b': _L0_gnn_in['ln_b'], 'L1_gnn_kernel': _L1_gnn_in['kernel'], 'L1_gnn_kernel_attention': _L1_gnn_in['kernel_attention'], 'L2_gnn_global_feat': _L2_gnn_in['global_feat'], 'L2_gnn_W_c': _L2_gnn_in['W_c'], 'L2_gnn_b_c': _L2_gnn_in['b_c'], 'L2_gnn_W1': _L2_gnn_in['W1'], 'L2_gnn_b1': _L2_gnn_in['b1'], 'L2_gnn_W2': _L2_gnn_in['W2'], 'L2_gnn_b2': _L2_gnn_in['b2'], 'L2_gnn_W3': _L2_gnn_in['W3'], 'L2_gnn_b3': _L2_gnn_in['b3'], 'L3_gnn_W': _L3_gnn_in['W'], 'L3_gnn_att': _L3_gnn_in['att']}

def reference(x, src, dst, edge_attr_128, L0_gnn_W, L0_gnn_a, L0_gnn_eb_w, L0_gnn_eb_b, L0_gnn_eg_w, L0_gnn_eg_b, L0_gnn_ln_g, L0_gnn_ln_b, L1_gnn_kernel, L1_gnn_kernel_attention, L2_gnn_global_feat, L2_gnn_W_c, L2_gnn_b_c, L2_gnn_W1, L2_gnn_b1, L2_gnn_W2, L2_gnn_b2, L2_gnn_W3, L2_gnn_b3, L3_gnn_W, L3_gnn_att):
    import jax
    import jax.numpy as jnp

    def _L0_gnn_ref(x, edge_index, edge_attr, W, a, eb_w, eb_b, eg_w, eg_b, ln_g, ln_b):
        import jax, jax.numpy as jnp
        import numpy as np
        N_NODES = 6250
        N_EDGES = 80000
        HIDDEN = 128
        HEADS = 8
        HEAD_DIM = HIDDEN // HEADS
        ALPHA = 0.2
        LN_EPS = 1e-05
        num_nodes = x.shape[0]
        x_heads = jnp.einsum('ni,hij->nhj', x, W)
        row, col = (edge_index[0], edge_index[1])
        src = x_heads[row]
        dst = x_heads[col]
        edge_bias = edge_attr @ eb_w.T + eb_b
        edge_gate = jax.nn.sigmoid(edge_attr @ eg_w.T + eg_b)
        edge_gate = edge_gate.reshape(-1, HEADS, HEAD_DIM)
        a_vec = a[..., 0]
        a_src, a_dst = (a_vec[:, :HEAD_DIM], a_vec[:, HEAD_DIM:])
        e = jnp.einsum('ehd,hd->eh', src, a_src) + jnp.einsum('ehd,hd->eh', dst, a_dst)
        e = e + edge_bias
        e = jnp.where(e > 0, e, ALPHA * e)
        max_per_node = jax.ops.segment_max(e, col, num_segments=num_nodes)
        exp_scores = jnp.exp(e - max_per_node[col])
        sum_per_node = jax.ops.segment_sum(exp_scores, col, num_segments=num_nodes)
        attn = exp_scores / jnp.maximum(sum_per_node[col], 1e-12)
        msg = src * edge_gate * attn[..., None]
        out_heads = jax.ops.segment_sum(msg.reshape(msg.shape[0], -1), col, num_segments=num_nodes)
        out = out_heads + x
        mu = jnp.mean(out, axis=-1, keepdims=True)
        var = jnp.mean((out - mu) ** 2, axis=-1, keepdims=True)
        out = (out - mu) / jnp.sqrt(var + LN_EPS) * ln_g + ln_b
        return out

    def _L1_gnn_ref(node_states, edges, kernel, kernel_attention):
        import jax, jax.numpy as jnp
        import numpy as np
        N_NODES = 6250
        N_EDGES = 200000
        F_IN = 128
        UNITS = 128
        LEAKY_SLOPE = 0.2
        n_nodes = node_states.shape[0]
        units = kernel.shape[1]
        dst = edges[:, 0]
        src = edges[:, 1]
        h = jnp.matmul(node_states, kernel)
        a_dst = kernel_attention[:units, 0]
        a_src = kernel_attention[units:, 0]
        score_dst = jnp.matmul(h, a_dst)
        score_src = jnp.matmul(h, a_src)
        scores = jax.nn.leaky_relu(score_dst[dst] + score_src[src], negative_slope=LEAKY_SLOPE)
        scores = jnp.exp(jnp.clip(scores, -2.0, 2.0))
        scores_sum = jax.ops.segment_sum(scores, dst, num_segments=n_nodes)
        attention_norm = scores / scores_sum[dst]
        out = jax.ops.segment_sum(h[src] * attention_norm[:, None], dst, num_segments=n_nodes)
        return out

    def _L2_gnn_ref(x, edge_index, edge_features, global_feat, W_c, b_c, W1, b1, W2, b2, W3, b3):
        import jax, jax.numpy as jnp
        import numpy as np
        N_NODES = 12500
        N_EDGES = 75000
        HIDDEN = 128
        n = x.shape[0]
        row = edge_index[0]
        edge_aggr = jnp.zeros((n, HIDDEN), dtype=x.dtype).at[row].add(edge_features)
        reps = n // global_feat.shape[0]
        global_expand = jnp.repeat(global_feat, reps, axis=0)
        combined = jnp.concatenate([x, edge_aggr, global_expand], axis=-1) @ W_c + b_c
        h = jax.nn.softplus(combined @ W1 + b1)
        h = jax.nn.softplus(h @ W2 + b2)
        return h @ W3 + b3

    def _L3_gnn_ref(x, W, att, edge_index):
        import jax, jax.numpy as jnp
        from jax import lax
        import numpy as np
        N_NODES = 6250
        N_EDGES = 100000
        IN_CH = 128
        HEADS = 4
        OUT_CH = 32
        TOP_K = 8

        def _topk_mask_1h(e_h, row, k):
            E = e_h.shape[0]
            order = jnp.lexsort((-e_h, row))
            srow = row[order]
            seg_start = jnp.searchsorted(srow, srow, side='left')
            pos_in_seg = jnp.arange(E, dtype=seg_start.dtype) - seg_start
            keep_sorted = pos_in_seg < k
            return jnp.zeros((E,), jnp.bool_).at[order].set(keep_sorted)
        N = x.shape[0]
        H, C = (HEADS, OUT_CH)
        h = (x @ W).reshape(N, H, C)
        loops = jnp.arange(N, dtype=edge_index.dtype)
        ei = jnp.concatenate([edge_index, jnp.stack([loops, loops])], axis=1)
        row, col = (ei[0], ei[1])
        x_i = h[row]
        x_j = h[col]
        a_i, a_j = (att[:, :C], att[:, C:])
        e = jnp.einsum('ehc,hc->eh', x_i, a_i) + jnp.einsum('ehc,hc->eh', x_j, a_j)
        e = jax.nn.leaky_relu(e, negative_slope=0.2)
        mask = jax.vmap(lambda eh: _topk_mask_1h(eh, row, TOP_K), in_axes=1, out_axes=1)(e)
        e = jnp.where(mask, e, -jnp.inf)
        seg_max = jax.ops.segment_max(e, row, num_segments=N)
        ez = jnp.exp(e - lax.stop_gradient(seg_max)[row])
        denom = jax.ops.segment_sum(ez, row, num_segments=N)
        alpha = ez / denom[row]
        out = jax.ops.segment_sum(alpha[:, :, None] * x_j, row, num_segments=N)
        out = out.reshape(N, H * C)
        return jax.nn.elu(out)
    edge_index = jnp.stack([src, dst])
    edge_index_t = jnp.stack([src, dst], axis=1)
    x = _layernorm(x + _L0_gnn_ref(x, edge_index, edge_attr_128, L0_gnn_W, L0_gnn_a, L0_gnn_eb_w, L0_gnn_eb_b, L0_gnn_eg_w, L0_gnn_eg_b, L0_gnn_ln_g, L0_gnn_ln_b), axis=-1)
    x = _layernorm(x + _L1_gnn_ref(x, edge_index_t, L1_gnn_kernel, L1_gnn_kernel_attention), axis=-1)
    x = _layernorm(x + _L2_gnn_ref(x, edge_index, edge_attr_128, L2_gnn_global_feat, L2_gnn_W_c, L2_gnn_b_c, L2_gnn_W1, L2_gnn_b1, L2_gnn_W2, L2_gnn_b2, L2_gnn_W3, L2_gnn_b3), axis=-1)
    x = _layernorm(x + _L3_gnn_ref(x, L3_gnn_W, L3_gnn_att, edge_index), axis=-1)
    return x

_drawn_inputs = setup_inputs


def setup_inputs(seed=0):
    import zlib

    import numpy as np

    out = dict(_drawn_inputs(seed))
    spreads = {'L0_gnn_eb_b': (0.0, 2.0),
     'L0_gnn_eg_b': (0.0, 0.392),
     'L0_gnn_ln_g': (1.0, 0.2),
     'L0_gnn_ln_b': (0.0, 0.1),
     'L2_gnn_b_c': (0.0, 0.607),
     'L2_gnn_b1': (0.0, 0.447),
     'L2_gnn_b2': (0.0, 0.1),
     'L2_gnn_b3': (0.0, 0.1)}
    factors = {}
    for name, (base, spread) in spreads.items():
        noise = np.random.default_rng([zlib.crc32(name.encode()), seed]).standard_normal(out[name].shape)
        drawn = base * np.exp(spread * noise) if base else spread * noise
        out[name] = jnp.asarray(drawn.astype(out[name].dtype))
    for name, factor in factors.items():
        out[name] = (out[name] * factor).astype(out[name].dtype)
    return out
```

```python
from contextlib import ExitStack

import concourse.bass as bass
from concourse import mybir

ALU = mybir.AluOpType
ACT = mybir.ActivationFunctionType
F32 = mybir.dt.float32
I32 = mybir.dt.int32
AX = mybir.AxisListType
ds = bass.ds

P = 128
C = 128
N = 6250
E = 206250
NB = -(-N // P)
NBX = NB + 1
NP = NB * P
TE = -(-E // P)
G = 4
GE = TE // G
TR = -(-TE // P) * P
KR = TR // P
TS = TR
GS = TS // G
LP = TE + NB
PADKEY = NP - 1
W = 136
X8 = 8
RW = 132
KE = GE + NB - 1
KS = GS + NB - 1
BIG = 1.0e30
LN_EPS = 1.0e-5
TAIL = N - (NB - 1) * P
ETAIL = E - (TE - 1) * P
assert TE % G == 0 and LP < TS


DBG = 0


class Env:
    pass


def stage_constants(nc, v):
    s_set, s_cp, s_io, s_pe = v.sem("c_set"), v.sem("c_cp"), v.sem("c_io"), v.sem("c_iota")
    with nc.Block() as block:
        @block.gpsimd
        def _(pool):
            nc.gpsimd.iota(v.iota_i[:, :], [[1, P]], base=0, channel_multiplier=0).then_inc(s_io, 1)
            nc.gpsimd.iota(v.part_i[:, :], [[0, 1]], base=0, channel_multiplier=1).then_inc(s_io, 1)
            nc.gpsimd.iota(v.blk_i[:, :], [[P, NBX]], base=0, channel_multiplier=0).then_inc(s_io, 1)
            nc.gpsimd.iota(v.stepn_i[:, :], [[1, 512]], base=0, channel_multiplier=0).then_inc(s_io, 1)

        @block.sync
        def _(sp):
            sp.wait_ge(s_set, 7)
            half = (TR * P - E) // 2
            for row, keys, at in ((v.src_row, v.src, 0), (v.dst_row, v.dst, 1)):
                sp.dma_start(row[:, at:at + E], keys[None, :]).then_inc(v.s_in, 16)
                for first in (E + at, E + at + half):
                    sp.dma_start(row[:, first:first + half], v.padrow[:, :]).then_inc(v.s_in, 16)
            for row in (v.dst_row, v.sorted_row):
                sp.dma_start(row[:, 0:1], v.blank[:, 0:1]).then_inc(v.s_in, 16)
                sp.dma_start(row[:, TR * P + 1:TR * P + 2], v.blank[:, 0:1]).then_inc(v.s_in, 16)
            sp.dma_start(v.X[:, 0:NB - 1, :],
                         v.x[0:(NB - 1) * P, :].rearrange("(b p) c -> p b c", p=P)).then_inc(v.s_in, 16)
            sp.dma_start(v.X[0:TAIL, NB - 1, :], v.x[(NB - 1) * P:N, :]).then_inc(v.s_in, 16)
            sp.dma_start(v.srci[:, 0:TE - 1], v.src_t).then_inc(v.s_in, 16)
            sp.dma_start(v.srci[0:ETAIL, TE - 1:TE], v.src[(TE - 1) * P:E, None]).then_inc(v.s_in, 16)
            sp.dma_start(v.dsti[:, 0:TE - 1], v.dst_t).then_inc(v.s_in, 16)
            sp.dma_start(v.dsti[0:ETAIL, TE - 1:TE], v.dst[(TE - 1) * P:E, None]).then_inc(v.s_in, 16)

        @block.vector
        def _(dve):
            nc.vector.memset(v.X[:, NB - 1:NBX, :], 0.0).then_inc(s_set, 1)
            nc.vector.memset(v.srci[:, TE - 1:TR], PADKEY).then_inc(s_set, 1)
            nc.vector.memset(v.dsti[:, TE - 1:TR], PADKEY).then_inc(s_set, 1)
            nc.vector.memset(v.ones[:, :], 1.0).then_inc(s_set, 1)
            nc.vector.memset(v.zeros[:, :], 0.0).then_inc(s_set, 1)
            nc.vector.memset(v.padrow[:, :], PADKEY).then_inc(s_set, 1)
            nc.vector.memset(v.blank[:, :], -1).then_inc(s_set, 1)
            dve.wait_ge(s_io, 4)
            nc.vector.tensor_copy(v.iota[:, :], v.iota_i[:, :]).then_inc(s_cp, 1)
            nc.vector.tensor_copy(v.part[:, :], v.part_i[:, :]).then_inc(s_cp, 1)
            nc.vector.tensor_copy(v.blk[:, :], v.blk_i[:, :]).then_inc(s_cp, 1)
            nc.vector.tensor_copy(v.stepn[:, :], v.stepn_i[:, :]).then_inc(s_cp, 1)
            dve.wait_ge(s_cp, 4)
            nc.vector.tensor_scalar(v.ident[:, :], v.iota[:, :], v.part[:, 0:1], None,
                                    ALU.is_equal).then_inc(s_cp, 1)
            nc.vector.tensor_scalar(v.before[:, :], v.iota[:, :], v.part[:, 0:1], None,
                                    ALU.is_gt).then_inc(s_cp, 1)
            nc.vector.tensor_scalar(v.after[:, :], v.iota[:, :], v.part[:, 0:1], None,
                                    ALU.is_lt).then_inc(s_cp, 1)
            dve.wait_ge(v.s_in, 256)
            nc.vector.tensor_copy(v.srck[:, :], v.srci[:, :]).then_inc(s_cp, 1)
            nc.vector.tensor_copy(v.dstk[:, :], v.dsti[:, :]).then_inc(s_cp, 1)


def stage_weights(nc, v, name, w_dram, wt_dram, vectors, rhs):
    s_z, s_d, s_p, s_e = v.sem(name + "_z"), v.sem(name + "_d"), v.sem(name + "_p"), v.sem(name + "_e")
    with ExitStack() as mem:
        wt = mem.enter_context(nc.sbuf_tensor(name + "_wt", [P, C], F32))
        ab = mem.enter_context(nc.sbuf_tensor(name + "_ab", [P, 2 * X8], F32))
        ps = mem.enter_context(nc.psum_tensor(name + "_ps", [P, 512], F32))
        with nc.Block() as block:
            @block.vector
            def _(dve):
                nc.vector.memset(ab[:, :], 0.0).then_inc(s_z, 1)
                dve.wait_ge(s_p, 1)
                nc.vector.tensor_copy(rhs[:, C:C + 2 * X8], ps[:, 0:2 * X8]).then_inc(s_e, 1)

            @block.sync
            def _(sp):
                sp.dma_start(wt[:, :], wt_dram).then_inc(s_d, 16)
                sp.dma_start(rhs[:, 0:C], w_dram).then_inc(s_d, 16)
                sp.wait_ge(s_z, 1)
                for row, first, n, col in vectors:
                    sp.dma_start(ab[first:first + n, col:col + 1], row).then_inc(s_d, 16)

            @block.tensor
            def _(pe):
                pe.wait_ge(s_d, 16 * (2 + len(vectors)))
                nc.tensor.matmul(ps[:, 0:2 * X8], wt[:, :], ab[:, :], start=True, stop=True).then_inc(s_p, 1)


def stage_node_table(nc, v, name, rhs, table, scores):
    s_x, s_xf = v.sem(name + "_x"), v.sem(name + "_xf")
    s_t, s_xt, s_h = v.sem(name + "_t"), v.sem(name + "_xt"), v.sem(name + "_h")
    s_row, s_sc = v.sem(name + "_row"), v.sem(name + "_sc")
    s_st = [v.sem(f"{name}_st{u}") for u in range(2)]
    with ExitStack() as mem:
        xs = mem.enter_context(nc.sbuf_tensor(name + "_xs", [P, 2, C], F32))
        xt = mem.enter_context(nc.sbuf_tensor(name + "_xt", [P, 2, P], F32))
        row = mem.enter_context(nc.sbuf_tensor(name + "_row", [P, 2, W], F32))
        pst = [mem.enter_context(nc.psum_tensor(f"{name}_pst{u}", [P, 512], F32)) for u in range(2)]
        psh = [mem.enter_context(nc.psum_tensor(f"{name}_psh{u}", [P, 512], F32)) for u in range(2)]
        out = table.rearrange("(b p) w -> p b w", p=P)
        with nc.Block() as block:
            @block.vector
            def _(dve):
                dve.sem_inc(s_xf, 2)
                with dve.Fori(0, NBX // 2) as i:
                    for u in range(2):
                        b = i * 2 + u
                        dve.wait_ge(s_xf, b + 1)
                        nc.vector.tensor_scalar(xs[:, u, :], v.X[:, ds(b, 1), :].rearrange("p a c -> p (a c)"),
                                                0.0, None, ALU.add).then_inc(s_x, 1)
                    for u in range(2):
                        b = i * 2 + u
                        dve.wait_ge(s_h, b + 1)
                        if True:
                            dve.wait_ge(s_st[u], i * 16 + 16)
                        nc.vector.tensor_copy(row[:, u, :], psh[u][:, 0:W]).then_inc(s_row, 1)
                        nc.vector.tensor_scalar(scores[:, ds(b, 1), :].rearrange("p a c -> p (a c)"),
                                                psh[u][:, W:W + X8], 0.0, None, ALU.add).then_inc(s_sc, 1)

            @block.tensor
            def _(pe):
                with pe.Fori(0, NBX // 2) as i:
                    for u in range(2):
                        b = i * 2 + u
                        pe.wait_ge(s_x, b + 1)
                        nc.tensor.transpose(pst[u][:, 0:P], xs[:, u, :], v.ident[:, :]).then_inc(s_xf, 1)
                    for u in range(2):
                        b = i * 2 + u
                        pe.wait_ge(s_xt, b + 1)
                        pe.wait_ge(s_sc, b + 1)
                        nc.tensor.matmul(psh[u][:, 0:W + X8], xt[:, u, :], rhs[:, :], start=True,
                                         stop=True).then_inc(s_h, 1)

            @block.scalar
            def _(act):
                act.sem_inc(s_sc, 2)
                with act.Fori(0, NBX // 2) as i:
                    for u in range(2):
                        b = i * 2 + u
                        act.wait_ge(s_xf, b + 3)
                        act.wait_ge(s_sc, b + 1)
                        nc.scalar.activation(xt[:, u, :], pst[u][:, 0:P], ACT.Copy).then_inc(s_xt, 1)

            @block.sync
            def _(sp):
                for u in range(2):
                    sp.sem_inc(s_st[u], 16)
                with sp.Fori(0, NBX // 2) as i:
                    for u in range(2):
                        b = i * 2 + u
                        sp.wait_ge(s_row, b + 1)
                        sp.dma_start(out[:, ds(b, 1), :], row[:, u:u + 1, :]).then_inc(s_st[u], 16)
                for u in range(2):
                    sp.wait_ge(s_st[u], 16 + 16 * (NBX // 2))


RING = 2


def pipeline(eng, n, *parts):
    last = max(lag for _, lag in parts)
    lead = -(-(last + RING) // RING) * RING

    def turn(t):
        for fn, lag in parts:
            if 0 <= t - lag < n:
                fn(t - lag, (t - lag) % RING, (t - lag) // RING)

    turns = max(0, n - lead) // RING
    for t in range(min(lead, n + last)):
        turn(t)
    if turns:
        with eng.Fori(0, turns) as i:
            for r in range(RING):
                for fn, lag in parts:
                    at = lead + r - lag
                    fn(i * RING + at, at % RING, i + at // RING)
    for t in range(lead + turns * RING, n + last):
        turn(t)


def later(item, by=RING):
    return not isinstance(item, int) or item >= by


def chain(eng, sem):
    count = [0]

    def link(ins):
        count[0] += 1
        ins.then_inc(sem, 1)
        eng.wait_ge(sem, count[0])
    return link


def flat(ap):
    return ap.rearrange("p a c -> p (a c)")


def stage_steps(nc, v, name, count, groups, steps):
    s_dve, s_pe = v.sem(name + "_dve"), v.sem(name + "_pe")
    with ExitStack() as mem:
        sb = lambda n, s, d=F32: mem.enter_context(nc.sbuf_tensor(name + n, s, d))
        first_i, first = sb("_fi", [P, 1], I32), sb("_f", [P, 1])
        started, row = sb("_st", [P, 512]), sb("_row", [1, 2, 512])
        ps = mem.enter_context(nc.psum_tensor(name + "_ps", [P, 512], F32))
        ps2 = mem.enter_context(nc.psum_tensor(name + "_ps2", [P, 512], F32))
        with nc.Block() as block:
            @block.tensor
            def _(pe):
                nc.tensor.matmul(ps[0:NBX, 0:1], count[:, 0:NBX], v.ones[:, 0:1], start=True,
                                 stop=True).then_inc(s_pe, 1)
                pe.wait_ge(s_dve, 5)
                nc.tensor.matmul(ps2[0:1, :], v.ones[0:NBX, 0:1], started[0:NBX, :], start=True,
                                 stop=True).then_inc(s_pe, 1)

            @block.vector
            def _(dve):
                link = chain(dve, s_dve)
                dve.wait_ge(s_pe, 1)
                size = float(G * P)
                link(nc.vector.tensor_scalar(first_i[0:NBX, :], ps[0:NBX, 0:1], 1.0 / size,
                                             -0.5 + 0.25 / size, ALU.mult, ALU.add))
                link(nc.vector.tensor_copy(first[0:NBX, :], first_i[0:NBX, :]))
                link(nc.vector.tensor_scalar(first[0:NBX, :], first[0:NBX, :], float(groups - 1), None, ALU.min))
                link(nc.vector.tensor_tensor(first[0:NBX, :], first[0:NBX, :], v.part[0:NBX, :], ALU.add))
                link(nc.vector.tensor_scalar(started[0:NBX, :], v.stepn[0:NBX, :], first[0:NBX, 0:1], None,
                                             ALU.is_ge))
                dve.wait_ge(s_pe, 2)
                link(nc.vector.tensor_scalar(row[:, 1, :], ps2[0:1, :], -1.0, None, ALU.add))
                link(nc.vector.tensor_tensor(row[:, 0, :], v.stepn[0:1, :], row[:, 1, :], ALU.subtract))
                link(nc.vector.tensor_copy(flat(steps[:, :, :]), flat(row[:, :, :])))


def stage_count_dst(nc, v, count):
    s = v.sem("cnt")
    with nc.sbuf_tensor("cnt_junk", [P, TR], F32) as junk, nc.Block() as block:
        @block.vector
        def _(dve):
            for b in range(NBX):
                if b:
                    dve.wait_ge(s, b)
                nc.vector.tensor_scalar(junk[:, :], v.dstk[:, :], float(b * P), None, ALU.is_lt, ALU.add,
                                        accum_out=count[:, b:b + 1]).then_inc(s, 1)


def step_of(eng, steps, k, groups):
    g = eng.value_load(steps[0:1, 0, ds(k, 1)], min_val=0, max_val=groups - 1)
    b = eng.value_load(steps[0:1, 1, ds(k, 1)], min_val=0, max_val=NBX - 1)
    return g, b


def stage_expand(nc, v, name, keys, steps, n_steps, groups, width, per_edge):
    s_zero, s_oh, s_t, s_oht = v.sem(name + "_z"), v.sem(name + "_oh"), v.sem(name + "_t"), v.sem(name + "_oht")
    s_got, s_add, s_kr = v.sem(name + "_got"), v.sem(name + "_add"), v.sem(name + "_kr")
    with ExitStack() as mem:
        sb = lambda n, s, d=F32: mem.enter_context(nc.sbuf_tensor(name + n, s, d))
        krel = sb("_kr", [P, RING, G])
        oh = sb("_oh", [P, RING, G, P])
        oht = sb("_oht", [P, RING, G * P])
        pst = [mem.enter_context(nc.psum_tensor(f"{name}_pt{u}", [P, 512], F32)) for u in range(RING)]
        psx = [mem.enter_context(nc.psum_tensor(f"{name}_px{u}", [P, 512], F32)) for u in range(RING)]
        with nc.Block() as block:
            @block.vector
            def _(dve):
                nc.vector.memset(per_edge[:, :, :], 0.0).then_inc(s_zero, 1)

                def onehot(k, u, use):
                    g, b = step_of(dve, steps, k, groups)
                    if later(k):
                        dve.wait_ge(s_t, k - 1)
                    nc.vector.tensor_scalar(krel[:, u, :], keys[:, ds(g * G, G)], v.blk[:, ds(b, 1)], None,
                                            ALU.subtract).then_inc(s_kr, 1)
                    dve.wait_ge(s_kr, k + 1)
                    nc.vector.tensor_tensor(oh[:, u, :, :], v.iota[:, None, :].broadcast_to([P, G, P]),
                                            krel[:, u, :, None].broadcast_to([P, G, P]),
                                            ALU.is_equal).then_inc(s_oh, 1)

                def add(k, u, use):
                    g = dve.value_load(steps[0:1, 0, ds(k, 1)], min_val=0, max_val=groups - 1)
                    dve.wait_ge(s_got, k + 1)
                    if later(k, 1):
                        dve.wait_ge(s_add, k)
                    else:
                        dve.wait_ge(s_zero, 1)
                    here = per_edge[:, ds(g * G, G), 0:width]
                    nc.vector.tensor_tensor(here, here, psx[u][:, 0:G * X8].rearrange(
                        "p (g c) -> p g c", g=G)[:, :, 0:width], ALU.add).then_inc(s_add, 1)

                pipeline(dve, n_steps, (onehot, 0), (add, 2))

            @block.tensor
            def _(pe):
                def turn(k, u, use):
                    pe.wait_ge(s_oh, k + 1)
                    if later(k):
                        pe.wait_ge(s_oht, k - 1)
                    for j in range(G):
                        last = nc.tensor.transpose(pst[u][:, j * P:(j + 1) * P], oh[:, u, j, :], v.ident[:, :])
                    last.then_inc(s_t, 1)

                def look(k, u, use):
                    b = pe.value_load(steps[0:1, 1, ds(k, 1)], min_val=0, max_val=NBX - 1)
                    pe.wait_ge(s_oht, k + 1)
                    if later(k):
                        pe.wait_ge(s_add, k - 1)
                    for j in range(G):
                        last = nc.tensor.matmul(psx[u][:, j * X8:(j + 1) * X8], oht[:, u, j * P:(j + 1) * P],
                                                flat(v.scores[:, ds(b, 1), :]), start=True, stop=True)
                    last.then_inc(s_got, 1)

                pipeline(pe, n_steps, (turn, 0), (look, 1))

            @block.scalar
            def _(act):
                nc.scalar.preload_act_table(ACT.Copy)

                def copy(k, u, use):
                    act.wait_ge(s_t, k + 1)
                    if later(k):
                        act.wait_ge(s_got, k - 1)
                    nc.scalar.activation(oht[:, u, :], pst[u][:, :], ACT.Copy).then_inc(s_oht, 1)

                pipeline(act, n_steps, (copy, 0))


def stage_histogram(nc, v, hist):
    s_split, s_oh, s_mm, s_end = v.sem("h_split"), v.sem("h_oh"), v.sem("h_mm"), v.sem("h_end")
    with ExitStack() as mem:
        sb = lambda n, s, d=F32: mem.enter_context(nc.sbuf_tensor("h" + n, s, d))
        lo_i = sb("_lo_i", [P, TR], I32)
        ohlo = sb("_ohlo", [P, RING, G, P])
        ohhi = sb("_ohhi", [P, RING, G, NBX])
        ps = mem.enter_context(nc.psum_tensor("h_ps", [P, 512], F32))
        with nc.Block() as block:
            @block.vector
            def _(dve):
                link = chain(dve, s_split)
                link(nc.vector.tensor_scalar(lo_i[:, :], v.srci[:, :], P - 1, None, ALU.bitwise_and))
                link(nc.vector.tensor_copy(v.lo[:, :], lo_i[:, :]))
                link(nc.vector.tensor_tensor(v.hi[:, :], v.srck[:, :], v.lo[:, :], ALU.subtract))
                link(nc.vector.tensor_scalar(v.hi[:, :], v.hi[:, :], 1.0 / P, None, ALU.mult))

                def onehots(g, u, use):
                    if later(g):
                        dve.wait_ge(s_mm, g - 1)
                    nc.vector.tensor_tensor(ohlo[:, u, :, :], v.iota[:, None, :].broadcast_to([P, G, P]),
                                            v.lo[:, ds(g * G, G), None].broadcast_to([P, G, P]),
                                            ALU.is_equal).then_inc(s_oh, 1)
                    nc.vector.tensor_tensor(ohhi[:, u, :, :], v.iota[:, None, 0:NBX].broadcast_to([P, G, NBX]),
                                            v.hi[:, ds(g * G, G), None].broadcast_to([P, G, NBX]),
                                            ALU.is_equal).then_inc(s_oh, 1)

                pipeline(dve, GE, (onehots, 0))
                dve.wait_ge(s_end, 1)
                nc.vector.tensor_copy(hist[:, :], ps[:, 0:NBX]).then_inc(s_end, 1)

            @block.tensor
            def _(pe):
                nc.tensor.matmul(ps[:, 0:NBX], v.zeros[:, :], v.zeros[:, 0:NBX], start=True, stop=False)

                def count(g, u, use):
                    pe.wait_ge(s_oh, g * 2 + 2)
                    for j in range(G):
                        last = nc.tensor.matmul(ps[:, 0:NBX], ohlo[:, u, j, :], ohhi[:, u, j, :],
                                                start=False, stop=False)
                    last.then_inc(s_mm, 1)

                pipeline(pe, GE, (count, 0))
                nc.tensor.matmul(ps[:, 0:NBX], v.zeros[:, :], v.zeros[:, 0:NBX], start=False,
                                 stop=True).then_inc(s_end, 1)


def stage_bases(nc, v, hist, run, below):
    s, s_pe = v.sem("b_dve"), v.sem("b_pe")
    with ExitStack() as mem:
        sb = lambda n, s, d=F32: mem.enter_context(nc.sbuf_tensor("b" + n, s, d))
        h1, tot, incl, zr = sb("_h1", [P, NBX]), sb("_tot", [P, NBX]), sb("_incl", [P, NBX]), sb("_z", [P, NBX])
        ps = mem.enter_context(nc.psum_tensor("b_ps", [P, 512], F32))
        with nc.Block() as block:
            @block.vector
            def _(dve):
                link = chain(dve, s)
                link(nc.vector.memset(zr[:, :], 0.0))
                link(nc.vector.tensor_scalar(h1[:, :], hist[:, :], 1.0, None, ALU.add))
                dve.wait_ge(s_pe, 1)
                link(nc.vector.tensor_copy(tot[:, :], ps[:, 64:64 + NBX]))
                link(nc.vector.tensor_tensor_scan(incl[:, :], zr[:, :], tot[:, :], 0.0, ALU.add, ALU.add))
                link(nc.vector.tensor_tensor(incl[:, :], incl[:, :], tot[:, :], ALU.subtract))
                link(nc.vector.tensor_tensor(run[:, :], ps[:, 0:NBX], incl[:, :], ALU.add))
                link(nc.vector.tensor_scalar(below[:, :], incl[:, :], 1.0 / P, None, ALU.mult))

            @block.tensor
            def _(pe):
                pe.wait_ge(s, 2)
                nc.tensor.matmul(ps[:, 0:NBX], v.before[:, :], h1[:, :], start=True, stop=True)
                nc.tensor.matmul(ps[:, 64:64 + NBX], v.ones[:, :], h1[:, :], start=True, stop=True).then_inc(s_pe, 1)


def stage_gate_and_rank(nc, v, e_score, gated, run, posf):
    sem = v.sem
    s_w, s_eT, s_gpe, s_gact, s_y = sem("g_w"), [sem(f"g_eT{u}") for u in range(2)], sem("g_pe"), sem("g_act"), sem("g_y")
    s_idx, s_xg, s_ys, s_es, s_e = sem("g_idx"), [v.pool_dma_sem(f"g_xg{u}") for u in range(2)], [sem(f"g_ys{u}") for u in range(2)], sem("g_es"), sem("g_e")
    s_row, s_rowf = [sem(f"r_row{u}") for u in range(2)], sem("r_rowf")
    s_oh, s_a, s_oht, s_run, s_eq = sem("r_oh"), sem("r_a"), sem("r_oht"), sem("r_run"), sem("r_eq")
    s_look, s_pos, s_m = sem("r_look"), sem("r_pos"), sem("r_m")
    s_one = sem("g_one")
    with ExitStack() as mem:
        sb = lambda n, s, d=F32: mem.enter_context(nc.sbuf_tensor("gr" + n, s, d))
        pb = lambda n, s: mem.enter_context(nc.psum_tensor("gr" + n, s, F32))
        wg, wgb = sb("_wg", [P, W]), sb("_wgb", [1, W])
        eT = sb("_eT", [P, RING, G * P])
        idx = sb("_idx", [P, RING, G], I32)
        xg = sb("_xg", [P, RING, G, W])
        gate = sb("_gate", [P, RING, G, C])
        y = sb("_y", [P, RING, G, C])
        es = sb("_es", [P, RING, G, X8])
        ohlo, ohhi = sb("_ohlo", [P, RING, G, P]), sb("_ohhi", [P, RING, G, NBX])
        row_i, row = sb("_rowi", [1, RING, G * P], I32), sb("_row", [1, RING, G * P])
        oht = sb("_oht", [P, RING, G * P])
        R = sb("_R", [P, RING, G, NBX])
        eq, inr = sb("_eq", [P, P]), sb("_inr", [P, RING, G])
        mul, red = sb("_mul", [P, G, NBX]), sb("_red", [P, G])
        psg = [pb(f"_psg{u}", [P, 2, 512]) for u in range(RING)]
        psk, pst, psu, psl = pb("_psk", [P, 512]), pb("_pst", [P, 512]), pb("_psu", [P, 512]), pb("_psl", [P, 512])
        attr_t, src_row = v.attr_t, v.src_row
        y_out = gated.rearrange("(t p) c -> p t c", p=P)
        H = G // 2

        with nc.Block() as block:
            @block.sync
            def _(sp):
                sp.dma_start(wg[:, 0:C], v.eg_wt).then_inc(s_w, 16)
                sp.dma_start(wg[:, C:W], v.eb_wt).then_inc(s_w, 16)
                sp.dma_start(wgb[:, 0:C], v.eg_b).then_inc(s_w, 16)
                sp.dma_start(wgb[:, C:W], v.eb_b).then_inc(s_w, 16)

                def load(g, u, use):
                    if later(g):
                        sp.wait_ge(s_gpe, g - 1)
                    n = G * P if g is not GE - 1 and not (isinstance(g, int) and g == GE - 1) else E - g * G * P
                    sp.dma_start(eT[:, u, 0:n], attr_t[:, ds(g * (G * P), n)]).then_inc(s_eT[u], 16)
                    if later(g):
                        sp.wait_ge(s_rowf, g - 1)
                    sp.dma_start(row_i[:, u, :], src_row[:, ds(g * (G * P), G * P)]).then_inc(s_row[u], 16)

                def store(g, u, use):
                    sp.wait_ge(s_y, g + 1)
                    sp.dma_start(y_out[:, ds(g * G, G), :], y[:, u, :, :]).then_inc(s_ys[u], 16)

                pipeline(sp, GE, (load, 0), (store, 1))
                for u in range(RING):
                    sp.wait_ge(s_ys[u], 16 * ((GE - u + 1) // 2))

            @block.gpsimd
            def _(pool):
                pool.sem_inc(s_one, 1)

                def gather(g, u, use):
                    if later(g):
                        pool.wait_ge(s_xg[u], use * (16 * G))
                    nc.gpsimd.tensor_copy(idx[:, u, :], v.srci[:, ds(g * G, G)]).then_inc(s_idx, 1)
                    if later(g):
                        pool.wait_ge(s_y, g - 1)
                        pool.wait_ge(s_es, g - 1)
                    pool.wait_ge(s_idx, g + 1)
                    for j in range(G):
                        nc.gpsimd.indirect_dma_start(
                            out=xg[:, u, j, :], out_offset=None, in_=v.table[:, :],
                            in_offset=bass.IndirectOffsetOnAxis(ap=idx[:, u, j:j + 1], axis=0)
                        ).wait_op(s_one, 1, "sem-ge").then_inc(s_xg[u], 16)

                pipeline(pool, GE, (gather, 0))

            @block.tensor
            def _(pe):
                pe.wait_ge(s_w, 64)

                def gates(g, u, use):
                    pe.wait_ge(s_eT[u], use * 16 + 16)
                    if later(g):
                        pe.wait_ge(s_gact, g - 1)
                        pe.wait_ge(s_es, g - 1)
                    for j in range(G):
                        to = psg[u][:, j // H, (j % H) * W:(j % H + 1) * W]
                        nc.tensor.matmul(to, v.ones[0:1, :], wgb[:, :], start=True, stop=False)
                        last = nc.tensor.matmul(to, eT[:, u, j * P:(j + 1) * P], wg[:, :], start=False, stop=True)
                    last.then_inc(s_gpe, 1)

                def ranks(g, u, use):
                    pe.wait_ge(s_rowf, g + 1)
                    pe.wait_ge(s_oh, g * 2 + 2)
                    if later(g, 1):
                        pe.wait_ge(s_eq, g)
                        pe.wait_ge(s_oht, g)
                    nc.tensor.matmul(psk[:, :], v.ones[0:1, :], row[:, u, :], start=True, stop=True)
                    for j in range(G):
                        nc.tensor.transpose(pst[:, j * P:(j + 1) * P], ohlo[:, u, j, :], v.ident[:, :])
                    for j in range(G):
                        for h in range(j + 1):
                            last = nc.tensor.matmul(psu[:, j * NBX:(j + 1) * NBX], ohlo[:, u, h, :],
                                                    ohhi[:, u, h, :], start=(h == 0), stop=(h == j))
                    last.then_inc(s_a, 1)

                def lookups(g, u, use):
                    pe.wait_ge(s_oht, g + 1)
                    pe.wait_ge(s_run, g * 2 + 2)
                    if later(g, 1):
                        pe.wait_ge(s_m, g)
                    for j in range(G):
                        last = nc.tensor.matmul(psl[:, j * NBX:(j + 1) * NBX], oht[:, u, j * P:(j + 1) * P],
                                                R[:, u, j, :], start=True, stop=True)
                    last.then_inc(s_look, 1)

                pipeline(pe, GE, (gates, 0), (ranks, 0), (lookups, 1))

            @block.scalar
            def _(act):
                nc.scalar.preload_act_table(ACT.Sigmoid)

                def rows(g, u, use):
                    act.wait_ge(s_row[u], use * 16 + 16)
                    if later(g):
                        act.wait_ge(s_a, g - 1)
                    nc.scalar.activation(row[:, u, :], row_i[:, u, :], ACT.Copy).then_inc(s_rowf, 1)

                def sigmoid(g, u, use):
                    act.wait_ge(s_gpe, g + 1)
                    if later(g):
                        act.wait_ge(s_y, g - 1)
                    for h in range(2):
                        last = nc.scalar.activation(gate[:, u, h * H:(h + 1) * H, :],
                                                    psg[u][:, h, 0:H * W].rearrange("p (t c) -> p t c", t=H)[:, :, 0:C],
                                                    ACT.Sigmoid)
                    last.then_inc(s_gact, 1)

                def turned(g, u, use):
                    act.wait_ge(s_a, g + 1)
                    if later(g):
                        act.wait_ge(s_look, g - 1)
                    nc.scalar.activation(oht[:, u, :], pst[:, :], ACT.Copy).then_inc(s_oht, 1)

                pipeline(act, GE, (rows, 0), (sigmoid, 0), (turned, 0))

            @block.vector
            def _(dve):
                nc.vector.tensor_copy(R[:, 0, 0, :], run[:, :]).then_inc(s_run, 1)

                def onehots(g, u, use):
                    if later(g):
                        dve.wait_ge(s_a, g - 1)
                        dve.wait_ge(s_m, g - 1)
                    nc.vector.tensor_tensor(ohlo[:, u, :, :], v.iota[:, None, :].broadcast_to([P, G, P]),
                                            v.lo[:, ds(g * G, G), None].broadcast_to([P, G, P]),
                                            ALU.is_equal).then_inc(s_oh, 1)
                    nc.vector.tensor_tensor(ohhi[:, u, :, :], v.iota[:, None, 0:NBX].broadcast_to([P, G, NBX]),
                                            v.hi[:, ds(g * G, G), None].broadcast_to([P, G, NBX]),
                                            ALU.is_equal).then_inc(s_oh, 1)

                def update(g, u, use):
                    dve.wait_ge(s_a, g + 1)
                    dve.wait_ge(s_run, g * 2 + 1)
                    if later(g, 1):
                        dve.wait_ge(s_look, g)
                    counts = psu[:, 0:G * NBX].rearrange("p (t c) -> p t c", t=G)
                    nc.vector.tensor_tensor(R[:, u, 1:G, :], counts[:, 0:G - 1, :],
                                            R[:, u, 0:1, :].broadcast_to([P, G - 1, NBX]), ALU.add).then_inc(s_run, 1)
                    nc.vector.tensor_tensor(R[:, 1 - u, 0, :], counts[:, G - 1, :], R[:, u, 0, :],
                                            ALU.add).then_inc(s_run, 1)
                    for j in range(G):
                        last = nc.vector.scalar_tensor_tensor(
                            eq[:, :], psk[:, j * P:(j + 1) * P], v.srck[:, ds(g * G + j, 1)], v.after[:, :],
                            ALU.is_equal, ALU.mult, accum_out=inr[:, u, j:j + 1])
                        if j < G - 1:
                            last.then_inc(s_e, 1)
                            dve.wait_ge(s_e, g * (G - 1) + j + 1)
                    last.then_inc(s_eq, 1)

                def position(g, u, use):
                    dve.wait_ge(s_look, g + 1)
                    if later(g, 1):
                        dve.wait_ge(s_pos, g * 2)
                    nc.vector.tensor_tensor(mul[:, :, :], psl[:, 0:G * NBX].rearrange("p (t c) -> p t c", t=G),
                                            ohhi[:, u, :, :], ALU.mult).then_inc(s_m, 1)
                    dve.wait_ge(s_m, g + 1)
                    nc.vector.tensor_reduce(red[:, :], mul[:, :, :], AX.X, ALU.add).then_inc(s_pos, 1)
                    dve.wait_ge(s_pos, g * 2 + 1)
                    dve.wait_ge(s_eq, g + 1)
                    nc.vector.tensor_tensor(posf[:, ds(g * G, G)], red[:, :], inr[:, u, :], ALU.add).then_inc(s_pos, 1)

                def gated_rows(g, u, use):
                    dve.wait_ge(s_gact, g + 1)
                    dve.wait_ge(s_xg[u], use * (16 * G) + 16 * G)
                    if later(g):
                        dve.wait_ge(s_ys[u], use * 16)
                    nc.vector.tensor_tensor(y[:, u, :, :], gate[:, u, :, :], xg[:, u, :, 0:C],
                                            ALU.mult).then_inc(s_y, 1)
                    for h in range(2):
                        last = nc.vector.tensor_tensor(
                            es[:, u, h * H:(h + 1) * H, :],
                            psg[u][:, h, 0:H * W].rearrange("p (t c) -> p t c", t=H)[:, :, C:W],
                            xg[:, u, h * H:(h + 1) * H, C:W], ALU.add)
                    last.then_inc(s_es, 1)
                    dve.wait_ge(s_es, g + 1)
                    here = e_score[:, ds(g * G, G), :]
                    nc.vector.tensor_tensor(here, here, es[:, u, :, :], ALU.add)

                pipeline(dve, GE, (position, 2), (onehots, 0), (update, 1), (gated_rows, 1))
                dve.wait_ge(s_run, 2 * GE + 1)
                nc.vector.tensor_copy(run[:, :], R[:, GE % 2, 0, :]).then_inc(s_e, 1)


def stage_scatter(nc, v, posf, run, rows_out):
    sem = v.sem
    s_pi, s_ld, s_meta, s_idx = sem("s_pi"), [sem(f"s_ld{u}") for u in range(2)], sem("s_meta"), sem("s_idx")
    s_sc, s_one, s_lp, s_pad = [v.pool_dma_sem(f"s_sc{u}") for u in range(2)], sem("s_one"), sem("s_lp"), sem("s_pad")
    s_loop = v.pool_dma_sem("s_loop")
    with ExitStack() as mem:
        sb = lambda n, s, d=F32: mem.enter_context(nc.sbuf_tensor("sc" + n, s, d))
        er = sb("_er", [P, RING, G, RW])
        posi, runi = sb("_posi", [P, TR], I32), sb("_runi", [P, NBX], I32)
        idx = sb("_idx", [P, RING, G], I32)
        loops = sb("_loops", [P, NB + 1, RW])
        attr = v.attr[0:(TE - 1) * P, :].rearrange("(t p) c -> p t c", p=P)
        pads = rows_out.rearrange("(t p) c -> p t c", p=P)
        with nc.Block() as block:
            @block.sync
            def _(sp):
                sp.wait_ge(s_lp, 5)
                for t in range(LP, TS):
                    sp.dma_start(pads[:, t:t + 1, :], loops[:, NB:NB + 1, :]).then_inc(s_pad, 16)
                sp.wait_ge(s_pi, 2)

                def load(g, u, use):
                    if later(g):
                        sp.wait_ge(s_sc[u], use * (16 * G))
                    if isinstance(g, int) and g == GE - 1:
                        sp.dma_start(er[:, u, 0:G - 1, 0:C], attr[:, ds(g * G, G - 1), :]).then_inc(s_ld[u], 16)
                        sp.dma_start(er[0:ETAIL, u, G - 1, 0:C], v.attr[(TE - 1) * P:E, :]).then_inc(s_ld[u], 16)
                    else:
                        sp.dma_start(er[:, u, :, 0:C], attr[:, ds(g * G, G), :]).then_inc(s_ld[u], 16)

                pipeline(sp, GE, (load, 0))
                sp.wait_ge(s_pad, 16 * (TS - LP))

            @block.vector
            def _(dve):
                nc.vector.tensor_copy(posi[:, 0:TE], posf[:, 0:TE]).then_inc(s_pi, 1)
                nc.vector.tensor_copy(runi[:, :], run[:, :]).then_inc(s_lp, 1)
                nc.vector.memset(loops[:, :, :], 0.0).then_inc(s_lp, 1)
                dve.wait_ge(s_lp, 2)
                nc.vector.tensor_scalar(loops[:, 0:NB, C + 1], v.blk[:, 0:NB], v.part[:, 0:1], None,
                                        ALU.add).then_inc(s_lp, 1)
                nc.vector.tensor_scalar(loops[:, 0:NB, C + 2], v.blk[:, 0:NB], v.part[:, 0:1], None,
                                        ALU.add).then_inc(s_lp, 1)
                nc.vector.memset(loops[:, NB, C + 1:C + 3], float(PADKEY)).then_inc(s_lp, 1)
                nc.vector.memset(er[:, :, :, :], 1.0).then_inc(s_pi, 1)

                def meta(g, u, use):
                    if later(g):
                        dve.wait_ge(s_sc[u], use * (16 * G))
                    else:
                        dve.wait_ge(s_pi, 2)
                    nc.vector.tensor_copy(er[:, u, :, C + 1], v.dstk[:, ds(g * G, G)]).then_inc(s_meta, 1)
                    nc.vector.tensor_copy(er[:, u, :, C + 2], v.srck[:, ds(g * G, G)]).then_inc(s_meta, 1)

                pipeline(dve, GE, (meta, 0))

            @block.gpsimd
            def _(pool):
                pool.sem_inc(s_one, 1)
                pool.wait_ge(s_pi, 2)

                def scatter(g, u, use):
                    if later(g):
                        pool.wait_ge(s_sc[u], use * (16 * G))
                    nc.gpsimd.tensor_copy(idx[:, u, :], posi[:, ds(g * G, G)]).then_inc(s_idx, 1)
                    pool.wait_ge(s_meta, g * 2 + 2)
                    pool.wait_ge(s_ld[u], (use * 16 + 16) + (16 if isinstance(g, int) and g == GE - 1 else 0))
                    pool.wait_ge(s_idx, g + 1)
                    for j in range(G):
                        nc.gpsimd.indirect_dma_start(
                            out=rows_out[:, :], out_offset=bass.IndirectOffsetOnAxis(ap=idx[:, u, j:j + 1], axis=0),
                            in_=er[:, u, j, :], in_offset=None
                        ).wait_op(s_one, 1, "sem-ge").then_inc(s_sc[u], 16)

                pipeline(pool, GE, (scatter, 0))
                pool.wait_ge(s_lp, 5)
                for b in range(NB):
                    nc.gpsimd.indirect_dma_start(
                        out=rows_out[:, :], out_offset=bass.IndirectOffsetOnAxis(ap=runi[:, b:b + 1], axis=0),
                        in_=loops[:, b, :], in_offset=None).then_inc(s_loop, 16)
                pool.wait_ge(s_loop, 16 * NB)
                for u in range(RING):
                    pool.wait_ge(s_sc[u], 16 * G * ((GE - u + 1) // 2))


def stage_flags(nc, v, name, row_dram, fl):
    s_ld, s, s_pe, s_cp = v.sem(name + "_ld"), v.sem(name + "_dve"), v.sem(name + "_pe"), v.sem(name + "_cp")
    n = TR * P
    H = fl.heads
    with ExitStack() as mem:
        sb = lambda m, sh, d=I32: mem.enter_context(nc.sbuf_tensor(name + m, sh, d))
        cur, prev, nxt = sb("_c", [P, KR, P]), sb("_p", [P, KR, P]), sb("_n", [P, KR, P])
        a4 = sb("_a4", [P, 2, KR, H], F32)
        ps = [mem.enter_context(nc.psum_tensor(f"{name}_ps{d}", [P, 4, 512], F32)) for d in range(2)]
        view = lambda off: row_dram[:, off:off + n].rearrange("a (k r p) -> r (a k) p", r=P, p=P)
        with nc.Block() as block:
            @block.sync
            def _(sp):
                sp.dma_start(cur[:, :, :], view(1)).then_inc(s_ld, 16)
                sp.dma_start(prev[:, :, :], view(0)).then_inc(s_ld, 16)
                sp.dma_start(nxt[:, :, :], view(2)).then_inc(s_ld, 16)

            @block.vector
            def _(dve):
                link = chain(dve, s)
                dve.wait_ge(s_ld, 48)
                for d, (other, r, g) in enumerate(((prev, fl.rf, fl.gf), (nxt, fl.rb, fl.gb))):
                    way = slice(None, None, -1) if d else slice(None)
                    edge = P - 1 if d else 0
                    link(nc.vector.tensor_tensor(r[:, :, :], cur[:, :, :], other[:, :, :], ALU.not_equal))
                    link(nc.vector.tensor_scalar(r[:, :, :], r[:, :, :], -BIG, None, ALU.mult))
                    for k in range(KR):
                        last = nc.vector.tensor_tensor_scan(g[:, k, way], v.zeros[:, :], r[:, k, way], 0.0,
                                                            ALU.add, ALU.min)
                    link(last)
                    link(nc.vector.memset(r[:, :, edge:edge + 1], -BIG))
                    link(nc.vector.tensor_copy(a4[:, d, :, :], g[:, :, P - 1 - edge:P - edge].broadcast_to([P, KR, H])))
                dve.wait_ge(s_pe, 1)
                for d, a in enumerate((fl.af, fl.ab)):
                    nc.vector.tensor_copy(a[:, :], ps[d][0:H, :, :].rearrange("p a c -> p (a c)")[:, 0:TR]).then_inc(s_cp, 1)

            @block.tensor
            def _(pe):
                pe.wait_ge(s, 10)
                for d in range(2):
                    for k in range(KR):
                        last = nc.tensor.transpose(ps[d][0:H, k // 4, (k % 4) * P:(k % 4 + 1) * P], a4[:, d, k, :],
                                                   v.ident[:, :])
                last.then_inc(s_pe, 1)


def stage_turn(nc, v, name, heads, source, target):
    s_t, s_c = v.sem(name + "_t"), v.sem(name + "_c")
    with ExitStack() as mem:
        ps = [mem.enter_context(nc.psum_tensor(f"{name}_ps{u}", [P, 512], F32)) for u in range(4)]
        jobs = [(h, k) for h in range(heads) for k in range(KR)]
        with nc.Block() as block:
            @block.tensor
            def _(pe):
                for n, (h, k) in enumerate(jobs):
                    if n >= 4:
                        pe.wait_ge(s_c, n - 3)
                    nc.tensor.transpose(ps[n % 4][:, 0:P], source(h, k), v.ident[:, :]).then_inc(s_t, 1)

            @block.scalar
            def _(act):
                for n, (h, k) in enumerate(jobs):
                    act.wait_ge(s_t, n + 1)
                    nc.scalar.activation(target(h, k), ps[n % 4][:, 0:P], ACT.Copy).then_inc(s_c, 1)


class Segments:
    DVE = 9

    def __init__(self, nc, v, mem, name, fl):
        self.nc, self.v, self.fl, self.heads = nc, v, fl, fl.heads
        H = fl.heads
        sb = lambda m, sh: mem.enter_context(nc.sbuf_tensor(name + m, sh, F32))
        self.V = sb("_V", [P, H, 1 + TR])
        self.before, self.behind = sb("_bef", [P, H, TR]), sb("_beh", [P, H, TR])
        self.ends = sb("_ends", [P, 2, KR, H])
        self.carry = [sb("_cf", [H, 1 + TR]), sb("_cb", [H, 1 + TR])]
        self.inn = sb("_in", [P, 2, KR, H])
        self.s, self.s_pe = v.sem(name + "_seg"), v.sem(name + "_segpe")
        self.name = name

    def psum(self, mem):
        self.ps = [mem.enter_context(self.nc.psum_tensor(f"{self.name}_psc{d}", [P, 4, 512], F32)) for d in range(2)]

    def dve_setup(self, dve, sem):
        nc = self.nc
        nc.vector.memset(self.V[:, :, 0:1], -BIG).then_inc(sem, 1)
        nc.vector.memset(self.carry[0][:, 0:1], -BIG).then_inc(sem, 1)
        nc.vector.memset(self.carry[1][:, TR:TR + 1], -BIG).then_inc(sem, 1)

    def dve(self, dve, it):
        nc, fl, V = self.nc, self.fl, self.V
        at = lambda n: dve.wait_ge(self.s, it * self.DVE + n)
        rows = lambda ap: ap.rearrange("p (k c) -> p k c", c=P)
        rf, rb = (x[:, :, :].rearrange("p k c -> p (k c)") for x in (fl.rf, fl.rb))
        for h in range(self.heads):
            last = nc.vector.tensor_tensor_scan(self.before[:, h, :], V[:, h, 0:TR], rf, -BIG, ALU.max, ALU.add)
        last.then_inc(self.s, 1)
        for h in range(self.heads):
            last = nc.vector.tensor_tensor_scan(self.behind[:, h, ::-1], rb[:, ::-1], V[:, h, TR:0:-1], -BIG,
                                                ALU.add, ALU.max)
        last.then_inc(self.s, 1)
        at(2)
        for h in range(self.heads):
            nc.vector.tensor_tensor(self.ends[:, 0, :, h], rows(self.before[:, h, :])[:, :, P - 1],
                                    rows(V[:, h, 1:1 + TR])[:, :, P - 1], ALU.max)
            last = nc.vector.tensor_copy(self.ends[:, 1, :, h], rows(self.behind[:, h, :])[:, :, 0])
        last.then_inc(self.s, 1)
        dve.wait_ge(self.s_pe, it * 2 + 1)
        wide = lambda d: self.ps[d][0:self.heads, :, :].rearrange("p a c -> p (a c)")[:, 0:TR]
        nc.vector.tensor_tensor_scan(self.carry[0][:, 1:1 + TR], fl.af[:, :], wide(0), -BIG, ALU.add,
                                     ALU.max).then_inc(self.s, 1)
        nc.vector.tensor_tensor_scan(self.carry[1][:, 0:TR][:, ::-1], fl.ab[:, ::-1], wide(1)[:, ::-1], -BIG,
                                     ALU.add, ALU.max).then_inc(self.s, 1)
        dve.wait_ge(self.s_pe, it * 2 + 2)
        for d in range(2):
            nc.vector.tensor_copy(self.inn[:, d, :, :].rearrange("p k h -> p (k h)"),
                                  self.ps[d][:, 0, 0:KR * self.heads]).then_inc(self.s, 1)
        at(7)
        for d, (g, to) in enumerate(((fl.gf, self.before), (fl.gb, self.behind))):
            for h in range(self.heads):
                for k in range(KR):
                    here = rows(to[:, h, :])[:, k, :]
                    last = nc.vector.scalar_tensor_tensor(here, g[:, k, :], self.inn[:, d, k, h:h + 1], here,
                                                          ALU.add, ALU.max)
            last.then_inc(self.s, 1)
        at(9)

    def pe(self, pe, it):
        nc, v = self.nc, self.v
        pe.wait_ge(self.s, it * self.DVE + 3)
        for d in range(2):
            for k in range(KR):
                last = nc.tensor.transpose(self.ps[d][0:self.heads, k // 4, (k % 4) * P:(k % 4 + 1) * P],
                                           self.ends[:, d, k, :], v.ident[:, :])
        last.then_inc(self.s_pe, 1)
        pe.wait_ge(self.s, it * self.DVE + 5)
        H = self.heads
        for d in range(2):
            for k in range(KR):
                last = nc.tensor.transpose(self.ps[d][:, 0, k * H:(k + 1) * H],
                                           self.carry[d][:, d + k * P:d + (k + 1) * P], v.ident[0:H, 0:H])
                if not d and not k:
                    last.wait_op(v.s_in, 16, "sem-ge")
        last.then_inc(self.s_pe, 1)


def stage_softmax(nc, v, name, e, first_head, fl):
    H = fl.heads
    with ExitStack() as mem:
        seg = Segments(nc, v, mem, name, fl)
        stage_turn(nc, v, name + "r", H, lambda h, k: e[:, k * P:(k + 1) * P, first_head + h],
                   lambda h, k: seg.V[:, h, 1 + k * P:1 + (k + 1) * P])
        s0, s1, s2 = v.sem(name + "_0"), v.sem(name + "_1"), v.sem(name + "_2")
        with ExitStack() as banks, nc.Block() as block:
            seg.psum(banks)
            @block.vector
            def _(dve):
                seg.dve_setup(dve, s0)
                dve.wait_ge(s0, 3)
                seg.dve(dve, 0)
                nc.vector.tensor_tensor(seg.before[:, :, :], seg.before[:, :, :], seg.behind[:, :, :],
                                        ALU.max).then_inc(s1, 1)
                dve.wait_ge(s1, 1)
                nc.vector.tensor_tensor(seg.before[:, :, :], seg.V[:, :, 1:1 + TR], seg.before[:, :, :],
                                        ALU.subtract).then_inc(s1, 1)

            @block.tensor
            def _(pe):
                seg.pe(pe, 0)

            @block.scalar
            def _(act):
                act.wait_ge(s1, 2)
                nc.scalar.activation(seg.behind[:, :, :], seg.before[:, :, :], ACT.Exp).then_inc(s2, 1)
        stage_turn(nc, v, name + "t", H, lambda h, k: seg.behind[:, h, k * P:(k + 1) * P],
                   lambda h, k: e[:, k * P:(k + 1) * P, first_head + h])


def stage_top8(nc, v, name, e, first_head, fl, top):
    H = fl.heads
    with ExitStack() as mem:
        seg = Segments(nc, v, mem, name, fl)
        orig = mem.enter_context(nc.sbuf_tensor(name + "_orig", [P, H, TR], F32))
        stage_turn(nc, v, name + "r", H, lambda h, k: e[:, k * P:(k + 1) * P, first_head + h],
                   lambda h, k: seg.V[:, h, 1 + k * P:1 + (k + 1) * P])
        s0, s1, s2, s3, s_k = (v.sem(f"{name}_{n}") for n in range(5))
        V = seg.V[:, :, 1:1 + TR]

        def knock_out(dve, it):
            nc.vector.tensor_tensor(seg.behind[:, :, :], V, seg.behind[:, :, :], ALU.is_ge).then_inc(s_k, 1)
            nc.vector.tensor_tensor(seg.before[:, :, :], V, seg.before[:, :, :], ALU.is_gt).then_inc(s_k, 1)
            dve.wait_ge(s_k, it * 4 + 2)
            nc.vector.tensor_tensor(seg.before[:, :, :], seg.behind[:, :, :], seg.before[:, :, :],
                                    ALU.mult).then_inc(s_k, 1)
            dve.wait_ge(s_k, it * 4 + 3)
            nc.vector.scalar_tensor_tensor(V, seg.before[:, :, :], -2 * BIG, V, ALU.mult, ALU.add).then_inc(s_k, 1)
            dve.wait_ge(s_k, it * 4 + 4)

        with ExitStack() as banks, nc.Block() as block:
            seg.psum(banks)
            @block.vector
            def _(dve):
                seg.dve_setup(dve, s0)
                dve.wait_ge(s0, 3)
                seg.dve(dve, 0)
                nc.vector.tensor_tensor(orig[:, :, :], seg.before[:, :, :], seg.behind[:, :, :],
                                        ALU.max).then_inc(s1, 1)
                dve.wait_ge(s1, 1)
                nc.vector.tensor_tensor(orig[:, :, :], V, orig[:, :, :], ALU.subtract).then_inc(s1, 1)
                dve.wait_ge(s1, 2)
                knock_out(dve, 0)
                with dve.Fori(1, top) as it:
                    seg.dve(dve, it)
                    knock_out(dve, it)
                nc.vector.tensor_scalar(seg.behind[:, :, :], V, -1.5 * BIG, None, ALU.is_lt).then_inc(s1, 1)
                dve.wait_ge(s1, 3)
                dve.wait_ge(s2, 1)
                nc.vector.tensor_tensor(seg.before[:, :, :], orig[:, :, :], seg.behind[:, :, :],
                                        ALU.mult).then_inc(s1, 1)

            @block.tensor
            def _(pe):
                seg.pe(pe, 0)
                with pe.Fori(1, top) as it:
                    seg.pe(pe, it)

            @block.scalar
            def _(act):
                act.wait_ge(s1, 2)
                nc.scalar.activation(orig[:, :, :], orig[:, :, :], ACT.Exp).then_inc(s2, 1)
        stage_turn(nc, v, name + "t", H, lambda h, k: seg.before[:, h, k * P:(k + 1) * P],
                   lambda h, k: e[:, k * P:(k + 1) * P, first_head + h])


def stage_aggregate(nc, v, name, rows, cols, keys, steps, n_steps, groups, weights, heads, acc):
    s_z, s_ld, s_kr, s_oh = v.sem(name + "_z"), [v.sem(f"{name}_ld{u}") for u in range(2)], v.sem(name + "_kr"), v.sem(name + "_oh")
    s_w, s_wc, s_mm, s_add = v.sem(name + "_w"), v.sem(name + "_wc"), v.sem(name + "_mm"), v.sem(name + "_add")
    width = C + heads
    with ExitStack() as mem:
        sb = lambda n, sh, d=F32: mem.enter_context(nc.sbuf_tensor(name + n, sh, d))
        buf = sb("_buf", [P, RING, G, C])
        krel, oh = sb("_kr", [P, RING, G]), sb("_oh", [P, RING, G, P])
        wrow = sb("_wrow", [P, RING, G, width]) if heads else buf
        ps = [mem.enter_context(nc.psum_tensor(f"{name}_ps{u}", [P, 512], F32)) for u in range(RING)]
        src = rows.rearrange("(t p) c -> p t c", p=P)
        with nc.Block() as block:
            @block.sync
            def _(sp):
                def load(k, u, use):
                    g = sp.value_load(steps[0:1, 0, ds(k, 1)], min_val=0, max_val=groups - 1)
                    if later(k):
                        sp.wait_ge(s_w if heads else s_mm, k - 1)
                    sp.dma_start(buf[:, u, :, :], src[:, ds(g * G, G), 0:C]).then_inc(s_ld[u], 16)

                pipeline(sp, n_steps, (load, 0))

            @block.vector
            def _(dve):
                nc.vector.memset(acc[:, :, 0:width], 0.0).then_inc(s_z, 1)

                def prepare(k, u, use):
                    g, b = step_of(dve, steps, k, groups)
                    if later(k):
                        dve.wait_ge(s_mm, k - 1)
                    nc.vector.tensor_scalar(krel[:, u, :], keys[:, ds(g * G, G)], v.blk[:, ds(b, 1)], None,
                                            ALU.subtract).then_inc(s_kr, 1)
                    dve.wait_ge(s_kr, k + 1)
                    nc.vector.tensor_tensor(oh[:, u, :, :], v.iota[:, None, :].broadcast_to([P, G, P]),
                                            krel[:, u, :, None].broadcast_to([P, G, P]),
                                            ALU.is_equal).then_inc(s_oh, 1)
                    if heads:
                        dve.wait_ge(s_ld[u], use * 16 + 16)
                        for j in range(G):
                            last = nc.vector.tensor_tensor(
                                wrow[:, u, j, 0:C].rearrange("p (h c) -> p h c", h=heads),
                                buf[:, u, j, :].rearrange("p (h c) -> p h c", h=heads),
                                weights[:, ds(g * G + j, 1), 0:heads].rearrange("p a h -> p (a h)")[:, :, None]
                                .broadcast_to([P, heads, C // heads]), ALU.mult)
                        last.then_inc(s_w, 1)

                def add(k, u, use):
                    b = dve.value_load(steps[0:1, 1, ds(k, 1)], min_val=0, max_val=NBX - 1)
                    dve.wait_ge(s_mm, k + 1)
                    if later(k, 1):
                        dve.wait_ge(s_add, k)
                    else:
                        dve.wait_ge(s_z, 1)
                    here = flat(acc[:, ds(b, 1), 0:width])
                    nc.vector.tensor_tensor(here, here, ps[u][:, 0:width], ALU.add).then_inc(s_add, 1)

                pipeline(dve, n_steps, (prepare, 0), (add, 1))

            if heads:
                @block.scalar
                def _(act):
                    nc.scalar.preload_act_table(ACT.Copy)

                    def put(k, u, use):
                        g = act.value_load(steps[0:1, 0, ds(k, 1)], min_val=0, max_val=groups - 1)
                        if later(k):
                            act.wait_ge(s_mm, k - 1)
                            act.wait_ge(s_z, 1)
                        nc.scalar.activation(wrow[:, u, :, C:width], weights[:, ds(g * G, G), 0:heads],
                                             ACT.Copy).then_inc(s_wc, 1)

                    pipeline(act, n_steps, (put, 0))

            @block.tensor
            def _(pe):
                def sums(k, u, use):
                    pe.wait_ge(s_oh, k + 1)
                    if heads:
                        pe.wait_ge(s_w, k + 1)
                        pe.wait_ge(s_wc, k + 1)
                    else:
                        pe.wait_ge(s_ld[u], use * 16 + 16)
                    if later(k):
                        pe.wait_ge(s_add, k - 1)
                    for j in range(G):
                        last = nc.tensor.matmul(ps[u][:, 0:width], oh[:, u, j, :], wrow[:, u, j, 0:width],
                                                start=(j == 0), stop=(j == G - 1))
                    last.then_inc(s_mm, 1)

                pipeline(pe, n_steps, (sums, 0))


def normalise(nc, link, act_sqrt, Z, T, m, r):
    wide = lambda a: a[:, :, None].broadcast_to([P, NBX, C])
    link(nc.vector.tensor_reduce(m[:, :], Z[:, :, :], AX.X, ALU.add))
    link(nc.vector.tensor_scalar(m[:, :], m[:, :], 1.0 / C, None, ALU.mult))
    link(nc.vector.tensor_tensor(Z[:, :, :], Z[:, :, :], wide(m), ALU.subtract))
    link(nc.vector.tensor_tensor(T, Z[:, :, :], Z[:, :, :], ALU.mult))
    link(nc.vector.tensor_reduce(r[:, :], T, AX.X, ALU.add))
    link(nc.vector.tensor_scalar(r[:, :], r[:, :], 1.0 / C, LN_EPS, ALU.mult, ALU.add))
    act_sqrt(r)
    link(nc.vector.reciprocal(r[:, :], r[:, :]))
    link(nc.vector.tensor_tensor(Z[:, :, :], Z[:, :, :], wide(r), ALU.mult))


def stage_update(nc, v, name, acc, heads, floor, inner):
    s, s_rt, s_sq, s_ex, s_gb = (v.sem(f"{name}_{n}") for n in ("dve", "rt", "sq", "ex", "gb"))
    with ExitStack() as mem:
        sb = lambda n, sh, d=F32: mem.enter_context(nc.sbuf_tensor(name + n, sh, d))
        Z, T = sb("_Z", [P, NBX, C]), sb("_T", [P, NBX, C])
        m, r, inv = sb("_m", [P, NBX]), sb("_r", [P, NBX]), sb("_inv", [P, NBX, X8])
        gb = sb("_gbt", [P, 2, C])
        roots = []
        with nc.Block() as block:
            if inner == "norm":
                @block.sync
                def _(sp):
                    sp.dma_start(gb[:, 0, :], v.ln_g.broadcast_to([P, C])).then_inc(s_gb, 16)
                    sp.dma_start(gb[:, 1, :], v.ln_b.broadcast_to([P, C])).then_inc(s_gb, 16)

            @block.vector
            def _(dve):
                link = chain(dve, s)

                def act_sqrt(x):
                    dve.sem_inc(s_rt, 1)
                    roots.append(x)
                    dve.wait_ge(s_sq, len(roots))

                if heads:
                    link(nc.vector.tensor_scalar(inv[:, :, 0:heads], acc[:, :, C:C + heads], floor, None, ALU.max))
                    link(nc.vector.reciprocal(inv[:, :, 0:heads], inv[:, :, 0:heads]))
                    for h in range(heads):
                        n = C // heads
                        last = nc.vector.tensor_tensor(Z[:, :, h * n:(h + 1) * n], acc[:, :, h * n:(h + 1) * n],
                                                       inv[:, :, h:h + 1].broadcast_to([P, NBX, n]), ALU.mult)
                    link(last)
                if inner == "norm":
                    link(nc.vector.tensor_tensor(Z[:, :, :], Z[:, :, :], v.X[:, :, :], ALU.add))
                    normalise(nc, link, act_sqrt, Z, T[:, :, :], m, r)
                    dve.wait_ge(s_gb, 32)
                    link(nc.vector.tensor_tensor(Z[:, :, :], Z[:, :, :], gb[:, 0:1, :].broadcast_to([P, NBX, C]),
                                                 ALU.mult))
                    link(nc.vector.tensor_tensor(Z[:, :, :], Z[:, :, :], gb[:, 1:2, :].broadcast_to([P, NBX, C]),
                                                 ALU.add))
                if inner == "elu":
                    link(nc.vector.tensor_scalar(T[:, :, :], Z[:, :, :], 0.0, None, ALU.min))
                    dve.sem_inc(s_ex, 1)
                    link(nc.vector.tensor_scalar(Z[:, :, :], Z[:, :, :], 0.0, -1.0, ALU.max, ALU.add))
                    dve.wait_ge(s_sq, 1)
                    link(nc.vector.tensor_tensor(Z[:, :, :], Z[:, :, :], T[:, :, :], ALU.add))
                    roots.append(None)
                link(nc.vector.tensor_tensor(v.X[:, :, :], Z[:, :, :] if heads else acc[:, :, 0:C], v.X[:, :, :],
                                             ALU.add))
                normalise(nc, link, act_sqrt, v.X, T[:, :, :], m, r)

            @block.scalar
            def _(act):
                if inner == "elu":
                    act.wait_ge(s_ex, 1)
                    nc.scalar.activation(T[:, :, :], T[:, :, :], ACT.Exp).then_inc(s_sq, 1)
                for n in range(1 + (inner == "norm")):
                    act.wait_ge(s_rt, n + 1)
                    nc.scalar.activation(r[:, :], r[:, :], ACT.Sqrt).then_inc(s_sq, 1)


def stage_leaky(nc, v, name, e):
    s = v.sem(name)
    with nc.Block() as block:
        @block.vector
        def _(dve):
            nc.vector.scalar_tensor_tensor(e, e, 0.2, e, ALU.mult, ALU.max).then_inc(s, 1)


def stage_gather(nc, v, name, idx_all, rows_out, scores_out, width):
    s_idx, s_one, s_cp = v.sem(name + "_idx"), v.sem(name + "_one"), v.sem(name + "_cp")
    s_xg = [v.pool_dma_sem(f"{name}_xg{u}") for u in range(RING)]
    s_st = [v.sem(f"{name}_st{u}") for u in range(RING)]
    with ExitStack() as mem:
        idx = mem.enter_context(nc.sbuf_tensor(name + "_idx", [P, RING, G], I32))
        xg = mem.enter_context(nc.sbuf_tensor(name + "_xg", [P, RING, G, W], F32))
        out = rows_out.rearrange("(t p) c -> p t c", p=P)
        with nc.Block() as block:
            @block.gpsimd
            def _(pool):
                pool.sem_inc(s_one, 1)

                def gather(g, u, use):
                    if later(g):
                        pool.wait_ge(s_xg[u], use * (16 * G))
                    nc.gpsimd.tensor_copy(idx[:, u, :], idx_all[:, ds(g * G, G)]).then_inc(s_idx, 1)
                    if later(g):
                        pool.wait_ge(s_st[u], use * 16)
                        pool.wait_ge(s_cp, g - 1)
                    pool.wait_ge(s_idx, g + 1)
                    for j in range(G):
                        nc.gpsimd.indirect_dma_start(
                            out=xg[:, u, j, :], out_offset=None, in_=v.table[:, :],
                            in_offset=bass.IndirectOffsetOnAxis(ap=idx[:, u, j:j + 1], axis=0)
                        ).wait_op(s_one, 1, "sem-ge").then_inc(s_xg[u], 16)

                pipeline(pool, GS, (gather, 0))

            @block.vector
            def _(dve):
                def scores(g, u, use):
                    dve.wait_ge(s_xg[u], use * (16 * G) + 16 * G)
                    nc.vector.tensor_scalar(scores_out[:, ds(g * G, G), 0:width], xg[:, u, :, C:C + width], 0.0,
                                            None, ALU.add).then_inc(s_cp, 1)

                pipeline(dve, GS, (scores, 0))

            @block.sync
            def _(sp):
                def store(g, u, use):
                    sp.wait_ge(s_xg[u], use * (16 * G) + 16 * G)
                    sp.dma_start(out[:, ds(g * G, G), :], xg[:, u, :, 0:C]).then_inc(s_st[u], 16)

                pipeline(sp, GS, (store, 0))
                for u in range(RING):
                    sp.wait_ge(s_st[u], 16 * ((GS - u + 1) // 2))


def stage_sorted_keys(nc, v, flag):
    s_ld, s, s_t, s_c, s_st = (v.sem("k_" + n) for n in ("ld", "dve", "t", "c", "st"))
    with ExitStack() as mem:
        meta = mem.enter_context(nc.sbuf_tensor("k_meta", [P, TS, RW - C], F32))
        rows = mem.enter_context(nc.sbuf_tensor("k_rows", [P, KR, P], I32))
        ps = [mem.enter_context(nc.psum_tensor(f"k_ps{u}", [P, 512], F32)) for u in range(2)]
        view = v.sorted.rearrange("(t p) c -> p t c", p=P)
        with nc.Block() as block:
            @block.sync
            def _(sp):
                for n in range(KR):
                    sp.dma_start(meta[:, n * P:(n + 1) * P, :], view[:, n * P:(n + 1) * P, C:RW]).then_inc(s_ld, 16)
                sp.wait_ge(s_c, KR)
                sp.dma_start(v.sorted_row[:, 1:1 + TS * P].rearrange("a (k r p) -> r (a k) p", r=P, p=P),
                             rows[:, :, :]).then_inc(s_st, 16)
                sp.wait_ge(s_st, 16)

            @block.vector
            def _(dve):
                dve.wait_ge(s_ld, 16 * KR)
                nc.vector.tensor_copy(v.srck[:, :], meta[:, :, 2]).then_inc(s, 1)
                nc.vector.tensor_copy(v.dsti[:, :], meta[:, :, 1]).then_inc(s, 1)
                nc.vector.tensor_copy(flag[:, :], meta[:, :, 0]).then_inc(s, 1)
                for k in range(KR):
                    dve.wait_ge(s_t, k + 1)
                    nc.vector.tensor_copy(rows[:, k, :], ps[k % 2][:, 0:P]).then_inc(s_c, 1)

            @block.tensor
            def _(pe):
                pe.wait_ge(s, 1)
                for k in range(KR):
                    if k >= 2:
                        pe.wait_ge(s_c, k - 1)
                    nc.tensor.transpose(ps[k % 2][:, 0:P], v.srck[:, k * P:(k + 1) * P], v.ident[:, :]).then_inc(s_t, 1)


def stage_clipped_weights(nc, v, e, other, flag):
    s, s2 = v.sem("cw"), v.sem("cw_e")
    a, b = e[:, :, 0], other[:, :, 0]
    with nc.Block() as block:
        @block.vector
        def _(dve):
            link = chain(dve, s)
            link(nc.vector.tensor_tensor(a, a, b, ALU.add))
            link(nc.vector.scalar_tensor_tensor(a, a, 0.2, a, ALU.mult, ALU.max))
            link(nc.vector.tensor_scalar(a, a, -2.0, 2.0, ALU.max, ALU.min))
            dve.wait_ge(s2, 1)
            link(nc.vector.tensor_tensor(a, a, flag[:, :], ALU.mult))

        @block.scalar
        def _(act):
            act.wait_ge(s, 3)
            nc.scalar.activation(a, a, ACT.Exp).then_inc(s2, 1)


def stage_add_leaky(nc, v, e, other):
    s = v.sem("al")
    with nc.Block() as block:
        @block.vector
        def _(dve):
            link = chain(dve, s)
            e2, o2 = flat(e[:, :, :]), flat(other[:, :, :])
            link(nc.vector.tensor_tensor(e2, e2, o2, ALU.add))
            link(nc.vector.scalar_tensor_tensor(e2, e2, 0.2, e2, ALU.mult, ALU.max))


def stage_mlp(nc, v, aggr):
    NX = NBX * P
    CH = 400
    NCH = NX // CH
    s_w, s_z = v.sem("m_w"), v.sem("m_z")
    names = ["wx", "wa", "wg", "m1", "m2", "m3"]
    with ExitStack() as mem:
        sb = lambda n, sh, d=F32: mem.enter_context(nc.sbuf_tensor("m" + n, sh, d))
        wt = {n: sb("_" + n, [P, C]) for n in names}
        gf, bc, b1, b2, b3 = sb("_gf", [P, 1]), sb("_bc", [P, 1]), sb("_b1", [P, 1]), sb("_b2", [P, 1]), sb("_b3", [1, C])
        xt, at, cc = sb("_xt", [P, NX]), sb("_at", [P, NX]), sb("_cc", [P, 1])
        psg = mem.enter_context(nc.psum_tensor("m_psg", [P, 512], F32))
        with nc.Block() as block:
            @block.sync
            def _(sp):
                for n, src in (("wx", v.Wc[0:C, :]), ("wa", v.Wc[C:2 * C, :]), ("wg", v.Wc[2 * C:3 * C, :]),
                               ("m1", v.M1), ("m2", v.M2), ("m3", v.M3)):
                    sp.dma_start(wt[n][:, :], src).then_inc(s_w, 16)
                for t, src in ((gf, v.gf), (bc, v.bc), (b1, v.m1b), (b2, v.m2b), (b3, v.m3b)):
                    sp.dma_start(t[:, :], src).then_inc(s_w, 16)

            @block.tensor
            def _(pe):
                pe.wait_ge(s_w, 16 * 11)
                nc.tensor.matmul(psg[:, 0:1], wt["wg"][:, :], gf[:, :], start=True, stop=True).then_inc(s_z, 1)

            @block.vector
            def _(dve):
                dve.wait_ge(s_z, 1)
                nc.vector.tensor_tensor(cc[:, :], psg[:, 0:1], bc[:, :], ALU.add).then_inc(s_z, 1)

        def transposed(name, source, target):
            s_x, s_t, s_c = v.sem(name + "_x"), v.sem(name + "_t"), v.sem(name + "_c")
            with ExitStack() as m2:
                xs = m2.enter_context(nc.sbuf_tensor(name + "_xs", [P, RING, C], F32))
                ps = [m2.enter_context(nc.psum_tensor(f"{name}_ps{u}", [P, 512], F32)) for u in range(RING)]
                with nc.Block() as block:
                    @block.vector
                    def _(dve):
                        def stage(b, u, use):
                            if later(b):
                                dve.wait_ge(s_t, b - 1)
                            nc.vector.tensor_scalar(xs[:, u, :], flat(source[:, ds(b, 1), 0:C]), 0.0, None,
                                                    ALU.add).then_inc(s_x, 1)

                        def put(b, u, use):
                            dve.wait_ge(s_t, b + 1)
                            nc.vector.tensor_scalar(target[:, ds(b * P, P)], ps[u][:, 0:P], 0.0, None,
                                                    ALU.add).then_inc(s_c, 1)

                        pipeline(dve, NBX, (stage, 0), (put, 1))

                    @block.tensor
                    def _(pe):
                        def turn(b, u, use):
                            pe.wait_ge(s_x, b + 1)
                            if later(b):
                                pe.wait_ge(s_c, b - 1)
                            nc.tensor.transpose(ps[u][:, 0:P], xs[:, u, :], v.ident[:, :]).then_inc(s_t, 1)

                        pipeline(pe, NBX, (turn, 0))

        def layer(name, terms, bias, out):
            s_mm, s_o = v.sem(name + "_mm"), v.sem(name + "_o")
            with ExitStack() as m2:
                ps = [m2.enter_context(nc.psum_tensor(f"{name}_ps{u}", [P, 512], F32)) for u in range(RING)]
                with nc.Block() as block:
                    @block.tensor
                    def _(pe):
                        def mm(c, u, use):
                            if later(c):
                                pe.wait_ge(s_o, c - 1)
                            for n, (w, x) in enumerate(terms):
                                last = nc.tensor.matmul(ps[u][:, 0:CH], w[:, :], x[:, ds(c * CH, CH)],
                                                        start=(n == 0), stop=(n == len(terms) - 1))
                            last.then_inc(s_mm, 1)

                        pipeline(pe, NCH, (mm, 0))

                    @block.vector
                    def _(dve):
                        def add(c, u, use):
                            dve.wait_ge(s_mm, c + 1)
                            nc.vector.tensor_scalar(out[:, ds(c * CH, CH)], ps[u][:, 0:CH], bias[:, 0:1], None,
                                                    ALU.add).then_inc(s_o, 1)

                        pipeline(dve, NCH, (add, 0))

        def softplus(name, z, t):
            s, s2 = v.sem(name), v.sem(name + "a")
            with nc.Block() as block:
                @block.vector
                def _(dve):
                    link = chain(dve, s)
                    link(nc.vector.scalar_tensor_tensor(t[:, :], z[:, :], -1.0, z[:, :], ALU.mult, ALU.min))
                    link(nc.vector.tensor_scalar(z[:, :], z[:, :], 0.0, None, ALU.max))
                    dve.wait_ge(s2, 2)
                    link(nc.vector.tensor_tensor(z[:, :], z[:, :], t[:, :], ALU.add))

                @block.scalar
                def _(act):
                    act.wait_ge(s, 1)
                    nc.scalar.activation(t[:, :], t[:, :], ACT.Exp).then_inc(s2, 1)
                    act.wait_ge(s2, 1)
                    nc.scalar.activation(t[:, :], t[:, :], ACT.Ln, bias=1.0).then_inc(s2, 1)

        transposed("mt0", v.X, xt)
        transposed("mt1", aggr, at)
        layer("ml0", [(wt["wx"], xt), (wt["wa"], at)], cc, xt)
        layer("ml1", [(wt["m1"], xt)], b1, at)
        softplus("mp1", at, xt)
        layer("ml2", [(wt["m2"], at)], b2, xt)
        softplus("mp2", xt, at)

        s_x, s_mm, s_o = v.sem("mo_x"), v.sem("mo_mm"), v.sem("mo_o")
        xs = sb("_xs", [P, RING, P])
        ps = [mem.enter_context(nc.psum_tensor(f"mo_ps{u}", [P, 512], F32)) for u in range(RING)]
        with nc.Block() as block:
            @block.vector
            def _(dve):
                def stage(b, u, use):
                    if later(b):
                        dve.wait_ge(s_mm, b - 1)
                    nc.vector.tensor_scalar(xs[:, u, :], xt[:, ds(b * P, P)], 0.0, None, ALU.add).then_inc(s_x, 1)

                def put(b, u, use):
                    dve.wait_ge(s_mm, b + 1)
                    nc.vector.tensor_scalar(flat(aggr[:, ds(b, 1), 0:C]), ps[u][:, 0:C], 0.0, None,
                                            ALU.add).then_inc(s_o, 1)

                pipeline(dve, NBX, (stage, 0), (put, 1))

            @block.tensor
            def _(pe):
                def mm(b, u, use):
                    pe.wait_ge(s_x, b + 1)
                    if later(b):
                        pe.wait_ge(s_o, b - 1)
                    nc.tensor.matmul(ps[u][:, 0:C], v.ones[0:1, :], b3[:, :], start=True, stop=False)
                    nc.tensor.matmul(ps[u][:, 0:C], xs[:, u, :], wt["m3"][:, :], start=False,
                                     stop=True).then_inc(s_mm, 1)

                pipeline(pe, NBX, (mm, 0))


def recycle(nc, v):
    with nc.Block() as block:
        @block.gpsimd
        def _(pool):
            for s in v.layer_sems:
                pool.sem_clear(s)
    for s in v.layer_sems:
        nc.release_semaphore(s)
    v.layer_sems = []


def make_flags(nc, mem, name, heads):
    fl = Env()
    fl.heads = heads
    sb = lambda k, sh: mem.enter_context(nc.sbuf_tensor(f"{name}_{k}", sh, F32))
    fl.rf, fl.rb, fl.gf, fl.gb = (sb(k, [P, KR, P]) for k in ("rf", "rb", "gf", "gb"))
    fl.af, fl.ab = (sb(k, [heads, TR]) for k in ("af", "ab"))
    return fl


def build(nc, v):
    with ExitStack() as ctx:
        def sb(name, shape, dt=F32, mem=ctx):
            return mem.enter_context(nc.sbuf_tensor(name, shape, dt))

        v.layer_sems = []
        v.sem = lambda name: v.layer_sems.append(nc.alloc_semaphore(name=name)) or v.layer_sems[-1]
        v.pool_dma_sem = lambda name: ctx.enter_context(nc.semaphore(name))

        def dram(name, shape, dt=F32):
            return nc.dram_tensor(name, shape, dt, kind="Internal").ap()

        v.s_in = v.pool_dma_sem("inputs")
        v.X = sb("X", [P, NBX, C])
        v.srck, v.dstk = sb("srck", [P, TR]), sb("dstk", [P, TR])
        v.srci = sb("srci", [P, TR], I32)
        v.iota, v.part, v.blk, v.stepn = sb("iota", [P, P]), sb("part", [P, 1]), sb("blk", [P, NBX]), sb("stepn", [P, 512])
        v.ident, v.before, v.after = sb("ident", [P, P]), sb("before", [P, P]), sb("after", [P, P])
        v.ones, v.zeros = sb("ones", [P, P]), sb("zeros", [P, P])
        v.scores = sb("scores", [P, NBX, X8])
        v.rhs = sb("rhs", [P, C + 2 * X8])
        hist, run, below, count = (sb(n, [P, NBX]) for n in ("hist", "run", "below", "count"))
        steps_e, steps_s = sb("steps_e", [1, 2, 512], I32), sb("steps_s", [1, 2, 512], I32)
        v.table = dram("table", (NBX * P, W))
        v.src_row = dram("src_row", (1, TR * P), I32)
        v.dst_row = dram("dst_row", (1, TR * P + 2), I32)
        v.sorted_row = dram("sorted_row", (1, TR * P + 2), I32)
        gated = dram("gated", (TE * P, C))
        gathered = dram("gathered", (TS * P, C))
        v.sorted = dram("sorted", (TS * P, RW))

        with ExitStack() as mem:
            v.iota_i, v.part_i = sb("iota_i", [P, P], I32, mem), sb("part_i", [P, 1], I32, mem)
            v.blk_i, v.stepn_i = sb("blk_i", [P, NBX], I32, mem), sb("stepn_i", [P, 512], I32, mem)
            v.padrow, v.blank = sb("padrow", [1, (TR * P - E) // 2], I32, mem), sb("blank", [1, 1], I32, mem)
            v.dsti = sb("dsti_in", [P, TR], I32, mem)
            stage_constants(nc, v)

        stage_weights(nc, v, "w0", v.W0, v.W0t,
                      [(v.a0[h, 16 * s:16 * s + 16, :], 16 * h, 16, X8 * s + h) for h in range(8) for s in range(2)],
                      v.rhs)
        stage_node_table(nc, v, "t0", v.rhs, v.table, v.scores)
        stage_count_dst(nc, v, count)
        stage_steps(nc, v, "se", count, GE, steps_e)
        with ExitStack() as layer:
            e_score = sb("e_score", [P, TR, X8], F32, layer)
            stage_expand(nc, v, "xe", v.dstk, steps_e, KE, GE, X8, e_score)
            with ExitStack() as mem:
                v.lo, v.hi, posf = (sb(n, [P, TR], F32, mem) for n in ("lo", "hi", "posf"))
                stage_histogram(nc, v, hist)
                stage_bases(nc, v, hist, run, below)
                stage_steps(nc, v, "ss", below, GS, steps_s)
                stage_gate_and_rank(nc, v, e_score, gated, run, posf)
                stage_scatter(nc, v, posf, run, v.sorted)
            with ExitStack() as mem:
                fl = make_flags(nc, mem, "fe", 2)
                stage_flags(nc, v, "fe", v.dst_row, fl)
                stage_leaky(nc, v, "lk0", flat(e_score[:, :, :]))
                for n in range(8 // fl.heads):
                    stage_softmax(nc, v, f"sm{n}", e_score, n * fl.heads, fl)
            acc = sb("acc0", [P, NBX, W], F32, layer)
            stage_aggregate(nc, v, "ag0", gated, C, v.dstk, steps_e, KE, GE, e_score, 8, acc)
            stage_update(nc, v, "up0", acc, 8, 1e-12, "norm")
            if v.dbg == 1:
                return dump(nc, v, acc, steps_s)
        recycle(nc, v)
        v.dsti = sb("dsti", [P, TR], I32)

        with ExitStack() as layer:
            flag = sb("flag", [P, TS], F32, layer)
            stage_sorted_keys(nc, v, flag)
            stage_weights(nc, v, "w1", v.W1, v.W1t, [(v.a1[C:2 * C, :], 0, C, 0), (v.a1[0:C, :], 0, C, X8)], v.rhs)
            stage_node_table(nc, v, "t1", v.rhs, v.table, v.scores)
            e1, o1 = sb("e1", [P, TS, 1], F32, layer), sb("o1", [P, TS, 1], F32, layer)
            stage_expand(nc, v, "x1", v.srck, steps_s, KS, GS, 1, e1)
            stage_gather(nc, v, "g1", v.dsti, gathered, o1, 1)
            stage_clipped_weights(nc, v, e1, o1, flag)
            acc = sb("acc1", [P, NBX, W], F32, layer)
            stage_aggregate(nc, v, "ag1", gathered, C, v.srck, steps_s, KS, GS, e1, 1, acc)
            stage_update(nc, v, "up1", acc, 1, 1e-30, None)
        if v.dbg == 2:
            return dump(nc, v, acc, steps_s)
        recycle(nc, v)

        with ExitStack() as layer:
            acc = sb("acc2", [P, NBX, W], F32, layer)
            stage_aggregate(nc, v, "ag2", v.sorted, RW, v.srck, steps_s, KS, GS, None, 0, acc)
            stage_mlp(nc, v, acc)
            stage_update(nc, v, "up2", acc, 0, None, None)
        if v.dbg == 3:
            return dump(nc, v, acc, steps_s)
        recycle(nc, v)

        stage_weights(nc, v, "w3", v.W3, v.W3t,
                      [(v.a3[h, 32 * (1 - s):32 * (1 - s) + 32, :], 32 * h, 32, X8 * s + h)
                       for h in range(4) for s in range(2)], v.rhs)
        stage_node_table(nc, v, "t3", v.rhs, v.table, v.scores)
        with ExitStack() as layer:
            e3 = sb("e3", [P, TS, 4], F32, layer)
            with ExitStack() as mem:
                o3 = sb("o3", [P, TS, 4], F32, mem)
                stage_expand(nc, v, "x3", v.srck, steps_s, KS, GS, 4, e3)
                stage_gather(nc, v, "g3", v.dsti, gathered, o3, 4)
                stage_add_leaky(nc, v, e3, o3)
            for n in range(2):
                with ExitStack() as mem:
                    fl = make_flags(nc, mem, f"fs{n}", 2)
                    stage_flags(nc, v, f"fs{n}", v.sorted_row, fl)
                    stage_top8(nc, v, f"tk{n}", e3, 2 * n, fl, 8)
            acc = sb("acc3", [P, NBX, W], F32, layer)
            stage_aggregate(nc, v, "ag3", gathered, C, v.srck, steps_s, KS, GS, e3, 4, acc)
            stage_update(nc, v, "up3", acc, 4, 1e-30, "elu")
        if v.dbg == 4:
            return dump(nc, v, acc, steps_s)
        s_out = v.sem("out")
        with nc.Block() as block:
            @block.sync
            def _(sp):
                sp.dma_start(v.out[0:(NB - 1) * P, :].rearrange("(b p) c -> p b c", p=P),
                             v.X[:, 0:NB - 1, :]).then_inc(s_out, 16)
                sp.dma_start(v.out[(NB - 1) * P:N, :], v.X[0:TAIL, NB - 1, :]).then_inc(s_out, 16)
                sp.wait_ge(s_out, 32)


def dump(nc, v, acc, steps):
    s_dbg = v.sem("dbg")
    with nc.Block() as block:
        @block.sync
        def _(sp):
            sp.dma_start(v.out[:, :], v.table[0:N, 0:C]).then_inc(s_dbg, 16)
            sp.dma_start(v.dbg0[:, :], acc[:, :, :].rearrange("p b c -> p (b c)")).then_inc(s_dbg, 16)
            sp.dma_start(v.dbg2[:, :], v.X[:, :, :].rearrange("p b c -> p (b c)")).then_inc(s_dbg, 16)
            sp.wait_ge(s_dbg, 48)


def kernel(**inputs):
    import numpy as np
    import concourse.bacc as bacc
    from concourse.bass_utils import run_bass_kernel_spmd

    nc = bacc.Bacc("TRN2", target_bir_lowering=False, num_devices=1)
    a = {k: np.asarray(x) for k, x in inputs.items()}
    full = (TE - 1) * P
    w0 = a["L0_gnn_W"].transpose(1, 0, 2).reshape(C, C)
    arrays = {
        "x": a["x"], "src": a["src"], "dst": a["dst"],
        "src_t": a["src"][:full].reshape(TE - 1, P).T, "dst_t": a["dst"][:full].reshape(TE - 1, P).T,
        "attr": a["edge_attr_128"], "attr_t": a["edge_attr_128"].T,
        "W0": w0, "W0t": w0.T, "a0": a["L0_gnn_a"],
        "eb_wt": a["L0_gnn_eb_w"].T, "eb_b": a["L0_gnn_eb_b"][None], "eg_wt": a["L0_gnn_eg_w"].T,
        "eg_b": a["L0_gnn_eg_b"][None], "ln_g": a["L0_gnn_ln_g"][None], "ln_b": a["L0_gnn_ln_b"][None],
        "W1": a["L1_gnn_kernel"], "W1t": a["L1_gnn_kernel"].T, "a1": a["L1_gnn_kernel_attention"],
        "gf": a["L2_gnn_global_feat"].T, "Wc": a["L2_gnn_W_c"], "bc": a["L2_gnn_b_c"][:, None],
        "M1": a["L2_gnn_W1"], "m1b": a["L2_gnn_b1"][:, None], "M2": a["L2_gnn_W2"], "m2b": a["L2_gnn_b2"][:, None],
        "M3": a["L2_gnn_W3"], "m3b": a["L2_gnn_b3"][None],
        "W3": a["L3_gnn_W"], "W3t": a["L3_gnn_W"].T, "a3": a["L3_gnn_att"][:, :, None],
    }
    arrays = {k: np.ascontiguousarray(x) for k, x in arrays.items()}
    v = Env()
    for k, x in arrays.items():
        v.__dict__[k] = nc.dram_tensor("in_" + k, x.shape, mybir.dt.from_np(x.dtype), kind="ExternalInput").ap()
    v.out = nc.dram_tensor("out_0", (N, C), F32, kind="ExternalOutput").ap()
    v.dbg = DBG
    if DBG:
        v.dbg0 = nc.dram_tensor("dbg0", (P, NBX * W), F32, kind="ExternalOutput").ap()
        v.dbg2 = nc.dram_tensor("dbg2", (P, NBX * C), F32, kind="ExternalOutput").ap()
    build(nc, v)
    r = run_bass_kernel_spmd(nc, [{"in_" + k: x for k, x in arrays.items()}], core_ids=[0])
    return r.results[0]["out_0"]
```

```python
from contextlib import ExitStack

import concourse.bass as bass
from concourse import mybir

ALU = mybir.AluOpType
ACT = mybir.ActivationFunctionType
F32 = mybir.dt.float32
I32 = mybir.dt.int32
BF16 = mybir.dt.bfloat16
AX = mybir.AxisListType
ds = bass.ds

P = 128
C = 128
N = 6250
E = 206250
NB = -(-N // P)
NBX = NB + 1
NP = NB * P
TE = -(-E // P)
G = 4
GE = TE // G
TR = -(-TE // P) * P
KR = TR // P
TS = TR
GS = TS // G
LP = TE + NB
PADKEY = NP - 1
W = 136
X8 = 8
RW = 132
KE = GE + NB - 1
KS = GS + NB - 1
BIG = 1.0e30
LN_EPS = 1.0e-5
TAIL = N - (NB - 1) * P
ETAIL = E - (TE - 1) * P
assert TE % G == 0 and LP < TS


class Env:
    pass


def stage_constants(nc, v):
    s_set, s_cp, s_io, s_pe = v.sem("c_set"), v.sem("c_cp"), v.sem("c_io"), v.sem("c_iota")
    with nc.Block() as block:
        @block.gpsimd
        def _(pool):
            nc.gpsimd.iota(v.iota_i[:, :], [[1, P]], base=0, channel_multiplier=0).then_inc(s_io, 1)
            nc.gpsimd.iota(v.part_i[:, :], [[0, 1]], base=0, channel_multiplier=1).then_inc(s_io, 1)
            nc.gpsimd.iota(v.blk_i[:, :], [[P, NBX]], base=0, channel_multiplier=0).then_inc(s_io, 1)
            nc.gpsimd.iota(v.stepn_i[:, :], [[1, 512]], base=0, channel_multiplier=0).then_inc(s_io, 1)

        @block.sync
        def _(sp):
            sp.wait_ge(s_set, 7)
            half = (TR * P - E) // 2
            for row, keys, at in ((v.src_row, v.src, 0), (v.dst_row, v.dst, 1)):
                sp.dma_start(row[:, at:at + E], keys[None, :]).then_inc(v.s_in, 16)
                for first in (E + at, E + at + half):
                    sp.dma_start(row[:, first:first + half], v.padrow[:, :]).then_inc(v.s_in, 16)
            for row in (v.dst_row, v.sorted_row):
                sp.dma_start(row[:, 0:1], v.blank[:, 0:1]).then_inc(v.s_in, 16)
                sp.dma_start(row[:, TR * P + 1:TR * P + 2], v.blank[:, 0:1]).then_inc(v.s_in, 16)
            sp.dma_start(v.X[:, 0:NB - 1, :],
                         v.x[0:(NB - 1) * P, :].rearrange("(b p) c -> p b c", p=P)).then_inc(v.s_in, 16)
            sp.dma_start(v.X[0:TAIL, NB - 1, :], v.x[(NB - 1) * P:N, :]).then_inc(v.s_in, 16)
            sp.dma_start(v.srci[:, 0:TE - 1], v.src_t).then_inc(v.s_in, 16)
            sp.dma_start(v.srci[0:ETAIL, TE - 1:TE], v.src[(TE - 1) * P:E, None]).then_inc(v.s_in, 16)
            sp.dma_start(v.dsti[:, 0:TE - 1], v.dst_t).then_inc(v.s_in, 16)
            sp.dma_start(v.dsti[0:ETAIL, TE - 1:TE], v.dst[(TE - 1) * P:E, None]).then_inc(v.s_in, 16)

        @block.vector
        def _(dve):
            nc.vector.memset(v.X[:, NB - 1:NBX, :], 0.0).then_inc(s_set, 1)
            nc.vector.memset(v.srci[:, TE - 1:TR], PADKEY).then_inc(s_set, 1)
            nc.vector.memset(v.dsti[:, TE - 1:TR], PADKEY).then_inc(s_set, 1)
            nc.vector.memset(v.ones[:, :], 1.0).then_inc(s_set, 1)
            nc.vector.memset(v.zeros[:, :], 0.0).then_inc(s_set, 1)
            nc.vector.memset(v.padrow[:, :], PADKEY).then_inc(s_set, 1)
            nc.vector.memset(v.blank[:, :], -1).then_inc(s_set, 1)
            dve.wait_ge(s_io, 4)
            nc.vector.tensor_copy(v.iota[:, :], v.iota_i[:, :]).then_inc(s_cp, 1)
            nc.vector.tensor_copy(v.part[:, :], v.part_i[:, :]).then_inc(s_cp, 1)
            nc.vector.tensor_copy(v.blk[:, :], v.blk_i[:, :]).then_inc(s_cp, 1)
            nc.vector.tensor_copy(v.stepn[:, :], v.stepn_i[:, :]).then_inc(s_cp, 1)
            dve.wait_ge(s_cp, 4)
            nc.vector.tensor_scalar(v.ident[:, :], v.iota[:, :], v.part[:, 0:1], None,
                                    ALU.is_equal).then_inc(s_cp, 1)
            nc.vector.tensor_scalar(v.before[:, :], v.iota[:, :], v.part[:, 0:1], None,
                                    ALU.is_gt).then_inc(s_cp, 1)
            nc.vector.tensor_scalar(v.after[:, :], v.iota[:, :], v.part[:, 0:1], None,
                                    ALU.is_lt).then_inc(s_cp, 1)
            dve.wait_ge(v.s_in, 256)
            nc.vector.tensor_copy(v.srck[:, :], v.srci[:, :]).then_inc(s_cp, 1)
            nc.vector.tensor_copy(v.dstk[:, :], v.dsti[:, :]).then_inc(s_cp, 1)


def stage_weights(nc, v, name, w_dram, wt_dram, vectors, rhs):
    s_z, s_d, s_p, s_e = v.sem(name + "_z"), v.sem(name + "_d"), v.sem(name + "_p"), v.sem(name + "_e")
    with ExitStack() as mem:
        wt = mem.enter_context(nc.sbuf_tensor(name + "_wt", [P, C], F32))
        ab = mem.enter_context(nc.sbuf_tensor(name + "_ab", [P, 2 * X8], F32))
        ps = mem.enter_context(nc.psum_tensor(name + "_ps", [P, 512], F32))
        with nc.Block() as block:
            @block.vector
            def _(dve):
                nc.vector.memset(ab[:, :], 0.0).then_inc(s_z, 1)
                dve.wait_ge(s_p, 1)
                nc.vector.tensor_copy(rhs[:, C:C + 2 * X8], ps[:, 0:2 * X8]).then_inc(s_e, 1)

            @block.sync
            def _(sp):
                sp.dma_start(wt[:, :], wt_dram).then_inc(s_d, 16)
                sp.dma_start(rhs[:, 0:C], w_dram).then_inc(s_d, 16)
                sp.wait_ge(s_z, 1)
                for row, first, n, col in vectors:
                    sp.dma_start(ab[first:first + n, col:col + 1], row).then_inc(s_d, 16)

            @block.tensor
            def _(pe):
                pe.wait_ge(s_d, 16 * (2 + len(vectors)))
                nc.tensor.matmul(ps[:, 0:2 * X8], wt[:, :], ab[:, :], start=True, stop=True).then_inc(s_p, 1)


RING = 2


def pipeline(eng, n, *parts, ring=RING):
    parts = [(p[0], p[1], p[2] if len(p) > 2 else n) for p in parts]
    t, end = 0, max(lag + items for _, lag, items in parts)
    while t < end:
        live = [p for p in parts if t < p[1] + p[2]]
        steady = t % ring == 0 and all(t - lag >= ring for _, lag, _ in live)
        turns = (min(lag + items for _, lag, items in live) - t) // ring if steady else 0
        if turns > 1:
            with eng.Fori(0, turns) as i:
                for r in range(ring):
                    for fn, lag, _ in live:
                        at = t + r - lag
                        fn(i * ring + at, at % ring, i + at // ring)
            t += turns * ring
        else:
            for fn, lag, items in live:
                if t >= lag:
                    fn(t - lag, (t - lag) % ring, (t - lag) // ring)
            t += 1


def later(item, by=RING):
    return not isinstance(item, int) or item >= by


def chain(eng, sem):
    count = [0]

    def link(ins):
        count[0] += 1
        ins.then_inc(sem, 1)
        eng.wait_ge(sem, count[0])
    return link


def flat(ap):
    return ap.rearrange("p a c -> p (a c)")


def stage_node_table(nc, v, name, rhs, table, scores, count=None, loads=()):
    R = 4
    s_x, s_t, s_xt, s_h, s_row, s_sc = (v.sem(f"{name}_{n}") for n in ("x", "t", "xt", "h", "row", "sc"))
    s_st = [v.sem(f"{name}_st{u}") for u in range(R)]
    with ExitStack() as mem:
        xs = mem.enter_context(nc.sbuf_tensor(name + "_xs", [P, R, C], F32))
        xt = mem.enter_context(nc.sbuf_tensor(name + "_xt", [P, R, P], F32))
        row = mem.enter_context(nc.sbuf_tensor(name + "_row", [P, R, W + X8], F32))
        pst = [mem.enter_context(nc.psum_tensor(f"{name}_pst{u}", [P, 512], F32)) for u in range(R)]
        psh = [mem.enter_context(nc.psum_tensor(f"{name}_psh{u}", [P, 512], F32)) for u in range(R)]
        if count is not None:
            s_cnt = v.sem(name + "_cnt")
            junk = mem.enter_context(nc.sbuf_tensor(name + "_junk", [P, TR], F32))
        out = table.rearrange("(b p) w -> p b w", p=P)
        with nc.Block() as block:
            @block.vector
            def _(dve):
                def stage(b, u, use):
                    if later(b, R):
                        dve.wait_ge(s_t, b - R + 1)
                    nc.vector.tensor_scalar(xs[:, u, :], flat(v.X[:, ds(b, 1), :]), 0.0, None,
                                            ALU.add).then_inc(s_x, 1)

                def put(b, u, use):
                    dve.wait_ge(s_row, b + 1)
                    nc.vector.tensor_scalar(flat(scores[:, ds(b, 1), :]), row[:, u, W:W + X8], 0.0, None,
                                            ALU.add).then_inc(s_sc, 1)

                def below(b, u, use):
                    if later(b, 1):
                        dve.wait_ge(s_cnt, b)
                    nc.vector.tensor_scalar(junk[:, :], v.dstk, v.blk[:, ds(b, 1)], None, ALU.is_lt, ALU.add,
                                            accum_out=count[:, ds(b, 1)]).then_inc(s_cnt, 1)

                side = [(below, 0)] if count is not None else []
                pipeline(dve, NBX, (stage, 0), *side, (put, 2), ring=R)

            @block.tensor
            def _(pe):
                def turn(b, u, use):
                    if later(b, R):
                        pe.wait_ge(s_xt, b - R + 1)
                    pe.wait_ge(s_x, b + 1)
                    nc.tensor.transpose(pst[u][:, 0:P], xs[:, u, :], v.ident[:, :]).then_inc(s_t, 1)

                def product(b, u, use):
                    if later(b, R):
                        pe.wait_ge(s_row, b - R + 1)
                    pe.wait_ge(s_xt, b + 1)
                    nc.tensor.matmul(psh[u][:, 0:W + X8], xt[:, u, :], rhs[:, :], start=True,
                                     stop=True).then_inc(s_h, 1)

                pipeline(pe, NBX, (turn, 0), (product, 1), ring=R)

            @block.scalar
            def _(act):
                nc.scalar.preload_act_table(ACT.Copy)
                for to, source, signal in loads:
                    act.dma_start(to, source).then_inc(signal, 16)

                def copy(b, u, use):
                    if later(b, R):
                        act.wait_ge(s_h, b - R + 1)
                    act.wait_ge(s_t, b + 1)
                    nc.scalar.activation(xt[:, u, :], pst[u][:, 0:P], ACT.Copy).then_inc(s_xt, 1)

                def rows(b, u, use):
                    if later(b, R):
                        act.wait_ge(s_st[u], use * 16)
                        act.wait_ge(s_sc, b - R + 1)
                    act.wait_ge(s_h, b + 1)
                    nc.scalar.activation(row[:, u, :], psh[u][:, 0:W + X8], ACT.Copy).then_inc(s_row, 1)

                pipeline(act, NBX, (copy, 0), (rows, 2), ring=R)

            @block.sync
            def _(sp):
                def store(b, u, use):
                    sp.wait_ge(s_row, b + 1)
                    sp.dma_start(out[:, ds(b, 1), :], row[:, u:u + 1, 0:W]).then_inc(s_st[u], 16)

                pipeline(sp, NBX, (store, 0), ring=R)
                for u in range(R):
                    sp.wait_ge(s_st[u], 16 * ((NBX - u + R - 1) // R))


def stage_steps(nc, v, name, count, groups, steps):
    s_dve, s_pe = v.sem(name + "_dve"), v.sem(name + "_pe")
    with ExitStack() as mem:
        sb = lambda n, s, d=F32: mem.enter_context(nc.sbuf_tensor(name + n, s, d))
        first_i, first = sb("_fi", [P, 1], I32), sb("_f", [P, 1])
        started, row = sb("_st", [P, 512]), sb("_row", [1, 2, 512])
        ps = mem.enter_context(nc.psum_tensor(name + "_ps", [P, 512], F32))
        ps2 = mem.enter_context(nc.psum_tensor(name + "_ps2", [P, 512], F32))
        with nc.Block() as block:
            @block.tensor
            def _(pe):
                nc.tensor.matmul(ps[0:NBX, 0:1], count[:, 0:NBX], v.ones[:, 0:1], start=True,
                                 stop=True).then_inc(s_pe, 1)
                pe.wait_ge(s_dve, 5)
                nc.tensor.matmul(ps2[0:1, :], v.ones[0:NBX, 0:1], started[0:NBX, :], start=True,
                                 stop=True).then_inc(s_pe, 1)

            @block.vector
            def _(dve):
                link = chain(dve, s_dve)
                dve.wait_ge(s_pe, 1)
                size = float(G * P)
                link(nc.vector.tensor_scalar(first_i[0:NBX, :], ps[0:NBX, 0:1], 1.0 / size,
                                             -0.5 + 0.25 / size, ALU.mult, ALU.add))
                link(nc.vector.tensor_copy(first[0:NBX, :], first_i[0:NBX, :]))
                link(nc.vector.tensor_scalar(first[0:NBX, :], first[0:NBX, :], float(groups - 1), None, ALU.min))
                link(nc.vector.tensor_tensor(first[0:NBX, :], first[0:NBX, :], v.part[0:NBX, :], ALU.add))
                link(nc.vector.tensor_scalar(started[0:NBX, :], v.stepn[0:NBX, :], first[0:NBX, 0:1], None,
                                             ALU.is_ge))
                dve.wait_ge(s_pe, 2)
                link(nc.vector.tensor_scalar(row[:, 1, :], ps2[0:1, :], -1.0, None, ALU.add))
                link(nc.vector.tensor_tensor(row[:, 0, :], v.stepn[0:1, :], row[:, 1, :], ALU.subtract))
                link(nc.vector.tensor_copy(flat(steps[:, :, :]), flat(row[:, :, :])))


def step_of(nc, eng, steps, k, groups):
    b = eng.value_load(steps[0:1, 1, ds(k, 1)], min_val=0, max_val=NBX - 1)
    g = nc.s_assert_within(k - b, 0, groups - 1,
                           skip_runtime_bounds_check_because="stage_steps makes group + block = step")
    return g, b


class Blocks:

    def __init__(self, nc, eng, steps, groups, lag, ring):
        self.nc, self.eng, self.steps, self.groups, self.lag, self.ring = nc, eng, steps, groups, lag, ring
        self.held = {}

    def load(self, k, u):
        g, b = step_of(self.nc, self.eng, self.steps, k, self.groups)
        self.held[u] = b
        return g, b

    def again(self, k, u):
        if isinstance(k, int) or u + self.lag >= self.ring:
            return step_of(self.nc, self.eng, self.steps, k, self.groups)
        b = self.held[u]
        return self.nc.s_assert_within(k - b, 0, self.groups - 1,
                                       skip_runtime_bounds_check_because="stage_steps makes group + block = step"), b


def stage_expand(nc, v, name, keys, steps, n_steps, groups, width, per_edge, scatter=None, gather=None):
    s_zero, s_oh, s_t, s_oht = v.sem(name + "_z"), v.sem(name + "_oh"), v.sem(name + "_t"), v.sem(name + "_oht")
    s_got, s_add = v.sem(name + "_got"), v.sem(name + "_add")
    R = 8
    with ExitStack() as mem:
        sb = lambda n, s, d=F32: mem.enter_context(nc.sbuf_tensor(name + n, s, d))
        oh = sb("_oh", [P, R, G, P])
        oht = sb("_oht", [P, R, G * P])
        pst = [mem.enter_context(nc.psum_tensor(f"{name}_pt{u}", [P, 512], F32)) for u in range(4)]
        psx = [mem.enter_context(nc.psum_tensor(f"{name}_px{u}", [P, 512], F32)) for u in range(4)]
        if scatter:
            scatter.buffers(mem)
        if gather:
            gather.buffers(mem)
        with nc.Block() as block:
            if scatter:
                @block.gpsimd
                def _(pool):
                    scatter.pool(pool)

                @block.sync
                def _(sp):
                    scatter.sync(sp)

            if gather:
                @block.gpsimd
                def _(pool):
                    gather.pool(pool)

                @block.sync
                def _(sp):
                    gather.sync(sp)

            @block.vector
            def _(dve):
                if not scatter:
                    nc.vector.memset(per_edge[:, :, :], 0.0).then_inc(s_zero, 1)

                blocks = Blocks(nc, dve, steps, groups, 4, R)

                def onehot(k, u, use):
                    g, b = blocks.load(k, u)
                    if later(k, R):
                        dve.wait_ge(s_t, k - R + 1)
                    nc.vector.scalar_tensor_tensor(
                        oh[:, u, :, :], v.iota[:, None, :].broadcast_to([P, G, P]), v.blk[:, ds(b, 1)],
                        keys[:, ds(g * G, G), None].broadcast_to([P, G, P]), ALU.add,
                        ALU.is_equal).then_inc(s_oh, 1)

                def add(k, u, use):
                    g, _ = blocks.again(k, u)
                    dve.wait_ge(s_got, k + 1)
                    if later(k, 1):
                        dve.wait_ge(s_add, k)
                    elif not scatter:
                        dve.wait_ge(s_zero, 1)
                    here = per_edge[:, ds(g * G, G), 0:width]
                    nc.vector.tensor_tensor(here, here, psx[u % 4][:, 0:G * X8].rearrange(
                        "p (g c) -> p g c", g=G)[:, :, 0:width], ALU.add).then_inc(s_add, 1)

                side = [(gather.scores(dve), 1, GS)] if gather else []
                pipeline(dve, n_steps, (onehot, 0), (add, 4), *side, ring=R)

            @block.tensor
            def _(pe):
                def turn(k, u, use):
                    pe.wait_ge(s_oh, k + 1)
                    if later(k, 4):
                        pe.wait_ge(s_oht, k - 3)
                    for j in range(G):
                        last = nc.tensor.transpose(pst[u % 4][:, j * P:(j + 1) * P], oh[:, u, j, :], v.ident[:, :])
                    last.then_inc(s_t, 1)

                def look(k, u, use):
                    b = pe.value_load(steps[0:1, 1, ds(k, 1)], min_val=0, max_val=NBX - 1)
                    pe.wait_ge(s_oht, k + 1)
                    if later(k, 4):
                        pe.wait_ge(s_add, k - 3)
                    for j in range(G):
                        last = nc.tensor.matmul(psx[u % 4][:, j * X8:(j + 1) * X8], oht[:, u, j * P:(j + 1) * P],
                                                flat(v.scores[:, ds(b, 1), :]), start=True, stop=True)
                    last.then_inc(s_got, 1)

                pipeline(pe, n_steps, (turn, 0), (look, 2), ring=R)

            @block.scalar
            def _(act):
                nc.scalar.preload_act_table(ACT.Copy)

                def copy(k, u, use):
                    act.wait_ge(s_t, k + 1)
                    if later(k, R):
                        act.wait_ge(s_got, k - R + 1)
                    nc.scalar.activation(oht[:, u, :], pst[u % 4][:, :], ACT.Copy).then_inc(s_oht, 1)

                side = [(gather.index(act), 0, GS)] if gather else []
                pipeline(act, n_steps, *side, (copy, 0), ring=R)


def stage_histogram(nc, v, hist):
    s_split, s_oh, s_mm, s_end = v.sem("h_split"), v.sem("h_oh"), v.sem("h_mm"), v.sem("h_end")
    R = 4
    with ExitStack() as mem:
        sb = lambda n, s, d=F32: mem.enter_context(nc.sbuf_tensor("h" + n, s, d))
        lo_i = sb("_lo_i", [P, TR], I32)
        ohlo = sb("_ohlo", [P, R, G, P], BF16)
        ohhi = sb("_ohhi", [P, R, G, NBX], BF16)
        ps = mem.enter_context(nc.psum_tensor("h_ps", [P, 512], F32))
        with nc.Block() as block:
            @block.vector
            def _(dve):
                link = chain(dve, s_split)
                link(nc.vector.tensor_scalar(lo_i[:, :], v.srci[:, :], P - 1, None, ALU.bitwise_and))
                link(nc.vector.tensor_copy(v.lo[:, :], lo_i[:, :]))
                link(nc.vector.tensor_tensor(v.hi[:, :], v.srck[:, :], v.lo[:, :], ALU.subtract))
                link(nc.vector.tensor_scalar(v.hi[:, :], v.hi[:, :], 1.0 / P, None, ALU.mult))

                def onehots(g, u, use):
                    if later(g, R):
                        dve.wait_ge(s_mm, g - R + 1)
                    nc.vector.tensor_tensor(ohlo[:, u, :, :], v.iota[:, None, :].broadcast_to([P, G, P]),
                                            v.lo[:, ds(g * G, G), None].broadcast_to([P, G, P]),
                                            ALU.is_equal).then_inc(s_oh, 1)
                    nc.vector.tensor_tensor(ohhi[:, u, :, :], v.iota[:, None, 0:NBX].broadcast_to([P, G, NBX]),
                                            v.hi[:, ds(g * G, G), None].broadcast_to([P, G, NBX]),
                                            ALU.is_equal).then_inc(s_oh, 1)

                pipeline(dve, GE, (onehots, 0), ring=R)
                dve.wait_ge(s_end, 1)
                nc.vector.tensor_copy(hist[:, :], ps[:, 0:NBX]).then_inc(s_end, 1)

            @block.tensor
            def _(pe):
                nc.tensor.matmul(ps[:, 0:NBX], v.zeros[:, :], v.zeros[:, 0:NBX], start=True, stop=False)

                def count(g, u, use):
                    pe.wait_ge(s_oh, g * 2 + 2)
                    for j in range(G):
                        last = nc.tensor.matmul(ps[:, 0:NBX], ohlo[:, u, j, :], ohhi[:, u, j, :],
                                                start=False, stop=False)
                    last.then_inc(s_mm, 1)

                pipeline(pe, GE, (count, 0), ring=R)
                nc.tensor.matmul(ps[:, 0:NBX], v.zeros[:, :], v.zeros[:, 0:NBX], start=False,
                                 stop=True).then_inc(s_end, 1)


def stage_bases(nc, v, hist, run, below):
    s, s_pe = v.sem("b_dve"), v.sem("b_pe")
    with ExitStack() as mem:
        sb = lambda n, s, d=F32: mem.enter_context(nc.sbuf_tensor("b" + n, s, d))
        h1, tot, incl, zr = sb("_h1", [P, NBX]), sb("_tot", [P, NBX]), sb("_incl", [P, NBX]), sb("_z", [P, NBX])
        ps = mem.enter_context(nc.psum_tensor("b_ps", [P, 512], F32))
        with nc.Block() as block:
            @block.vector
            def _(dve):
                link = chain(dve, s)
                link(nc.vector.memset(zr[:, :], 0.0))
                link(nc.vector.tensor_scalar(h1[:, :], hist[:, :], 1.0, None, ALU.add))
                dve.wait_ge(s_pe, 1)
                link(nc.vector.tensor_copy(tot[:, :], ps[:, 64:64 + NBX]))
                link(nc.vector.tensor_tensor_scan(incl[:, :], zr[:, :], tot[:, :], 0.0, ALU.add, ALU.add))
                link(nc.vector.tensor_tensor(incl[:, :], incl[:, :], tot[:, :], ALU.subtract))
                link(nc.vector.tensor_tensor(run[:, :], ps[:, 0:NBX], incl[:, :], ALU.add))
                link(nc.vector.tensor_scalar(below[:, :], incl[:, :], 1.0 / P, None, ALU.mult))

            @block.tensor
            def _(pe):
                pe.wait_ge(s, 2)
                nc.tensor.matmul(ps[:, 0:NBX], v.before[:, :], h1[:, :], start=True, stop=True)
                nc.tensor.matmul(ps[:, 64:64 + NBX], v.ones[:, :], h1[:, :], start=True, stop=True).then_inc(s_pe, 1)


def stage_gate_and_rank(nc, v, e_score, gated, run, posf):
    sem = v.sem
    R = 4
    s_w, s_split, s_bias = sem("g_w"), sem("g_split"), sem("g_bias")
    s_gpe, s_gact, s_y, s_es, s_acc = (sem("g_" + n) for n in ("pe", "act", "y", "es", "acc"))
    s_idx, s_one = sem("g_idx"), sem("g_one")
    s_eT, s_ys = [sem(f"g_eT{u}") for u in range(R)], [sem(f"g_ys{u}") for u in range(R)]
    s_xg = [v.pool_dma_sem(f"g_xg{u}") for u in range(R)]
    s_oh, s_cnt, s_run, s_oht, s_ohtb = (sem("r_" + n) for n in ("oh", "cnt", "run", "oht", "ohtb"))
    s_q, s_qm, s_look, s_mul, s_pos = (sem("r_" + n) for n in ("q", "qm", "look", "mul", "pos"))
    with ExitStack() as mem:
        sb = lambda n, s, d=F32: mem.enter_context(nc.sbuf_tensor("gr" + n, s, d))
        pb = lambda n, s, d=F32: mem.enter_context(nc.psum_tensor("gr" + n, s, d))
        H = G // 2
        wg, b1, b3 = sb("_wg", [P, W]), sb("_b1", [1, 4, H * W]), sb("_b3", [1, 3, H * W], BF16)
        bias, ones = sb("_bias", [3, H * W], BF16), sb("_ones", [3, P], BF16)
        ident = sb("_ident", [P, P], BF16)
        eT, idx, xg = sb("_eT", [P, R, G * P]), sb("_idx", [P, R, G], I32), sb("_xg", [P, R, G, W])
        gate, y, es = sb("_gate", [P, R, G, C]), sb("_y", [P, R, G, C]), sb("_es", [P, R, G, X8])
        ohlo, ohhi = sb("_ohlo", [P, R, G, P], BF16), sb("_ohhi", [P, R, G, NBX], BF16)
        oht, ohtb, qm = sb("_oht", [P, R, G * P]), sb("_ohtb", [P, R, G * P], BF16), sb("_qm", [P, R, G, P], BF16)
        cnt, mul = sb("_cnt", [P, R, G + 1, NBX]), sb("_mul", [P, 2, G, NBX])
        psg = [pb(f"_psg{u}", [P, 2, 512]) for u in range(2)]
        pst, psu, psq, psl = pb("_pst", [P, 512], BF16), pb("_psu", [P, 512]), pb("_psq", [P, 512]), pb("_psl", [P, 512])
        y_out = gated.rearrange("(t p) c -> p t c", p=P)
        tiles = lambda ps: ps.rearrange("p (t c) -> p t c", t=G)
        halves = lambda a: a.rearrange("p (b t) c -> p b t c", b=2)

        with nc.Block() as block:
            @block.sync
            def _(sp):
                sp.dma_start(wg[:, 0:C], v.eg_wt).then_inc(s_w, 16)
                sp.dma_start(wg[:, C:W], v.eb_wt).then_inc(s_w, 16)
                for h in range(H):
                    sp.dma_start(b1[:, 0, h * W:h * W + C], v.eg_b).then_inc(s_w, 16)
                    sp.dma_start(b1[:, 0, h * W + C:(h + 1) * W], v.eb_b).then_inc(s_w, 16)
                sp.wait_ge(s_split, 5)
                for n in range(3):
                    sp.dma_start(bias[n:n + 1, :], b3[:, n, :]).then_inc(s_bias, 16)

                def load(g, u, use):
                    if later(g, R):
                        sp.wait_ge(s_gpe, g - R + 1)
                    n = E - g * G * P if isinstance(g, int) and g == GE - 1 else G * P
                    sp.dma_start(eT[:, u, 0:n], v.attr_t[:, ds(g * (G * P), n)]).then_inc(s_eT[u], 16)

                def store(g, u, use):
                    sp.wait_ge(s_y, g + 1)
                    sp.dma_start(y_out[:, ds(g * G, G), :], y[:, u, :, :]).then_inc(s_ys[u], 16)

                pipeline(sp, GE, (load, 0), (store, 3), ring=R)
                for u in range(R):
                    sp.wait_ge(s_ys[u], 16 * ((GE - u + R - 1) // R))

            @block.gpsimd
            def _(pool):
                pool.sem_inc(s_one, 1)

                def gather(g, u, use):
                    if later(g, R):
                        pool.wait_ge(s_y, g - R + 1)
                        pool.wait_ge(s_es, g - R + 1)
                    pool.wait_ge(s_idx, g + 1)
                    for j in range(G):
                        nc.gpsimd.indirect_dma_start(
                            out=xg[:, u, j, :], out_offset=None, in_=v.table[:, :],
                            in_offset=bass.IndirectOffsetOnAxis(ap=idx[:, u, j:j + 1], axis=0)
                        ).wait_op(s_one, 1, "sem-ge").then_inc(s_xg[u], 16)

                pipeline(pool, GE, (gather, 0), ring=R)

            @block.tensor
            def _(pe):
                pe.wait_ge(s_w, 16 * (2 + 2 * H))
                pe.wait_ge(s_bias, 48)
                pe.wait_ge(s_split, 7)

                def gates(g, u, use):
                    pe.wait_ge(s_eT[u], use * 16 + 16)
                    if later(g):
                        pe.wait_ge(s_gact, g - 1)
                        pe.wait_ge(s_es, g - 1)
                    for h in range(2):
                        nc.tensor.matmul(psg[u % 2][:, h, 0:H * W], ones[:, :], bias[:, :], start=True, stop=False)
                        for j in range(H):
                            last = nc.tensor.matmul(psg[u % 2][:, h, j * W:(j + 1) * W],
                                                    eT[:, u, (h * H + j) * P:(h * H + j + 1) * P], wg[:, :],
                                                    start=False, stop=(j == H - 1))
                    last.then_inc(s_gpe, 1)

                def counts(g, u, use):
                    pe.wait_ge(s_oh, g * 2 + 2)
                    if later(g, 1):
                        pe.wait_ge(s_run, g + 1)
                        pe.wait_ge(s_oht, g)
                        pe.wait_ge(s_ohtb, g)
                    for j in range(G):
                        nc.tensor.transpose(pst[:, j * P:(j + 1) * P], ohlo[:, u, j, :], ident[:, :])
                    for j in range(G):
                        for h in range(j + 1):
                            last = nc.tensor.matmul(psu[:, j * NBX:(j + 1) * NBX], ohlo[:, u, h, :],
                                                    ohhi[:, u, h, :], start=(h == 0), stop=(h == j))
                    last.then_inc(s_cnt, 1)

                def same(g, u, use):
                    pe.wait_ge(s_ohtb, g + 1)
                    if later(g, 1):
                        pe.wait_ge(s_qm, g)
                    for j in range(G):
                        one = ohtb[:, u, j * P:(j + 1) * P]
                        last = nc.tensor.matmul(psq[:, j * P:(j + 1) * P], one, one, start=True, stop=True)
                    last.then_inc(s_q, 1)

                def lookups(g, u, use):
                    pe.wait_ge(s_qm, g + 1)
                    pe.wait_ge(s_oht, g + 1)
                    pe.wait_ge(s_run, g + 2)
                    if later(g, 1):
                        pe.wait_ge(s_mul, g)
                    for j in range(G):
                        to = psl[:, j * NBX:(j + 1) * NBX]
                        before = cnt[:, u, j, :] if j else cnt[:, (u - 1) % R, G, :]
                        nc.tensor.matmul(to, oht[:, u, j * P:(j + 1) * P], before, start=True, stop=False)
                        last = nc.tensor.matmul(to, qm[:, u, j, :], ohhi[:, u, j, :], start=False, stop=True)
                    last.then_inc(s_look, 1)

                pipeline(pe, GE, (gates, 0), (lookups, 3), (same, 1), (counts, 0), ring=R)

            @block.scalar
            def _(act):
                nc.scalar.preload_act_table(ACT.Sigmoid)

                def index(g, u, use):
                    if later(g, R):
                        act.wait_ge(s_xg[u], use * (16 * G))
                    act.wait_ge(s_one, 1)
                    nc.scalar.activation(idx[:, u, :], v.srci[:, ds(g * G, G)], ACT.Copy).then_inc(s_idx, 1)

                def sigmoid(g, u, use):
                    if later(g, R):
                        act.wait_ge(s_y, g - R + 1)
                    act.wait_ge(s_gpe, g + 1)
                    nc.scalar.activation(
                        halves(gate[:, u, :, :]),
                        psg[u % 2][:, :, 0:H * W].rearrange("p b (t c) -> p b t c", t=H)[:, :, :, 0:C],
                        ACT.Sigmoid).then_inc(s_gact, 1)

                def turned(g, u, use):
                    if later(g, R):
                        act.wait_ge(s_look, g - R + 1)
                        act.wait_ge(s_q, g - R + 1)
                    act.wait_ge(s_cnt, g + 1)
                    nc.scalar.activation(ohtb[:, u, :], pst[:, :], ACT.Copy).then_inc(s_ohtb, 1)
                    nc.scalar.activation(oht[:, u, :], pst[:, :], ACT.Copy).then_inc(s_oht, 1)

                pipeline(act, GE, (index, 0), (sigmoid, 2), (turned, 2), ring=R)

            @block.vector
            def _(dve):
                nc.vector.tensor_copy(cnt[:, R - 1, G, :], run[:, :]).then_inc(s_run, 1)
                dve.wait_ge(s_w, 16 * (2 + 2 * H))
                link = chain(dve, s_split)
                link(nc.vector.tensor_copy(b3[:, 0, :], b1[:, 0, :]))
                link(nc.vector.tensor_tensor(b1[:, 1, :], b1[:, 0, :], b3[:, 0, :], ALU.subtract))
                link(nc.vector.tensor_copy(b3[:, 1, :], b1[:, 1, :]))
                link(nc.vector.tensor_tensor(b1[:, 2, :], b1[:, 1, :], b3[:, 1, :], ALU.subtract))
                link(nc.vector.tensor_copy(b3[:, 2, :], b1[:, 2, :]))
                link(nc.vector.memset(ones[:, :], 1.0))
                link(nc.vector.tensor_copy(ident[:, :], v.ident[:, :]))

                def onehots(g, u, use):
                    if later(g, R):
                        dve.wait_ge(s_look, g - R + 1)
                        dve.wait_ge(s_mul, g - R + 1)
                    nc.vector.tensor_tensor(ohlo[:, u, :, :], v.iota[:, None, :].broadcast_to([P, G, P]),
                                            v.lo[:, ds(g * G, G), None].broadcast_to([P, G, P]),
                                            ALU.is_equal).then_inc(s_oh, 1)
                    nc.vector.tensor_tensor(ohhi[:, u, :, :], v.iota[:, None, 0:NBX].broadcast_to([P, G, NBX]),
                                            v.hi[:, ds(g * G, G), None].broadcast_to([P, G, NBX]),
                                            ALU.is_equal).then_inc(s_oh, 1)

                def running(g, u, use):
                    dve.wait_ge(s_run, g + 1)
                    if later(g, R):
                        dve.wait_ge(s_look, g - R + 2)
                    dve.wait_ge(s_cnt, g + 1)
                    nc.vector.tensor_tensor(cnt[:, u, 1:G + 1, :], tiles(psu[:, 0:G * NBX]),
                                            cnt[:, (u - 1) % R, G:G + 1, :].broadcast_to([P, G, NBX]),
                                            ALU.add).then_inc(s_run, 1)

                def earlier(g, u, use):
                    if later(g, R):
                        dve.wait_ge(s_look, g - R + 1)
                    dve.wait_ge(s_q, g + 1)
                    nc.vector.tensor_tensor(qm[:, u, :, :], tiles(psq[:, :]),
                                            v.before[:, None, :].broadcast_to([P, G, P]), ALU.mult).then_inc(s_qm, 1)

                def choose(g, u, use):
                    if later(g, 2):
                        dve.wait_ge(s_pos, g - 1)
                    dve.wait_ge(s_look, g + 1)
                    nc.vector.tensor_tensor(mul[:, u % 2, :, :], tiles(psl[:, 0:G * NBX]), ohhi[:, u, :, :],
                                            ALU.mult).then_inc(s_mul, 1)

                def position(g, u, use):
                    dve.wait_ge(s_mul, g + 1)
                    nc.vector.tensor_reduce(posf[:, ds(g * G, G)], mul[:, u % 2, :, :], AX.X, ALU.add).then_inc(s_pos, 1)

                def gated_rows(g, u, use):
                    if later(g, R):
                        dve.wait_ge(s_ys[u], use * 16)
                        dve.wait_ge(s_acc, g - R + 1)
                    dve.wait_ge(s_gact, g + 1)
                    dve.wait_ge(s_xg[u], use * (16 * G) + 16 * G)
                    nc.vector.tensor_tensor(y[:, u, :, :], gate[:, u, :, :], xg[:, u, :, 0:C],
                                            ALU.mult).then_inc(s_y, 1)
                    nc.vector.tensor_tensor(
                        halves(es[:, u, :, :]),
                        psg[u % 2][:, :, 0:H * W].rearrange("p b (t c) -> p b t c", t=H)[:, :, :, C:W],
                        halves(xg[:, u, :, C:W]), ALU.add).then_inc(s_es, 1)

                def scores(g, u, use):
                    dve.wait_ge(s_es, g + 1)
                    here = e_score[:, ds(g * G, G), :]
                    nc.vector.tensor_tensor(here, here, es[:, u, :, :], ALU.add).then_inc(s_acc, 1)

                pipeline(dve, GE, (choose, 4), (onehots, 0), (running, 1), (gated_rows, 1), (earlier, 2),
                         (scores, 2), (position, 4), ring=R)
                dve.wait_ge(s_run, GE + 1)
                nc.vector.tensor_copy(run[:, :], cnt[:, (GE - 1) % R, G, :])


class Scatter:
    R = 4

    def __init__(self, nc, v, posi, runi, posf, run, rows_out, ranges):
        self.ranges, self.done = ranges, [0] * self.R
        self.nc, self.v, self.rows_out, self.part = nc, v, rows_out, 0
        self.posi, self.runi = posi, runi
        self.s_sc = [v.pool_dma_sem(f"s_sc{u}") for u in range(self.R)]
        self.s_loop = v.pool_dma_sem("s_loop")
        s_pos = v.sem("s_pos")
        with nc.Block() as block:
            @block.vector
            def _(dve):
                for (first, count), to in zip(ranges, posi):
                    nc.vector.tensor_copy(to[:, :], posf[:, first * G:(first + count) * G]).then_inc(s_pos, 1)
                nc.vector.tensor_copy(self.runi[:, :], run[:, :]).then_inc(s_pos, 1)

    def buffers(self, mem):
        nc, v = self.nc, self.v
        if self.part:
            self.done = [self.total(u) for u in range(self.R)]
        self.first, self.count = self.ranges[self.part]
        loops = self.part == 0
        self.name = f"sc{self.part}"
        self.part += 1
        sb = lambda n, s, d=F32: mem.enter_context(nc.sbuf_tensor(self.name + n, s, d))
        self.er, self.idx = sb("_er", [P, self.R, G, RW]), sb("_idx", [P, self.R, G], I32)
        self.loops = sb("_loops", [P, NB + 1, RW]) if loops else None
        self.s_ld = [v.sem(f"{self.name}_ld{u}") for u in range(self.R)]
        self.s_idx, self.s_one, self.s_set = (v.sem(f"{self.name}_{n}") for n in ("idx", "one", "set"))
        self.s_lp, self.s_pad = v.sem(self.name + "_lp"), v.sem(self.name + "_pad")

    def sync(self, sp):
        nc, v, R, er = self.nc, self.v, self.R, self.er
        attr = v.attr[0:(TE - 1) * P, :].rearrange("(t p) c -> p t c", p=P)
        pads = self.rows_out.rearrange("(t p) c -> p t c", p=P)
        sp.wait_ge(self.s_set, 1)
        if self.loops is not None:
            sp.wait_ge(self.s_lp, 4)
            for t in range(LP, TS):
                sp.dma_start(pads[:, t:t + 1, :], self.loops[:, NB:NB + 1, :]).then_inc(self.s_pad, 16)

        def load(n, u, use):
            g = n + self.first
            if later(n, R):
                sp.wait_ge(self.s_sc[u], self.done[u] + use * (16 * G))
            if isinstance(g, int) and g == GE - 1:
                sp.dma_start(er[:, u, 0:G - 1, 0:C], attr[:, ds(g * G, G - 1), :]).then_inc(self.s_ld[u], 16)
                sp.dma_start(er[0:ETAIL, u, G - 1, 0:C], v.attr[(TE - 1) * P:E, :]).then_inc(self.s_ld[u], 16)
            else:
                sp.dma_start(er[:, u, :, 0:C], attr[:, ds(g * G, G), :]).then_inc(self.s_ld[u], 16)

        pipeline(sp, self.count, (load, 0), ring=R)
        if self.loops is not None:
            sp.wait_ge(self.s_pad, 16 * (TS - LP))

    def pool(self, pool):
        nc, v, R, er, idx = self.nc, self.v, self.R, self.er, self.idx
        posi = self.posi[self.part - 1]
        pool.sem_inc(self.s_one, 1)
        nc.gpsimd.memset(er[:, :, :, :], 1.0).then_inc(self.s_set, 1)
        if self.loops is not None:
            loops, s_lp = self.loops, self.s_lp
            nc.gpsimd.memset(loops[:, :, :], 0.0).then_inc(s_lp, 1)
            pool.wait_ge(s_lp, 1)
            for c in (C + 1, C + 2):
                nc.gpsimd.tensor_scalar(loops[:, 0:NB, c], v.blk[:, 0:NB], v.part[:, 0:1], None,
                                        ALU.add).then_inc(s_lp, 1)
            nc.gpsimd.memset(loops[:, NB, C + 1:C + 3], float(PADKEY)).then_inc(s_lp, 1)
            pool.wait_ge(s_lp, 4)
            for b in range(NB):
                nc.gpsimd.indirect_dma_start(
                    out=self.rows_out[:, :], out_offset=bass.IndirectOffsetOnAxis(ap=self.runi[:, b:b + 1], axis=0),
                    in_=loops[:, b, :], in_offset=None).then_inc(self.s_loop, 16)
        pool.wait_ge(self.s_set, 1)

        def scatter(n, u, use):
            g = n + self.first
            if later(n, R):
                pool.wait_ge(self.s_sc[u], self.done[u] + use * (16 * G))
            nc.gpsimd.tensor_copy(idx[:, u, :], posi[:, ds(n * G, G)]).then_inc(self.s_idx, 1)
            nc.gpsimd.tensor_copy(er[:, u, :, C + 1:C + 3],
                                  v.keys2[:, :, ds(g * G, G)].rearrange("p k t -> p t k")).then_inc(self.s_idx, 1)
            pool.wait_ge(self.s_ld[u], (use * 16 + 16) + (16 if isinstance(g, int) and g == GE - 1 else 0))
            pool.wait_ge(self.s_idx, n * 2 + 2)
            for j in range(G):
                nc.gpsimd.indirect_dma_start(
                    out=self.rows_out[:, :], out_offset=bass.IndirectOffsetOnAxis(ap=idx[:, u, j:j + 1], axis=0),
                    in_=er[:, u, j, :], in_offset=None
                ).wait_op(self.s_one, 1, "sem-ge").then_inc(self.s_sc[u], 16)

        pipeline(pool, self.count, (scatter, 0), ring=R)
        for u in range(R):
            pool.wait_ge(self.s_sc[u], self.total(u))
        if self.loops is not None:
            pool.wait_ge(self.s_loop, 16 * NB)

    def total(self, u):
        return self.done[u] + 16 * G * ((self.count - u + self.R - 1) // self.R)


def stage_flags(nc, v, name, row_dram, fl):
    s_ld, s, s_pe, s_cp = v.sem(name + "_ld"), v.sem(name + "_dve"), v.sem(name + "_pe"), v.sem(name + "_cp")
    n = TR * P
    H = fl.heads
    with ExitStack() as mem:
        sb = lambda m, sh, d=I32: mem.enter_context(nc.sbuf_tensor(name + m, sh, d))
        cur, prev, nxt = sb("_c", [P, KR, P]), sb("_p", [P, KR, P]), sb("_n", [P, KR, P])
        a4 = sb("_a4", [P, 2, KR, H], F32)
        ps = [mem.enter_context(nc.psum_tensor(f"{name}_ps{d}", [P, 4, 512], F32)) for d in range(2)]
        view = lambda off: row_dram[:, off:off + n].rearrange("a (k r p) -> r (a k) p", r=P, p=P)
        with nc.Block() as block:
            @block.sync
            def _(sp):
                sp.dma_start(cur[:, :, :], view(1)).then_inc(s_ld, 16)
                sp.dma_start(prev[:, :, :], view(0)).then_inc(s_ld, 16)
                sp.dma_start(nxt[:, :, :], view(2)).then_inc(s_ld, 16)

            @block.vector
            def _(dve):
                link = chain(dve, s)
                dve.wait_ge(s_ld, 48)
                for d, (other, r, g) in enumerate(((prev, fl.rf, fl.gf), (nxt, fl.rb, fl.gb))):
                    way = slice(None, None, -1) if d else slice(None)
                    edge = P - 1 if d else 0
                    link(nc.vector.tensor_tensor(r[:, :, :], cur[:, :, :], other[:, :, :], ALU.not_equal))
                    link(nc.vector.tensor_scalar(r[:, :, :], r[:, :, :], -BIG, None, ALU.mult))
                    for k in range(KR):
                        last = nc.vector.tensor_tensor_scan(g[:, k, way], v.zeros[:, :], r[:, k, way], 0.0,
                                                            ALU.add, ALU.min)
                    link(last)
                    link(nc.vector.memset(r[:, :, edge:edge + 1], -BIG))
                    link(nc.vector.tensor_copy(a4[:, d, :, :], g[:, :, P - 1 - edge:P - edge].broadcast_to([P, KR, H])))
                dve.wait_ge(s_pe, 1)
                for d, a in enumerate((fl.af, fl.ab)):
                    nc.vector.tensor_copy(a[:, :], ps[d][0:H, :, :].rearrange("p a c -> p (a c)")[:, 0:TR]).then_inc(s_cp, 1)

            @block.tensor
            def _(pe):
                pe.wait_ge(s, 10)
                for d in range(2):
                    for k in range(KR):
                        last = nc.tensor.transpose(ps[d][0:H, k // 4, (k % 4) * P:(k % 4 + 1) * P], a4[:, d, k, :],
                                                   v.ident[:, :])
                last.then_inc(s_pe, 1)


def stage_turn(nc, v, name, heads, source, target):
    s_t, s_c = v.sem(name + "_t"), v.sem(name + "_c")
    with ExitStack() as mem:
        ps = [mem.enter_context(nc.psum_tensor(f"{name}_ps{u}", [P, 512], F32)) for u in range(4)]
        jobs = [(h, k) for h in range(heads) for k in range(KR)]
        with nc.Block() as block:
            @block.tensor
            def _(pe):
                for n, (h, k) in enumerate(jobs):
                    if n >= 4:
                        pe.wait_ge(s_c, n - 3)
                    nc.tensor.transpose(ps[n % 4][:, 0:P], source(h, k), v.ident[:, :]).then_inc(s_t, 1)

            @block.scalar
            def _(act):
                for n, (h, k) in enumerate(jobs):
                    act.wait_ge(s_t, n + 1)
                    nc.scalar.activation(target(h, k), ps[n % 4][:, 0:P], ACT.Copy).then_inc(s_c, 1)


class Segments:
    DVE = 9

    def __init__(self, nc, v, mem, name, fl):
        self.nc, self.v, self.fl, self.heads = nc, v, fl, fl.heads
        H = fl.heads
        sb = lambda m, sh: mem.enter_context(nc.sbuf_tensor(name + m, sh, F32))
        self.V = sb("_V", [P, H, 1 + TR])
        self.before, self.behind = sb("_bef", [P, H, TR]), sb("_beh", [P, H, TR])
        self.ends = sb("_ends", [P, 2, KR, H])
        self.carry = [sb("_cf", [H, 1 + TR]), sb("_cb", [H, 1 + TR])]
        self.inn = sb("_in", [P, 2, KR, H])
        self.s, self.s_pe = v.sem(name + "_seg"), v.sem(name + "_segpe")
        self.name = name

    def psum(self, mem):
        self.ps = [mem.enter_context(self.nc.psum_tensor(f"{self.name}_psc{d}", [P, 4, 512], F32)) for d in range(2)]

    def dve_setup(self, dve, sem):
        nc = self.nc
        nc.vector.memset(self.V[:, :, 0:1], -BIG).then_inc(sem, 1)
        nc.vector.memset(self.carry[0][:, 0:1], -BIG).then_inc(sem, 1)
        nc.vector.memset(self.carry[1][:, TR:TR + 1], -BIG).then_inc(sem, 1)

    def dve(self, dve, it):
        nc, fl, V = self.nc, self.fl, self.V
        at = lambda n: dve.wait_ge(self.s, it * self.DVE + n)
        rows = lambda ap: ap.rearrange("p (k c) -> p k c", c=P)
        rf, rb = (x[:, :, :].rearrange("p k c -> p (k c)") for x in (fl.rf, fl.rb))
        for h in range(self.heads):
            last = nc.vector.tensor_tensor_scan(self.before[:, h, :], V[:, h, 0:TR], rf, -BIG, ALU.max, ALU.add)
        last.then_inc(self.s, 1)
        for h in range(self.heads):
            last = nc.vector.tensor_tensor_scan(self.behind[:, h, ::-1], rb[:, ::-1], V[:, h, TR:0:-1], -BIG,
                                                ALU.add, ALU.max)
        last.then_inc(self.s, 1)
        at(2)
        for h in range(self.heads):
            nc.vector.tensor_tensor(self.ends[:, 0, :, h], rows(self.before[:, h, :])[:, :, P - 1],
                                    rows(V[:, h, 1:1 + TR])[:, :, P - 1], ALU.max)
            last = nc.vector.tensor_copy(self.ends[:, 1, :, h], rows(self.behind[:, h, :])[:, :, 0])
        last.then_inc(self.s, 1)
        dve.wait_ge(self.s_pe, it * 2 + 1)
        wide = lambda d: self.ps[d][0:self.heads, :, :].rearrange("p a c -> p (a c)")[:, 0:TR]
        nc.vector.tensor_tensor_scan(self.carry[0][:, 1:1 + TR], fl.af[:, :], wide(0), -BIG, ALU.add,
                                     ALU.max).then_inc(self.s, 1)
        nc.vector.tensor_tensor_scan(self.carry[1][:, 0:TR][:, ::-1], fl.ab[:, ::-1], wide(1)[:, ::-1], -BIG,
                                     ALU.add, ALU.max).then_inc(self.s, 1)
        dve.wait_ge(self.s_pe, it * 2 + 2)
        for d in range(2):
            nc.vector.tensor_copy(self.inn[:, d, :, :].rearrange("p k h -> p (k h)"),
                                  self.ps[d][:, 0, 0:KR * self.heads]).then_inc(self.s, 1)
        at(7)
        for d, (g, to) in enumerate(((fl.gf, self.before), (fl.gb, self.behind))):
            for h in range(self.heads):
                for k in range(KR):
                    here = rows(to[:, h, :])[:, k, :]
                    last = nc.vector.scalar_tensor_tensor(here, g[:, k, :], self.inn[:, d, k, h:h + 1], here,
                                                          ALU.add, ALU.max)
            last.then_inc(self.s, 1)
        at(9)

    def pe(self, pe, it):
        nc, v = self.nc, self.v
        pe.wait_ge(self.s, it * self.DVE + 3)
        for d in range(2):
            for k in range(KR):
                last = nc.tensor.transpose(self.ps[d][0:self.heads, k // 4, (k % 4) * P:(k % 4 + 1) * P],
                                           self.ends[:, d, k, :], v.ident[:, :])
        last.then_inc(self.s_pe, 1)
        pe.wait_ge(self.s, it * self.DVE + 5)
        H = self.heads
        for d in range(2):
            for k in range(KR):
                last = nc.tensor.transpose(self.ps[d][:, 0, k * H:(k + 1) * H],
                                           self.carry[d][:, d + k * P:d + (k + 1) * P], v.ident[0:H, 0:H])
                if not d and not k:
                    last.wait_op(v.s_in, 16, "sem-ge")
        last.then_inc(self.s_pe, 1)


def stage_softmax(nc, v, name, e, first_head, fl):
    H = fl.heads
    with ExitStack() as mem:
        seg = Segments(nc, v, mem, name, fl)
        stage_turn(nc, v, name + "r", H, lambda h, k: e[:, k * P:(k + 1) * P, first_head + h],
                   lambda h, k: seg.V[:, h, 1 + k * P:1 + (k + 1) * P])
        s0, s1, s2 = v.sem(name + "_0"), v.sem(name + "_1"), v.sem(name + "_2")
        with ExitStack() as banks, nc.Block() as block:
            seg.psum(banks)
            @block.vector
            def _(dve):
                seg.dve_setup(dve, s0)
                dve.wait_ge(s0, 3)
                seg.dve(dve, 0)
                nc.vector.tensor_tensor(seg.before[:, :, :], seg.before[:, :, :], seg.behind[:, :, :],
                                        ALU.max).then_inc(s1, 1)
                dve.wait_ge(s1, 1)
                nc.vector.tensor_tensor(seg.before[:, :, :], seg.V[:, :, 1:1 + TR], seg.before[:, :, :],
                                        ALU.subtract).then_inc(s1, 1)

            @block.tensor
            def _(pe):
                seg.pe(pe, 0)

            @block.scalar
            def _(act):
                act.wait_ge(s1, 2)
                nc.scalar.activation(seg.behind[:, :, :], seg.before[:, :, :], ACT.Exp).then_inc(s2, 1)
        stage_turn(nc, v, name + "t", H, lambda h, k: seg.behind[:, h, k * P:(k + 1) * P],
                   lambda h, k: e[:, k * P:(k + 1) * P, first_head + h])


def stage_top8(nc, v, name, e, first_head, fl, top):
    H = fl.heads
    with ExitStack() as mem:
        seg = Segments(nc, v, mem, name, fl)
        orig = mem.enter_context(nc.sbuf_tensor(name + "_orig", [P, H, TR], F32))
        stage_turn(nc, v, name + "r", H, lambda h, k: e[:, k * P:(k + 1) * P, first_head + h],
                   lambda h, k: seg.V[:, h, 1 + k * P:1 + (k + 1) * P])
        s0, s1, s2, s3, s_k = (v.sem(f"{name}_{n}") for n in range(5))
        V = seg.V[:, :, 1:1 + TR]

        def knock_out(dve, it):
            nc.vector.tensor_tensor(seg.behind[:, :, :], V, seg.behind[:, :, :], ALU.is_ge).then_inc(s_k, 1)
            nc.vector.tensor_tensor(seg.before[:, :, :], V, seg.before[:, :, :], ALU.is_gt).then_inc(s_k, 1)
            dve.wait_ge(s_k, it * 4 + 2)
            nc.vector.tensor_tensor(seg.before[:, :, :], seg.behind[:, :, :], seg.before[:, :, :],
                                    ALU.mult).then_inc(s_k, 1)
            dve.wait_ge(s_k, it * 4 + 3)
            nc.vector.scalar_tensor_tensor(V, seg.before[:, :, :], -2 * BIG, V, ALU.mult, ALU.add).then_inc(s_k, 1)
            dve.wait_ge(s_k, it * 4 + 4)

        with ExitStack() as banks, nc.Block() as block:
            seg.psum(banks)
            @block.vector
            def _(dve):
                seg.dve_setup(dve, s0)
                dve.wait_ge(s0, 3)
                seg.dve(dve, 0)
                nc.vector.tensor_tensor(orig[:, :, :], seg.before[:, :, :], seg.behind[:, :, :],
                                        ALU.max).then_inc(s1, 1)
                dve.wait_ge(s1, 1)
                nc.vector.tensor_tensor(orig[:, :, :], V, orig[:, :, :], ALU.subtract).then_inc(s1, 1)
                dve.wait_ge(s1, 2)
                knock_out(dve, 0)
                with dve.Fori(1, top) as it:
                    seg.dve(dve, it)
                    knock_out(dve, it)
                nc.vector.tensor_scalar(seg.behind[:, :, :], V, -1.5 * BIG, None, ALU.is_lt).then_inc(s1, 1)
                dve.wait_ge(s1, 3)
                dve.wait_ge(s2, 1)
                nc.vector.tensor_tensor(seg.before[:, :, :], orig[:, :, :], seg.behind[:, :, :],
                                        ALU.mult).then_inc(s1, 1)

            @block.tensor
            def _(pe):
                seg.pe(pe, 0)
                with pe.Fori(1, top) as it:
                    seg.pe(pe, it)

            @block.scalar
            def _(act):
                act.wait_ge(s1, 2)
                nc.scalar.activation(orig[:, :, :], orig[:, :, :], ACT.Exp).then_inc(s2, 1)
        stage_turn(nc, v, name + "t", H, lambda h, k: seg.before[:, h, k * P:(k + 1) * P],
                   lambda h, k: e[:, k * P:(k + 1) * P, first_head + h])


def stage_aggregate(nc, v, name, rows, keys, steps, n_steps, groups, weights, heads, acc, scatter=None):
    R = 8
    s_z, s_ld, s_oh = v.sem(name + "_z"), [v.sem(f"{name}_ld{u}") for u in range(R)], v.sem(name + "_oh")
    s_w, s_wc, s_mm, s_add = v.sem(name + "_w"), v.sem(name + "_wc"), v.sem(name + "_mm"), v.sem(name + "_add")
    width = C + heads
    with ExitStack() as mem:
        sb = lambda n, sh, d=F32: mem.enter_context(nc.sbuf_tensor(name + n, sh, d))
        buf = sb("_buf", [P, R, G, C])
        oh = sb("_oh", [P, R, G, P])
        wrow = sb("_wrow", [P, R, G, width])
        ps = [mem.enter_context(nc.psum_tensor(f"{name}_ps{u}", [P, 512], F32)) for u in range(4)]
        src = rows.rearrange("(t p) c -> p t c", p=P)
        if scatter:
            scatter.buffers(mem)
        with nc.Block() as block:
            def load(queue, k, u, g):
                if later(k, R):
                    queue.wait_ge(s_w, k - R + 1)
                queue.dma_start(buf[:, u, :, :], src[:, ds(g * G, G), 0:C]).then_inc(s_ld[u], 16)

            def weigh(engine, queue, k, u, use, g):
                queue.wait_ge(s_ld[u], use * 16 + 16)
                engine.tensor_tensor(
                    wrow[:, u, :, 0:C].rearrange("p t (h c) -> p t h c", h=heads),
                    buf[:, u, :, :].rearrange("p t (h c) -> p t h c", h=heads),
                    weights[:, ds(g * G, G), 0:heads][:, :, :, None].broadcast_to([P, G, heads, C // heads]),
                    ALU.mult).then_inc(s_w, 1)

            if not scatter:
                @block.sync
                def _(sp):
                    def loads(k, u, use):
                        g, _ = step_of(nc, sp, steps, k, groups)
                        load(sp, k, u, g)

                    pipeline(sp, n_steps, (loads, 0), ring=R)

                @block.gpsimd
                def _(pool):
                    def weighted(k, u, use):
                        g, _ = step_of(nc, pool, steps, k, groups)
                        if later(k, R):
                            pool.wait_ge(s_mm, k - R + 1)
                        weigh(nc.gpsimd, pool, k, u, use, g)

                    pipeline(pool, n_steps, (weighted, 0), ring=R)

            if scatter:
                @block.gpsimd
                def _(pool):
                    scatter.pool(pool)

                @block.sync
                def _(sp):
                    scatter.sync(sp)

            @block.vector
            def _(dve):
                nc.vector.memset(acc[:, :, 0:width], 0.0).then_inc(s_z, 1)

                blocks = Blocks(nc, dve, steps, groups, 3, R)

                def prepare(k, u, use):
                    g, b = blocks.load(k, u)
                    if later(k, R):
                        dve.wait_ge(s_mm, k - R + 1)
                    nc.vector.scalar_tensor_tensor(
                        oh[:, u, :, :], v.iota[:, None, :].broadcast_to([P, G, P]), v.blk[:, ds(b, 1)],
                        keys[:, ds(g * G, G), None].broadcast_to([P, G, P]), ALU.add,
                        ALU.is_equal).then_inc(s_oh, 1)
                    if scatter:
                        weigh(nc.vector, dve, k, u, use, g)

                def add(k, u, use):
                    _, b = blocks.again(k, u)
                    dve.wait_ge(s_mm, k + 1)
                    if later(k, 1):
                        dve.wait_ge(s_add, k)
                    else:
                        dve.wait_ge(s_z, 1)
                    here = flat(acc[:, ds(b, 1), 0:width])
                    nc.vector.tensor_tensor(here, here, ps[u % 4][:, 0:width], ALU.add).then_inc(s_add, 1)

                pipeline(dve, n_steps, (prepare, 0), (add, 3), ring=R)

            @block.scalar
            def _(act):
                nc.scalar.preload_act_table(ACT.Copy)

                def put(k, u, use):
                    g, _ = step_of(nc, act, steps, k, groups)
                    if scatter:
                        load(act, k, u, g)
                    if later(k, R):
                        act.wait_ge(s_mm, k - R + 1)
                        act.wait_ge(s_z, 1)
                    nc.scalar.activation(wrow[:, u, :, C:width], weights[:, ds(g * G, G), 0:heads],
                                         ACT.Copy).then_inc(s_wc, 1)

                pipeline(act, n_steps, (put, 0), ring=R)

            @block.tensor
            def _(pe):
                def sums(k, u, use):
                    pe.wait_ge(s_oh, k + 1)
                    pe.wait_ge(s_w, k + 1)
                    pe.wait_ge(s_wc, k + 1)
                    if later(k, 4):
                        pe.wait_ge(s_add, k - 3)
                    for j in range(G):
                        last = nc.tensor.matmul(ps[u % 4][:, 0:width], oh[:, u, j, :], wrow[:, u, j, 0:width],
                                                start=(j == 0), stop=(j == G - 1))
                    last.then_inc(s_mm, 1)

                pipeline(pe, n_steps, (sums, 0), ring=R)


def normalise(nc, link, act_sqrt, Z, T, m, r):
    wide = lambda a: a[:, :, None].broadcast_to([P, NBX, C])
    link(nc.vector.tensor_reduce(m[:, :], Z[:, :, :], AX.X, ALU.add))
    link(nc.vector.tensor_scalar(m[:, :], m[:, :], 1.0 / C, None, ALU.mult))
    link(nc.vector.tensor_tensor(Z[:, :, :], Z[:, :, :], wide(m), ALU.subtract))
    link(nc.vector.tensor_tensor(T, Z[:, :, :], Z[:, :, :], ALU.mult))
    link(nc.vector.tensor_reduce(r[:, :], T, AX.X, ALU.add))
    link(nc.vector.tensor_scalar(r[:, :], r[:, :], 1.0 / C, LN_EPS, ALU.mult, ALU.add))
    act_sqrt(r)
    link(nc.vector.reciprocal(r[:, :], r[:, :]))
    link(nc.vector.tensor_tensor(Z[:, :, :], Z[:, :, :], wide(r), ALU.mult))


def stage_update(nc, v, name, acc, heads, floor, inner):
    s, s_rt, s_sq, s_ex, s_gb = (v.sem(f"{name}_{n}") for n in ("dve", "rt", "sq", "ex", "gb"))
    with ExitStack() as mem:
        sb = lambda n, sh, d=F32: mem.enter_context(nc.sbuf_tensor(name + n, sh, d))
        Z, T = sb("_Z", [P, NBX, C]), sb("_T", [P, NBX, C])
        m, r, inv = sb("_m", [P, NBX]), sb("_r", [P, NBX]), sb("_inv", [P, NBX, X8])
        gb = sb("_gbt", [P, 2, C])
        roots = []
        with nc.Block() as block:
            if inner == "norm":
                @block.sync
                def _(sp):
                    sp.dma_start(gb[:, 0, :], v.ln_g.broadcast_to([P, C])).then_inc(s_gb, 16)
                    sp.dma_start(gb[:, 1, :], v.ln_b.broadcast_to([P, C])).then_inc(s_gb, 16)

            @block.vector
            def _(dve):
                link = chain(dve, s)

                def act_sqrt(x):
                    dve.sem_inc(s_rt, 1)
                    roots.append(x)
                    dve.wait_ge(s_sq, len(roots))

                if heads:
                    link(nc.vector.tensor_scalar(inv[:, :, 0:heads], acc[:, :, C:C + heads], floor, None, ALU.max))
                    link(nc.vector.reciprocal(inv[:, :, 0:heads], inv[:, :, 0:heads]))
                    for h in range(heads):
                        n = C // heads
                        last = nc.vector.tensor_tensor(Z[:, :, h * n:(h + 1) * n], acc[:, :, h * n:(h + 1) * n],
                                                       inv[:, :, h:h + 1].broadcast_to([P, NBX, n]), ALU.mult)
                    link(last)
                if inner == "norm":
                    link(nc.vector.tensor_tensor(Z[:, :, :], Z[:, :, :], v.X[:, :, :], ALU.add))
                    normalise(nc, link, act_sqrt, Z, T[:, :, :], m, r)
                    dve.wait_ge(s_gb, 32)
                    link(nc.vector.tensor_tensor(Z[:, :, :], Z[:, :, :], gb[:, 0:1, :].broadcast_to([P, NBX, C]),
                                                 ALU.mult))
                    link(nc.vector.tensor_tensor(Z[:, :, :], Z[:, :, :], gb[:, 1:2, :].broadcast_to([P, NBX, C]),
                                                 ALU.add))
                if inner == "elu":
                    link(nc.vector.tensor_scalar(T[:, :, :], Z[:, :, :], 0.0, None, ALU.min))
                    dve.sem_inc(s_ex, 1)
                    link(nc.vector.tensor_scalar(Z[:, :, :], Z[:, :, :], 0.0, -1.0, ALU.max, ALU.add))
                    dve.wait_ge(s_sq, 1)
                    link(nc.vector.tensor_tensor(Z[:, :, :], Z[:, :, :], T[:, :, :], ALU.add))
                    roots.append(None)
                link(nc.vector.tensor_tensor(v.X[:, :, :], Z[:, :, :] if heads else acc[:, :, 0:C], v.X[:, :, :],
                                             ALU.add))
                normalise(nc, link, act_sqrt, v.X, T[:, :, :], m, r)

            @block.scalar
            def _(act):
                if inner == "elu":
                    act.wait_ge(s_ex, 1)
                    nc.scalar.activation(T[:, :, :], T[:, :, :], ACT.Exp).then_inc(s_sq, 1)
                for n in range(1 + (inner == "norm")):
                    act.wait_ge(s_rt, n + 1)
                    nc.scalar.activation(r[:, :], r[:, :], ACT.Sqrt).then_inc(s_sq, 1)


def stage_clear(nc, v, name, x):
    s = v.sem(name)
    with nc.Block() as block:
        @block.vector
        def _(dve):
            nc.vector.memset(x[:, :, :], 0.0).then_inc(s, 1)


def stage_leaky(nc, v, name, e):
    s = v.sem(name)
    with nc.Block() as block:
        @block.vector
        def _(dve):
            nc.vector.scalar_tensor_tensor(e, e, 0.2, e, ALU.mult, ALU.max).then_inc(s, 1)


def stage_clipped_attention(nc, v, keys, steps, acc):
    R = 8
    sem = v.sem
    s_z, s_idx, s_oh, s_t, s_oht, s_got = (sem("ca_" + n) for n in ("z", "idx", "oh", "t", "oht", "got"))
    s_sum, s_leaky, s_clip, s_exp, s_w = (sem("ca_" + n) for n in ("sum", "leaky", "clip", "exp", "w"))
    s_mm, s_add, s_one = (sem("ca_" + n) for n in ("mm", "add", "one"))
    s_xg = [v.pool_dma_sem(f"ca_xg{u}") for u in range(R)]
    s_at = [sem(f"ca_at{u}") for u in range(R)]
    ROW = C + 1 + C
    groups = GS
    with ExitStack() as mem:
        sb = lambda n, sh, d=F32: mem.enter_context(nc.sbuf_tensor("ca" + n, sh, d))
        idx, xg = sb("_idx", [P, R, G], I32), sb("_xg", [P, R, G, W])
        oh, oht = sb("_oh", [P, R, G, P]), sb("_oht", [P, R, G * P])
        t = sb("_t", [P, R, 3, G])
        row = sb("_row", [P, R, G, ROW])
        pst, psx, ps = ([mem.enter_context(nc.psum_tensor(f"ca_{n}{u}", [P, 512], F32)) for u in range(2)]
                        for n in ("pt", "px", "ps"))
        src = v.sorted.rearrange("(t p) c -> p t c", p=P)
        with nc.Block() as block:
            @block.sync
            def _(sp):
                def load(k, u, use):
                    g, _ = step_of(nc, sp, steps, k, groups)
                    if later(k, R):
                        sp.wait_ge(s_mm, k - R + 1)
                    sp.dma_start(row[:, u, :, C + 1:ROW], src[:, ds(g * G, G), 0:C]).then_inc(s_at[u], 16)

                pipeline(sp, KS, (load, 0), ring=R)

            @block.gpsimd
            def _(pool):
                pool.sem_inc(s_one, 1)

                def gather(k, u, use):
                    if later(k, R):
                        pool.wait_ge(s_w, k - R + 1)
                    pool.wait_ge(s_idx, k + 1)
                    for j in range(G):
                        nc.gpsimd.indirect_dma_start(
                            out=xg[:, u, j, :], out_offset=None, in_=v.table[:, :],
                            in_offset=bass.IndirectOffsetOnAxis(ap=idx[:, u, j:j + 1], axis=0)
                        ).wait_op(s_one, 1, "sem-ge").then_inc(s_xg[u], 16)

                pipeline(pool, KS, (gather, 0), ring=R)

            @block.scalar
            def _(act):
                def index(k, u, use):
                    g, _ = step_of(nc, act, steps, k, groups)
                    if later(k, R):
                        act.wait_ge(s_xg[u], use * (16 * G))
                    act.wait_ge(s_one, 1)
                    nc.scalar.activation(idx[:, u, :], v.dsti[:, ds(g * G, G)], ACT.Copy).then_inc(s_idx, 1)

                def turned(k, u, use):
                    act.wait_ge(s_t, k + 1)
                    if later(k, R):
                        act.wait_ge(s_got, k - R + 1)
                    nc.scalar.activation(oht[:, u, :], pst[u % 2][:, :], ACT.Copy).then_inc(s_oht, 1)

                def weigh(k, u, use):
                    if later(k, R):
                        act.wait_ge(s_mm, k - R + 1)
                    act.wait_ge(s_clip, k + 1)
                    nc.scalar.activation(row[:, u, :, C], t[:, u, 2, :], ACT.Exp).then_inc(s_exp, 1)

                pipeline(act, KS, (index, 0), (turned, 0), (weigh, 4), ring=R)

            @block.vector
            def _(dve):
                nc.vector.memset(acc[:, :, :], 0.0).then_inc(s_z, 1)

                def onehot(k, u, use):
                    g, b = step_of(nc, dve, steps, k, groups)
                    if later(k, R):
                        dve.wait_ge(s_mm, k - R + 1)
                    nc.vector.scalar_tensor_tensor(
                        oh[:, u, :, :], v.iota[:, None, :].broadcast_to([P, G, P]), v.blk[:, ds(b, 1)],
                        keys[:, ds(g * G, G), None].broadcast_to([P, G, P]), ALU.add,
                        ALU.is_equal).then_inc(s_oh, 1)

                def score(k, u, use):
                    dve.wait_ge(s_got, k + 1)
                    dve.wait_ge(s_xg[u], use * (16 * G) + 16 * G)
                    nc.vector.tensor_tensor(t[:, u, 0, :],
                                            psx[u % 2][:, 0:G * X8].rearrange("p (g c) -> p g c", g=G)[:, :, 0],
                                            xg[:, u, :, C], ALU.add).then_inc(s_sum, 1)

                def leaky(k, u, use):
                    dve.wait_ge(s_sum, k + 1)
                    nc.vector.scalar_tensor_tensor(t[:, u, 1, :], t[:, u, 0, :], 0.2, t[:, u, 0, :], ALU.mult,
                                                   ALU.max).then_inc(s_leaky, 1)

                def clip(k, u, use):
                    if later(k, R):
                        dve.wait_ge(s_exp, k - R + 1)
                    dve.wait_ge(s_leaky, k + 1)
                    nc.vector.tensor_scalar(t[:, u, 2, :], t[:, u, 1, :], -2.0, 2.0, ALU.max,
                                            ALU.min).then_inc(s_clip, 1)

                def weighted(k, u, use):
                    dve.wait_ge(s_exp, k + 1)
                    nc.vector.tensor_tensor(row[:, u, :, 0:C], xg[:, u, :, 0:C],
                                            row[:, u, :, C:C + 1].broadcast_to([P, G, C]),
                                            ALU.mult).then_inc(s_w, 1)

                def add(k, u, use):
                    _, b = step_of(nc, dve, steps, k, groups)
                    dve.wait_ge(s_mm, k + 1)
                    if later(k, 1):
                        dve.wait_ge(s_add, k)
                    else:
                        dve.wait_ge(s_z, 1)
                    here = flat(acc[:, ds(b, 1), :])
                    nc.vector.tensor_tensor(here, here, ps[u % 2][:, 0:ROW], ALU.add).then_inc(s_add, 1)

                pipeline(dve, KS, (clip, 4), (onehot, 0), (leaky, 3), (add, 7), (score, 2), (weighted, 5), ring=R)

            @block.tensor
            def _(pe):
                def turn(k, u, use):
                    pe.wait_ge(s_oh, k + 1)
                    if later(k):
                        pe.wait_ge(s_oht, k - 1)
                    for j in range(G):
                        last = nc.tensor.transpose(pst[u % 2][:, j * P:(j + 1) * P], oh[:, u, j, :], v.ident[:, :])
                    last.then_inc(s_t, 1)

                def look(k, u, use):
                    _, b = step_of(nc, pe, steps, k, groups)
                    if later(k):
                        pe.wait_ge(s_sum, k - 1)
                    pe.wait_ge(s_oht, k + 1)
                    for j in range(G):
                        last = nc.tensor.matmul(psx[u % 2][:, j * X8:(j + 1) * X8], oht[:, u, j * P:(j + 1) * P],
                                                flat(v.scores[:, ds(b, 1), :]), start=True, stop=True)
                    last.then_inc(s_got, 1)

                def sums(k, u, use):
                    pe.wait_ge(s_w, k + 1)
                    pe.wait_ge(s_at[u], use * 16 + 16)
                    if later(k):
                        pe.wait_ge(s_add, k - 1)
                    for j in range(G):
                        last = nc.tensor.matmul(ps[u % 2][:, 0:ROW], oh[:, u, j, :], row[:, u, j, :],
                                                start=(j == 0), stop=(j == G - 1))
                    last.then_inc(s_mm, 1)

                pipeline(pe, KS, (turn, 0), (look, 1), (sums, 6), ring=R)


class Gather:
    R = 4

    def __init__(self, nc, v, name, idx_all, rows_out, scores_out, width):
        self.nc, self.v, self.name, self.idx_all = nc, v, name, idx_all
        self.rows_out, self.scores_out, self.width = rows_out, scores_out, width

    def buffers(self, mem):
        nc, v, R, name = self.nc, self.v, self.R, self.name
        self.s_idx, self.s_one, self.s_cp = v.sem(name + "_idx"), v.sem(name + "_one"), v.sem(name + "_cp")
        self.s_xg = [v.pool_dma_sem(f"{name}_xg{u}") for u in range(R)]
        self.s_st = [v.sem(f"{name}_st{u}") for u in range(R)]
        self.idx = mem.enter_context(nc.sbuf_tensor(name + "_idx", [P, R, G], I32))
        self.xg = mem.enter_context(nc.sbuf_tensor(name + "_xg", [P, R, G, W], F32))

    def index(self, act):
        def index(g, u, use):
            u, use = u % self.R, use * 2 + u // self.R
            if later(g, self.R):
                act.wait_ge(self.s_xg[u], use * (16 * G))
            act.wait_ge(self.s_one, 1)
            self.nc.scalar.activation(self.idx[:, u, :], self.idx_all[:, ds(g * G, G)],
                                      ACT.Copy).then_inc(self.s_idx, 1)
        return index

    def pool(self, pool):
        nc, v, R = self.nc, self.v, self.R
        pool.sem_inc(self.s_one, 1)

        def gather(g, u, use):
            if later(g, R):
                pool.wait_ge(self.s_st[u], use * 16)
                pool.wait_ge(self.s_cp, g - R + 1)
            pool.wait_ge(self.s_idx, g + 1)
            for j in range(G):
                nc.gpsimd.indirect_dma_start(
                    out=self.xg[:, u, j, :], out_offset=None, in_=v.table[:, :],
                    in_offset=bass.IndirectOffsetOnAxis(ap=self.idx[:, u, j:j + 1], axis=0)
                ).wait_op(self.s_one, 1, "sem-ge").then_inc(self.s_xg[u], 16)

        pipeline(pool, GS, (gather, 0), ring=R)

    def scores(self, dve):
        def scores(g, u, use):
            u, use = u % self.R, use * 2 + u // self.R
            dve.wait_ge(self.s_xg[u], use * (16 * G) + 16 * G)
            self.nc.vector.tensor_scalar(self.scores_out[:, ds(g * G, G), 0:self.width],
                                         self.xg[:, u, :, C:C + self.width], 0.0, None,
                                         ALU.add).then_inc(self.s_cp, 1)
        return scores

    def sync(self, sp):
        out = self.rows_out.rearrange("(t p) c -> p t c", p=P)

        def store(g, u, use):
            sp.wait_ge(self.s_xg[u], use * (16 * G) + 16 * G)
            sp.dma_start(out[:, ds(g * G, G), :], self.xg[:, u, :, 0:C]).then_inc(self.s_st[u], 16)

        pipeline(sp, GS, (store, 0), ring=self.R)
        for u in range(self.R):
            sp.wait_ge(self.s_st[u], 16 * ((GS - u + self.R - 1) // self.R))


def meta_loads(v, meta, signal):
    view = v.sorted.rearrange("(t p) c -> p t c", p=P)
    return [(meta[:, n * P:(n + 1) * P, :], view[:, n * P:(n + 1) * P, C:RW], signal) for n in range(KR)]


def stage_sorted_keys(nc, v, meta, s_ld, taking):
    s, s_t, s_c, s_st = (v.sem("k_" + n) for n in ("dve", "t", "c", "st"))
    with ExitStack() as mem:
        rows = mem.enter_context(nc.sbuf_tensor("k_rows", [P, KR, P], I32))
        ps = [mem.enter_context(nc.psum_tensor(f"k_ps{u}", [P, 512], F32)) for u in range(2)]
        with nc.Block() as block:
            @block.sync
            def _(sp):
                sp.wait_ge(s_c, KR)
                sp.dma_start(v.sorted_row[:, 1:1 + TS * P].rearrange("a (k r p) -> r (a k) p", r=P, p=P),
                             rows[:, :, :]).then_inc(s_st, 16)
                sp.wait_ge(s_st, 16)

            @block.vector
            def _(dve):
                dve.wait_ge(s_ld, 16 * KR)
                nc.vector.tensor_copy(v.srck[:, :], meta[:, :, 2]).then_inc(s, 1)
                nc.vector.tensor_copy(v.dsti[:, :], meta[:, :, 1]).then_inc(s, 1)
                nc.vector.scalar_tensor_tensor(taking[:, :], meta[:, :, 2], 1.0, meta[:, :, 0], ALU.add,
                                               ALU.mult).then_inc(s, 1)
                dve.wait_ge(s, 3)
                nc.vector.tensor_scalar(taking[:, :], taking[:, :], -1.0, None, ALU.add).then_inc(s, 1)
                for k in range(KR):
                    dve.wait_ge(s_t, k + 1)
                    nc.vector.tensor_copy(rows[:, k, :], ps[k % 2][:, 0:P]).then_inc(s_c, 1)

            @block.tensor
            def _(pe):
                pe.wait_ge(s, 1)
                for k in range(KR):
                    if k >= 2:
                        pe.wait_ge(s_c, k - 1)
                    nc.tensor.transpose(ps[k % 2][:, 0:P], v.srck[:, k * P:(k + 1) * P], v.ident[:, :]).then_inc(s_t, 1)


def stage_add_leaky(nc, v, e, other):
    s = v.sem("al")
    with nc.Block() as block:
        @block.vector
        def _(dve):
            link = chain(dve, s)
            e2, o2 = flat(e[:, :, :]), flat(other[:, :, :])
            link(nc.vector.tensor_tensor(e2, e2, o2, ALU.add))
            link(nc.vector.scalar_tensor_tensor(e2, e2, 0.2, e2, ALU.mult, ALU.max))


def stage_mlp(nc, v, aggr):
    NX = NBX * P
    CH = 400
    NCH = NX // CH
    s_w, s_z = v.sem("m_w"), v.sem("m_z")
    names = ["wx", "wa", "wg", "m1", "m2", "m3"]
    with ExitStack() as mem:
        sb = lambda n, sh, d=F32: mem.enter_context(nc.sbuf_tensor("m" + n, sh, d))
        wt = {n: sb("_" + n, [P, C]) for n in names}
        gf, bc, b1, b2, b3 = sb("_gf", [P, 1]), sb("_bc", [P, 1]), sb("_b1", [P, 1]), sb("_b2", [P, 1]), sb("_b3", [1, C])
        xt, at, cc = sb("_xt", [P, NX]), sb("_at", [P, NX]), sb("_cc", [P, 1])
        psg = mem.enter_context(nc.psum_tensor("m_psg", [P, 512], F32))
        with nc.Block() as block:
            @block.sync
            def _(sp):
                for n, src in (("wx", v.Wc[0:C, :]), ("wa", v.Wc[C:2 * C, :]), ("wg", v.Wc[2 * C:3 * C, :]),
                               ("m1", v.M1), ("m2", v.M2), ("m3", v.M3)):
                    sp.dma_start(wt[n][:, :], src).then_inc(s_w, 16)
                for t, src in ((gf, v.gf), (bc, v.bc), (b1, v.m1b), (b2, v.m2b), (b3, v.m3b)):
                    sp.dma_start(t[:, :], src).then_inc(s_w, 16)

            @block.tensor
            def _(pe):
                pe.wait_ge(s_w, 16 * 11)
                nc.tensor.matmul(psg[:, 0:1], wt["wg"][:, :], gf[:, :], start=True, stop=True).then_inc(s_z, 1)

            @block.vector
            def _(dve):
                dve.wait_ge(s_z, 1)
                nc.vector.tensor_tensor(cc[:, :], psg[:, 0:1], bc[:, :], ALU.add).then_inc(s_z, 1)

        def transposed(name, source, target):
            s_x, s_t, s_c = v.sem(name + "_x"), v.sem(name + "_t"), v.sem(name + "_c")
            with ExitStack() as m2:
                xs = m2.enter_context(nc.sbuf_tensor(name + "_xs", [P, 4, C], F32))
                ps = [m2.enter_context(nc.psum_tensor(f"{name}_ps{u}", [P, 512], F32)) for u in range(4)]
                with nc.Block() as block:
                    @block.vector
                    def _(dve):
                        def stage(b, u, use):
                            if later(b, 4):
                                dve.wait_ge(s_t, b - 3)
                            nc.vector.tensor_scalar(xs[:, u, :], flat(source[:, ds(b, 1), 0:C]), 0.0, None,
                                                    ALU.add).then_inc(s_x, 1)

                        def put(b, u, use):
                            dve.wait_ge(s_t, b + 1)
                            nc.vector.tensor_scalar(target[:, ds(b * P, P)], ps[u][:, 0:P], 0.0, None,
                                                    ALU.add).then_inc(s_c, 1)

                        pipeline(dve, NBX, (stage, 0), (put, 2), ring=4)

                    @block.tensor
                    def _(pe):
                        def turn(b, u, use):
                            pe.wait_ge(s_x, b + 1)
                            if later(b, 4):
                                pe.wait_ge(s_c, b - 3)
                            nc.tensor.transpose(ps[u][:, 0:P], xs[:, u, :], v.ident[:, :]).then_inc(s_t, 1)

                        pipeline(pe, NBX, (turn, 0), ring=4)

        def layer(name, terms, bias, out):
            s_mm, s_o = v.sem(name + "_mm"), v.sem(name + "_o")
            with ExitStack() as m2:
                ps = [m2.enter_context(nc.psum_tensor(f"{name}_ps{u}", [P, 512], F32)) for u in range(RING)]
                with nc.Block() as block:
                    @block.tensor
                    def _(pe):
                        def mm(c, u, use):
                            if later(c):
                                pe.wait_ge(s_o, c - 1)
                            for n, (w, x) in enumerate(terms):
                                last = nc.tensor.matmul(ps[u][:, 0:CH], w[:, :], x[:, ds(c * CH, CH)],
                                                        start=(n == 0), stop=(n == len(terms) - 1))
                            last.then_inc(s_mm, 1)

                        pipeline(pe, NCH, (mm, 0))

                    @block.vector
                    def _(dve):
                        def add(c, u, use):
                            dve.wait_ge(s_mm, c + 1)
                            nc.vector.tensor_scalar(out[:, ds(c * CH, CH)], ps[u][:, 0:CH], bias[:, 0:1], None,
                                                    ALU.add).then_inc(s_o, 1)

                        pipeline(dve, NCH, (add, 0))

        def softplus(name, z, t):
            s, s2 = v.sem(name), v.sem(name + "a")
            with nc.Block() as block:
                @block.vector
                def _(dve):
                    link = chain(dve, s)
                    link(nc.vector.scalar_tensor_tensor(t[:, :], z[:, :], -1.0, z[:, :], ALU.mult, ALU.min))
                    link(nc.vector.tensor_scalar(z[:, :], z[:, :], 0.0, None, ALU.max))
                    dve.wait_ge(s2, 2)
                    link(nc.vector.tensor_tensor(z[:, :], z[:, :], t[:, :], ALU.add))

                @block.scalar
                def _(act):
                    act.wait_ge(s, 1)
                    nc.scalar.activation(t[:, :], t[:, :], ACT.Exp).then_inc(s2, 1)
                    act.wait_ge(s2, 1)
                    nc.scalar.activation(t[:, :], t[:, :], ACT.Ln, bias=1.0).then_inc(s2, 1)

        transposed("mt0", v.X, xt)
        transposed("mt1", aggr, at)
        layer("ml0", [(wt["wx"], xt), (wt["wa"], at)], cc, xt)
        layer("ml1", [(wt["m1"], xt)], b1, at)
        softplus("mp1", at, xt)
        layer("ml2", [(wt["m2"], at)], b2, xt)
        softplus("mp2", xt, at)

        s_x, s_mm, s_o = v.sem("mo_x"), v.sem("mo_mm"), v.sem("mo_o")
        xs = sb("_xs", [P, 4, P])
        ps = [mem.enter_context(nc.psum_tensor(f"mo_ps{u}", [P, 512], F32)) for u in range(4)]
        with nc.Block() as block:
            @block.vector
            def _(dve):
                def stage(b, u, use):
                    if later(b, 4):
                        dve.wait_ge(s_mm, b - 3)
                    nc.vector.tensor_scalar(xs[:, u, :], xt[:, ds(b * P, P)], 0.0, None, ALU.add).then_inc(s_x, 1)

                def put(b, u, use):
                    dve.wait_ge(s_mm, b + 1)
                    nc.vector.tensor_scalar(flat(aggr[:, ds(b, 1), 0:C]), ps[u][:, 0:C], 0.0, None,
                                            ALU.add).then_inc(s_o, 1)

                pipeline(dve, NBX, (stage, 0), (put, 2), ring=4)

            @block.tensor
            def _(pe):
                def mm(b, u, use):
                    pe.wait_ge(s_x, b + 1)
                    if later(b, 4):
                        pe.wait_ge(s_o, b - 3)
                    nc.tensor.matmul(ps[u][:, 0:C], v.ones[0:1, :], b3[:, :], start=True, stop=False)
                    nc.tensor.matmul(ps[u][:, 0:C], xs[:, u, :], wt["m3"][:, :], start=False,
                                     stop=True).then_inc(s_mm, 1)

                pipeline(pe, NBX, (mm, 0), ring=4)


def recycle(nc, v):
    with nc.Block() as block:
        @block.gpsimd
        def _(pool):
            for s in v.layer_sems:
                pool.sem_clear(s)
    for s in v.layer_sems:
        nc.release_semaphore(s)
    v.layer_sems = []


def make_flags(nc, mem, name, heads):
    fl = Env()
    fl.heads = heads
    sb = lambda k, sh: mem.enter_context(nc.sbuf_tensor(f"{name}_{k}", sh, F32))
    fl.rf, fl.rb, fl.gf, fl.gb = (sb(k, [P, KR, P]) for k in ("rf", "rb", "gf", "gb"))
    fl.af, fl.ab = (sb(k, [heads, TR]) for k in ("af", "ab"))
    return fl


def build(nc, v):
    with ExitStack() as ctx:
        def sb(name, shape, dt=F32, mem=ctx):
            return mem.enter_context(nc.sbuf_tensor(name, shape, dt))

        v.layer_sems = []
        v.sem = lambda name: v.layer_sems.append(nc.alloc_semaphore(name=name)) or v.layer_sems[-1]
        v.pool_dma_sem = lambda name: ctx.enter_context(nc.semaphore(name))

        def dram(name, shape, dt=F32):
            return nc.dram_tensor(name, shape, dt, kind="Internal").ap()

        v.s_in = v.pool_dma_sem("inputs")
        v.X = sb("X", [P, NBX, C])
        v.keys2 = sb("keys2", [P, 2, TR])
        v.dstk, v.srck = v.keys2[:, 0, :], v.keys2[:, 1, :]
        v.srci = sb("srci", [P, TR], I32)
        v.iota, v.part, v.blk, v.stepn = sb("iota", [P, P]), sb("part", [P, 1]), sb("blk", [P, NBX]), sb("stepn", [P, 512])
        v.ident, v.before, v.after = sb("ident", [P, P]), sb("before", [P, P]), sb("after", [P, P])
        v.ones, v.zeros = sb("ones", [P, P]), sb("zeros", [P, P])
        v.scores = sb("scores", [P, NBX, X8])
        v.rhs = sb("rhs", [P, C + 2 * X8])
        hist, run, below, count = (sb(n, [P, NBX]) for n in ("hist", "run", "below", "count"))
        steps_e, steps_s = sb("steps_e", [1, 2, 512], I32), sb("steps_s", [1, 2, 512], I32)
        v.table = dram("table", (NBX * P, W))
        v.src_row = dram("src_row", (1, TR * P), I32)
        v.dst_row = dram("dst_row", (1, TR * P + 2), I32)
        v.sorted_row = dram("sorted_row", (1, TR * P + 2), I32)
        gated = dram("gated", (TE * P, C))
        gathered = dram("gathered", (TS * P, C))
        v.sorted = dram("sorted", (TS * P, RW))

        with ExitStack() as mem:
            v.iota_i, v.part_i = sb("iota_i", [P, P], I32, mem), sb("part_i", [P, 1], I32, mem)
            v.blk_i, v.stepn_i = sb("blk_i", [P, NBX], I32, mem), sb("stepn_i", [P, 512], I32, mem)
            v.padrow, v.blank = sb("padrow", [1, (TR * P - E) // 2], I32, mem), sb("blank", [1, 1], I32, mem)
            v.dsti = sb("dsti_in", [P, TR], I32, mem)
            stage_constants(nc, v)

        stage_weights(nc, v, "w0", v.W0, v.W0t,
                      [(v.a0[h, 16 * s:16 * s + 16, :], 16 * h, 16, X8 * s + h) for h in range(8) for s in range(2)],
                      v.rhs)
        stage_node_table(nc, v, "t0", v.rhs, v.table, v.scores, count)
        stage_steps(nc, v, "se", count, GE, steps_e)
        with ExitStack() as layer:
            e_score = sb("e_score", [P, TR, X8], F32, layer)
            stage_clear(nc, v, "ce", e_score)
            split = GE - (4 * (GE * 11 // 96) + 1)
            with ExitStack() as moved:
                runi = sb("runi", [P, NBX], I32, moved)
                ranges = [(0, split), (split, GE - split)]
                late = sb("pos_late", [P, (GE - split) * G], I32, moved)
                with ExitStack() as soon:
                    early = sb("pos_early", [P, split * G], I32, soon)
                    with ExitStack() as mem:
                        v.lo, v.hi, posf = (sb(n, [P, TR], F32, mem) for n in ("lo", "hi", "posf"))
                        stage_histogram(nc, v, hist)
                        stage_bases(nc, v, hist, run, below)
                        stage_steps(nc, v, "ss", below, GS, steps_s)
                        stage_gate_and_rank(nc, v, e_score, gated, run, posf)
                        scatter = Scatter(nc, v, [early, late], runi, posf, run, v.sorted, ranges)
                    stage_expand(nc, v, "xe", v.dstk, steps_e, KE, GE, X8, e_score, scatter=scatter)
                with ExitStack() as mem:
                    fl = make_flags(nc, mem, "fe", 2)
                    stage_flags(nc, v, "fe", v.dst_row, fl)
                    stage_leaky(nc, v, "lk0", flat(e_score[:, :, :]))
                    for n in range(8 // fl.heads):
                        stage_softmax(nc, v, f"sm{n}", e_score, n * fl.heads, fl)
                acc = sb("acc0", [P, NBX, W], F32, moved)
                stage_aggregate(nc, v, "ag0", gated, v.dstk, steps_e, KE, GE, e_score, 8, acc, scatter=scatter)
                stage_update(nc, v, "up0", acc, 8, 1e-12, "norm")
        recycle(nc, v)
        v.dsti = sb("dsti", [P, TR], I32)

        with ExitStack() as layer:
            taking = sb("taking", [P, TS], F32, layer)
            stage_weights(nc, v, "w1", v.W1, v.W1t, [(v.a1[C:2 * C, :], 0, C, 0), (v.a1[0:C, :], 0, C, X8)], v.rhs)
            with ExitStack() as mem:
                meta, s_meta = sb("meta", [P, TS, RW - C], F32, mem), v.sem("meta")
                stage_node_table(nc, v, "t1", v.rhs, v.table, v.scores, loads=meta_loads(v, meta, s_meta))
                stage_sorted_keys(nc, v, meta, s_meta, taking)
            acc = sb("acc1", [P, NBX, 2 * C + 1], F32, layer)
            stage_clipped_attention(nc, v, taking, steps_s, acc)
            stage_update(nc, v, "up1", acc, 1, 1e-30, None)
            recycle(nc, v)

            acc = acc[:, :, C + 1:]
            stage_mlp(nc, v, acc)
            stage_update(nc, v, "up2", acc, 0, None, None)
        recycle(nc, v)

        stage_weights(nc, v, "w3", v.W3, v.W3t,
                      [(v.a3[h, 32 * (1 - s):32 * (1 - s) + 32, :], 32 * h, 32, X8 * s + h)
                       for h in range(4) for s in range(2)], v.rhs)
        stage_node_table(nc, v, "t3", v.rhs, v.table, v.scores)
        with ExitStack() as layer:
            e3 = sb("e3", [P, TS, 4], F32, layer)
            with ExitStack() as mem:
                o3 = sb("o3", [P, TS, 4], F32, mem)
                gather = Gather(nc, v, "g3", v.dsti, gathered, o3, 4)
                stage_expand(nc, v, "x3", v.srck, steps_s, KS, GS, 4, e3, gather=gather)
                stage_add_leaky(nc, v, e3, o3)
            for n in range(2):
                with ExitStack() as mem:
                    fl = make_flags(nc, mem, f"fs{n}", 2)
                    stage_flags(nc, v, f"fs{n}", v.sorted_row, fl)
                    stage_top8(nc, v, f"tk{n}", e3, 2 * n, fl, 8)
            acc = sb("acc3", [P, NBX, W], F32, layer)
            stage_aggregate(nc, v, "ag3", gathered, v.srck, steps_s, KS, GS, e3, 4, acc)
            stage_update(nc, v, "up3", acc, 4, 1e-30, "elu")
        s_out = v.sem("out")
        with nc.Block() as block:
            @block.sync
            def _(sp):
                sp.dma_start(v.out[0:(NB - 1) * P, :].rearrange("(b p) c -> p b c", p=P),
                             v.X[:, 0:NB - 1, :]).then_inc(s_out, 16)
                sp.dma_start(v.out[(NB - 1) * P:N, :], v.X[0:TAIL, NB - 1, :]).then_inc(s_out, 16)
                sp.wait_ge(s_out, 32)


def kernel(**inputs):
    import numpy as np
    import concourse.bacc as bacc
    from concourse.bass_utils import run_bass_kernel_spmd

    nc = bacc.Bacc("TRN2", target_bir_lowering=False, num_devices=1)
    a = {k: np.asarray(x) for k, x in inputs.items()}
    full = (TE - 1) * P
    w0 = a["L0_gnn_W"].transpose(1, 0, 2).reshape(C, C)
    arrays = {
        "x": a["x"], "src": a["src"], "dst": a["dst"],
        "src_t": a["src"][:full].reshape(TE - 1, P).T, "dst_t": a["dst"][:full].reshape(TE - 1, P).T,
        "attr": a["edge_attr_128"], "attr_t": a["edge_attr_128"].T,
        "W0": w0, "W0t": w0.T, "a0": a["L0_gnn_a"],
        "eb_wt": a["L0_gnn_eb_w"].T, "eb_b": a["L0_gnn_eb_b"][None], "eg_wt": a["L0_gnn_eg_w"].T,
        "eg_b": a["L0_gnn_eg_b"][None], "ln_g": a["L0_gnn_ln_g"][None], "ln_b": a["L0_gnn_ln_b"][None],
        "W1": a["L1_gnn_kernel"], "W1t": a["L1_gnn_kernel"].T, "a1": a["L1_gnn_kernel_attention"],
        "gf": a["L2_gnn_global_feat"].T, "Wc": a["L2_gnn_W_c"], "bc": a["L2_gnn_b_c"][:, None],
        "M1": a["L2_gnn_W1"], "m1b": a["L2_gnn_b1"][:, None], "M2": a["L2_gnn_W2"], "m2b": a["L2_gnn_b2"][:, None],
        "M3": a["L2_gnn_W3"], "m3b": a["L2_gnn_b3"][None],
        "W3": a["L3_gnn_W"], "W3t": a["L3_gnn_W"].T, "a3": a["L3_gnn_att"][:, :, None],
    }
    arrays = {k: np.ascontiguousarray(x) for k, x in arrays.items()}
    v = Env()
    for k, x in arrays.items():
        v.__dict__[k] = nc.dram_tensor("in_" + k, x.shape, mybir.dt.from_np(x.dtype), kind="ExternalInput").ap()
    v.out = nc.dram_tensor("out_0", (N, C), F32, kind="ExternalOutput").ap()
    build(nc, v)
    r = run_bass_kernel_spmd(nc, [{"in_" + k: x for k, x in arrays.items()}], core_ids=[0])
    return r.results[0]["out_0"]
```
